# Optimizing a Trainium2 kernel written in Bass

```python
import numpy as np
import jax
import jax.numpy as jnp

def _softmax(x, axis=-1):
    return jax.nn.softmax(x, axis=axis)

def _gelu(x):
    return jax.nn.gelu(x, approximate=True)

def _silu(x):
    return jax.nn.silu(x)

def _sigmoid(x):
    return jax.nn.sigmoid(x)

def _layernorm(x, axis=-1, eps=1e-05):
    m = jnp.mean(x, axis=axis, keepdims=True)
    v = jnp.var(x, axis=axis, keepdims=True)
    return (x - m) / jnp.sqrt(v + eps)

def _scatter_add(tgt, idx, src, axis=0):
    return tgt.at[idx].add(src)

def _segment_sum(src, seg, n):
    return jax.ops.segment_sum(src, seg, n)
kernel_name = 'mk_gnn_preln_d2_gnn_r32_a3cde5'

def setup_inputs(seed: int=0):
    np.random.seed(seed)
    _w = jnp.asarray

    def _rec_inputs():
        import jax
        import jax.numpy as jnp
        _gk = jax.random.key(seed)
        x = 0.0003989 + 1 * jax.random.normal(jax.random.fold_in(_gk, 1), (3125, 128), jnp.float32)
        src = jax.random.randint(jax.random.fold_in(_gk, 2), (100000,), 0, 3125, jnp.int32)
        dst = jax.random.randint(jax.random.fold_in(_gk, 3), (100000,), 0, 3125, jnp.int32)
        _o = jnp.argsort(dst, stable=True)
        src = src[_o]
        dst = dst[_o]
        edge_weight = jax.random.uniform(jax.random.fold_in(_gk, 13), (100000,), jnp.float32, 0.0, 0.999999)
        return (x, src, dst, edge_weight)
    x, src, dst, edge_weight = _rec_inputs()

    def _L0_gnn_setup():
        import jax, jax.numpy as jnp
        import numpy as np
        N = 50000
        E_RAND = 25000
        D_IN = 128
        H = 8
        HD = 16
        D_OUT = H * HD
        D_FF = 4 * D_OUT
        HOP = 5
        ALPHA = 0.15
        SLOPE = 0.2
        EPS = 1e-05

        def _layer_norm(x, g, b):
            mu = jnp.mean(x, axis=-1, keepdims=True)
            var = jnp.var(x, axis=-1, keepdims=True)
            return (x - mu) * jax.lax.rsqrt(var + EPS) * g + b
        key = jax.random.key(seed)
        ks = jax.random.split(key, 10)
        src_r = jax.random.randint(ks[0], (E_RAND,), 0, N)
        dst_r = jax.random.randint(ks[1], (E_RAND,), 0, N)
        loop = jnp.arange(N)
        src = jnp.concatenate([src_r, loop])
        dst = jnp.concatenate([dst_r, loop])
        feat = jax.random.normal(ks[2], (N, D_IN), dtype=jnp.float32)
        s = 0.05
        return {'feat': feat, 'src': src, 'dst': dst, 'ln1_g': jnp.ones((D_IN,), jnp.float32), 'ln1_b': jnp.zeros((D_IN,), jnp.float32), 'W_head': jax.random.normal(ks[3], (D_OUT, D_IN), jnp.float32) * s, 'W_tail': jax.random.normal(ks[4], (D_OUT, D_IN), jnp.float32) * s, 'W_ent': jax.random.normal(ks[5], (D_OUT, D_IN), jnp.float32) * s, 'attn': jax.random.normal(ks[6], (1, H, HD), jnp.float32) * s, 'ln2_g': jnp.ones((D_OUT,), jnp.float32), 'ln2_b': jnp.zeros((D_OUT,), jnp.float32), 'W_ff1': jax.random.normal(ks[7], (D_FF, D_OUT), jnp.float32) * s, 'b_ff1': jnp.zeros((D_FF,), jnp.float32), 'W_ff2': jax.random.normal(ks[8], (D_OUT, D_FF), jnp.float32) * s, 'b_ff2': jnp.zeros((D_OUT,), jnp.float32)}
    _L0_gnn_all = _L0_gnn_setup()
    _L0_gnn_in = {k: v for k, v in _L0_gnn_all.items() if k in ('ln1_g', 'ln1_b', 'W_head', 'W_tail', 'W_ent', 'attn', 'ln2_g', 'ln2_b', 'W_ff1', 'b_ff1', 'W_ff2', 'b_ff2')}
    del _L0_gnn_all

    def _L1_gnn_setup():
        import jax, jax.numpy as jnp
        import numpy as np
        N = 50000
        E = 50000
        F = 128

        def _gcn_norm(src, dst, w, n):
            loops = jnp.arange(n, dtype=src.dtype)
            src_a = jnp.concatenate([src, loops])
            dst_a = jnp.concatenate([dst, loops])
            w_a = jnp.concatenate([w, jnp.ones((n,), w.dtype)])
            deg = jax.ops.segment_sum(w_a, dst_a, num_segments=n)
            dinv = jnp.where(deg > 0, jax.lax.rsqrt(deg), 0.0)
            norm = dinv[src_a] * w_a * dinv[dst_a]
            return (src_a, dst_a, norm)

        def _gcn_conv(x, src_a, dst_a, norm, W, b, n):
            h = x @ W
            msg = h[src_a] * norm[:, None]
            out = jax.ops.segment_sum(msg, dst_a, num_segments=n)
            return out + b
        key = jax.random.key(seed)
        ks = jax.random.split(key, 10)
        s = 1.0 / np.sqrt(F)
        return {'x': jax.random.normal(ks[0], (N, F), jnp.float32), 'edge_index': jax.random.randint(ks[1], (2, E), 0, N, dtype=jnp.int64), 'edge_attr': jax.random.uniform(ks[2], (E,), jnp.float32), 'W0': jax.random.normal(ks[3], (F, F), jnp.float32) * s, 'b0': jnp.zeros((F,), jnp.float32), 'W1': jax.random.normal(ks[4], (F, F), jnp.float32) * s, 'b1': jnp.zeros((F,), jnp.float32), 'W2': jax.random.normal(ks[5], (F, F), jnp.float32) * s, 'b2': jnp.zeros((F,), jnp.float32)}
    _L1_gnn_all = _L1_gnn_setup()
    _L1_gnn_in = {k: v for k, v in _L1_gnn_all.items() if k in ('W0', 'b0', 'W1', 'b1', 'W2', 'b2')}
    del _L1_gnn_all
    return {'x': x, 'src': src, 'dst': dst, 'edge_weight': edge_weight, 'L0_gnn_ln1_g': _L0_gnn_in['ln1_g'], 'L0_gnn_ln1_b': _L0_gnn_in['ln1_b'], 'L0_gnn_W_head': _L0_gnn_in['W_head'], 'L0_gnn_W_tail': _L0_gnn_in['W_tail'], 'L0_gnn_W_ent': _L0_gnn_in['W_ent'], 'L0_gnn_attn': _L0_gnn_in['attn'], 'L0_gnn_ln2_g': _L0_gnn_in['ln2_g'], 'L0_gnn_ln2_b': _L0_gnn_in['ln2_b'], 'L0_gnn_W_ff1': _L0_gnn_in['W_ff1'], 'L0_gnn_b_ff1': _L0_gnn_in['b_ff1'], 'L0_gnn_W_ff2': _L0_gnn_in['W_ff2'], 'L0_gnn_b_ff2': _L0_gnn_in['b_ff2'], 'L1_gnn_W0': _L1_gnn_in['W0'], 'L1_gnn_b0': _L1_gnn_in['b0'], 'L1_gnn_W1': _L1_gnn_in['W1'], 'L1_gnn_b1': _L1_gnn_in['b1'], 'L1_gnn_W2': _L1_gnn_in['W2'], 'L1_gnn_b2': _L1_gnn_in['b2']}

def reference(x, src, dst, edge_weight, L0_gnn_ln1_g, L0_gnn_ln1_b, L0_gnn_W_head, L0_gnn_W_tail, L0_gnn_W_ent, L0_gnn_attn, L0_gnn_ln2_g, L0_gnn_ln2_b, L0_gnn_W_ff1, L0_gnn_b_ff1, L0_gnn_W_ff2, L0_gnn_b_ff2, L1_gnn_W0, L1_gnn_b0, L1_gnn_W1, L1_gnn_b1, L1_gnn_W2, L1_gnn_b2):
    import jax
    import jax.numpy as jnp

    def _L0_gnn_ref(feat, src, dst, ln1_g, ln1_b, W_head, W_tail, W_ent, attn, ln2_g, ln2_b, W_ff1, b_ff1, W_ff2, b_ff2):
        import jax, jax.numpy as jnp
        import numpy as np
        N = 50000
        E_RAND = 25000
        D_IN = 128
        H = 8
        HD = 16
        D_OUT = H * HD
        D_FF = 4 * D_OUT
        HOP = 5
        ALPHA = 0.15
        SLOPE = 0.2
        EPS = 1e-05

        def _layer_norm(x, g, b):
            mu = jnp.mean(x, axis=-1, keepdims=True)
            var = jnp.var(x, axis=-1, keepdims=True)
            return (x - mu) * jax.lax.rsqrt(var + EPS) * g + b
        n = feat.shape[0]
        h = _layer_norm(feat, ln1_g, ln1_b)
        fh = (h @ W_head.T).reshape(n, H, HD)
        ft = (h @ W_tail.T).reshape(n, H, HD)
        fe = (h @ W_ent.T).reshape(n, H, HD)
        e = jax.nn.leaky_relu(fh[src] * ft[dst], SLOPE)
        e = jnp.einsum('ehd,xhd->eh', e, attn)
        deg = jax.ops.segment_sum(jnp.ones_like(dst, dtype=feat.dtype), dst, num_segments=n)
        log_in = jnp.log(deg)
        e = e * log_in[dst][:, None] / HD
        emax = jax.ops.segment_max(e, dst, num_segments=n)
        ex = jnp.exp(e - emax[dst])
        esum = jax.ops.segment_sum(ex, dst, num_segments=n)
        a = ex / esum[dst]
        feat0 = fe
        f = feat0
        for _ in range(HOP):
            msg = f[src] * a[:, :, None]
            agg = jax.ops.segment_sum(msg, dst, num_segments=n)
            f = (1.0 - ALPHA) * agg + ALPHA * feat0
        rst = f + feat.reshape(n, H, HD)
        rst = rst.reshape(n, D_OUT)
        x = _layer_norm(rst, ln2_g, ln2_b)
        ff = jax.nn.relu(x @ W_ff1.T + b_ff1) @ W_ff2.T + b_ff2
        return ff + rst

    def _L1_gnn_ref(x, edge_index, edge_attr, W0, b0, W1, b1, W2, b2):
        import jax, jax.numpy as jnp
        import numpy as np
        N = 50000
        E = 50000
        F = 128

        def _gcn_norm(src, dst, w, n):
            loops = jnp.arange(n, dtype=src.dtype)
            src_a = jnp.concatenate([src, loops])
            dst_a = jnp.concatenate([dst, loops])
            w_a = jnp.concatenate([w, jnp.ones((n,), w.dtype)])
            deg = jax.ops.segment_sum(w_a, dst_a, num_segments=n)
            dinv = jnp.where(deg > 0, jax.lax.rsqrt(deg), 0.0)
            norm = dinv[src_a] * w_a * dinv[dst_a]
            return (src_a, dst_a, norm)

        def _gcn_conv(x, src_a, dst_a, norm, W, b, n):
            h = x @ W
            msg = h[src_a] * norm[:, None]
            out = jax.ops.segment_sum(msg, dst_a, num_segments=n)
            return out + b
        n = x.shape[0]
        src, dst = (edge_index[0], edge_index[1])
        src_a, dst_a, norm = _gcn_norm(src, dst, edge_attr, n)
        h = jax.nn.relu(_gcn_conv(x, src_a, dst_a, norm, W0, b0, n))
        h = jax.nn.relu(_gcn_conv(h, src_a, dst_a, norm, W1, b1, n))
        return _gcn_conv(h, src_a, dst_a, norm, W2, b2, n)
    edge_index = jnp.stack([src, dst])
    h = jnp.maximum(_layernorm(x, axis=-1), 0.0)
    x = x + _L0_gnn_ref(h, src, dst, L0_gnn_ln1_g, L0_gnn_ln1_b, L0_gnn_W_head, L0_gnn_W_tail, L0_gnn_W_ent, L0_gnn_attn, L0_gnn_ln2_g, L0_gnn_ln2_b, L0_gnn_W_ff1, L0_gnn_b_ff1, L0_gnn_W_ff2, L0_gnn_b_ff2)
    h = jnp.maximum(_layernorm(x, axis=-1), 0.0)
    x = x + _L1_gnn_ref(h, edge_index, edge_weight, L1_gnn_W0, L1_gnn_b0, L1_gnn_W1, L1_gnn_b1, L1_gnn_W2, L1_gnn_b2)
    return x

_drawn_inputs = setup_inputs


def setup_inputs(seed=0):
    import zlib

    import numpy as np

    out = dict(_drawn_inputs(seed))
    spreads = {'L0_gnn_ln1_g': (1.0, 0.6),
     'L0_gnn_ln1_b': (0.0, 0.1),
     'L0_gnn_ln2_g': (1.0, 0.2),
     'L0_gnn_ln2_b': (0.0, 0.282),
     'L0_gnn_b_ff1': (0.0, 0.1),
     'L0_gnn_b_ff2': (0.0, 0.1),
     'L1_gnn_b0': (0.0, 0.269),
     'L1_gnn_b1': (0.0, 0.1),
     'L1_gnn_b2': (0.0, 0.1)}
    factors = {'edge_weight': 48.759, 'L0_gnn_W_head': 8.0, 'L0_gnn_W_tail': 8.0, 'L0_gnn_attn': 8.0}
    for name, (base, spread) in spreads.items():
        noise = np.random.default_rng([zlib.crc32(name.encode()), seed]).standard_normal(out[name].shape)
        drawn = base * np.exp(spread * noise) if base else spread * noise
        out[name] = jnp.asarray(drawn.astype(out[name].dtype))
    for name, factor in factors.items():
        out[name] = (out[name] * factor).astype(out[name].dtype)
    return out
```

```python
from contextlib import ExitStack

import concourse.bass as bass
from concourse import mybir

F32 = mybir.dt.float32
BF16 = mybir.dt.bfloat16
I32 = mybir.dt.int32
ALU = mybir.AluOpType
ACT = mybir.ActivationFunctionType
AX = mybir.AxisListType

P = 128
N_NODES = 3125
N_EDGES = 100000
F = 128
BN = 125
NB = N_NODES // BN
HEADS, HD = 8, 16
D_FF = 4 * F
FFC = D_FF // P
HOPS, ALPHA, SLOPE, EPS = 5, 0.15, 0.2, 1e-5
LAYERS = 3
TILES = -(-N_EDGES // P)
CHUNKS = 16
ITEM_COUNT = N_EDGES // P + NB
G = 4
SLOTS = 4
PER_ITER = G * SLOTS
ITEMS = -(-ITEM_COUNT // PER_ITER) * PER_ITER
ITERS = ITEMS // PER_ITER
GROUPS = ITERS * SLOTS
CI = ITEMS // CHUNKS
L = CI * P
KB = -(-ITEMS // P)
BANK = 512
BPB = BANK // F
BANKS = -(-NB // BPB)
BIG = 1e30
PROJ_BATCHES = -(-NB // BANKS)
EXP_PARTS = 3
MASKS = 5
assert PER_ITER == CHUNKS and ITEMS % CHUNKS == 0 and CHUNKS * HEADS == P and NB * BN == N_NODES
assert (NB + 1) * F <= BANKS * BANK and BANKS < 8


def bank_buckets(k):
    return k * BPB, min(NB, (k + 1) * BPB)


def gnn_stack(nc, a, out):
    ctx = ExitStack()
    with ctx:
        def sb(name, shape, dt=F32):
            return ctx.enter_context(nc.sbuf_tensor(name, shape, dt))

        def sem(name):
            return ctx.enter_context(nc.semaphore(name))

        def dram(name, shape, dt=F32):
            return nc.dram_tensor(name, shape, dt, kind="Internal").ap()

        tab_head = dram("tab_head", (N_NODES, F))
        tab_tail = dram("tab_tail", (N_NODES, F))
        tab_f = dram("tab_f", (N_NODES, F))
        item_bucket_d = dram("item_bucket_d", (KB * P,), I32)
        item_dst_d = dram("item_dst_d", (KB * P, P), I32)

        ps = ctx.enter_context(nc.psum_tensor("ps", [P, 8 * BANK], F32))

        def bank(k, n=BANK):
            return ps[:, k * BANK:k * BANK + n]

        small = bank(7)

        h0 = sb("h0", [P, NB, F])
        fe_a = sb("fe_a", [P, NB, F])
        src_it = sb("src_it", [P, KB * P], I32)
        dst_it = sb("dst_it", [P, KB * P], I32)
        dloc = sb("dloc", [P, KB * P])
        w_it = sb("w_it", [P, KB * P, 2])
        ex_it = sb("ex_it", [P, ITEMS, HEADS])
        bucket_row = sb("bucket_row", [1, KB * P], I32)
        stage_a = sb("stage_a", [P, SLOTS, G], I32)
        stage_b = sb("stage_b", [P, SLOTS, G], I32)
        ident = sb("ident", [P, P])
        iota_bn = sb("iota_bn", [P, BN])
        ones = sb("ones", [P, P])
        zeros = sb("zeros", [1, BANK])
        w_raw = sb("w_raw", [P, 3, F])
        w_qkv = sb("w_qkv", [P, 3 * F])
        ff1_raw = sb("ff1_raw", [P, FFC, F])
        ff1_t = sb("ff1_t", [P, D_FF])
        ff2_raw = sb("ff2_raw", [P, D_FF])
        ff2_t = sb("ff2_t", [P, FFC, F])
        w_gcn = sb("w_gcn", [P, LAYERS, F])
        b_ff1 = sb("b_ff1", [P, FFC])
        rowvec = sb("rowvec", [P, 9, F])
        G1, B1, G2, B2, BFF2, BG0, BG1, BG2, ATTN = range(9)
        deg = sb("deg", [P, NB, 2])
        log_deg = sb("log_deg", [P, NB])
        dinv = sb("dinv", [P, NB])
        inv_sum = sb("inv_sum", [P, NB, HEADS])
        stat = sb("stat", [P, 4, NB])
        thr = sb("thr", [P, 3, NB])
        thr_i = sb("thr_i", [P, NB], I32)
        item_f = sb("item_f", [P, 4, KB])
        item_t = sb("item_t", [P, KB], I32)
        item_b = sb("item_b", [P, KB], I32)
        ge = sb("ge", [P, KB, NB])
        ends = sb("ends", [P, 4])
        rows = sb("rows", [1, 4, HEADS, CHUNKS])
        carry = sb("carry", [1, 5, HEADS * CHUNKS])
        carry_col = sb("carry_col", [P, 2])

        U = sb("U", [P, 3 * L])
        gap = sb("gap", [P, L + 1], BF16)
        e_sc, fw, bw = (U[:, k * L:(k + 1) * L] for k in range(3))
        key = bw.bitcast(I32)
        at = [0]

        def part(n):
            at[0] += n
            assert at[0] <= 3 * L
            return U[:, at[0] - n:at[0]]

        node = [part(NB * F).rearrange("p (b f) -> p b f", f=F) for _ in range(3)]
        x_sb, na, nb_ = node
        hT = part(NB * BN)
        ga_flat = part(SLOTS * G * F)
        ga = ga_flat.rearrange("p (s g f) -> p s g f", s=SLOTS, g=G)
        ffa = ga_flat[:, 0:FFC * BPB * BN].rearrange("p (c n) -> p c n", c=FFC)
        gb = part(SLOTS * G * F).rearrange("p (s g f) -> p s g f", s=SLOTS, g=G)
        hot = part(SLOTS * G * BN).rearrange("p (s g f) -> p s g f", s=SLOTS, g=G)
        dst_all = ga_flat[:, 0:TILES].bitcast(I32)
        dst_allf = hT[:, 0:TILES]
        row_raw = [node[k].rearrange("p b f -> p (b f)")[:, 0:KB * P].rearrange("p (k e) -> p k e", e=P)
                   for k in range(3)]
        row_i = [row_raw[0].bitcast(I32), row_raw[1].bitcast(I32), row_raw[2]]
        row_f = [node[k].rearrange("p b f -> p (b f)")[:, KB * P:2 * KB * P].rearrange("p (k e) -> p k e", e=P)
                 for k in range(3)]

        consts_in = sem("consts_in")
        dst_in = sem("dst_in")
        x_in = sem("x_in")
        masks_set = sem("masks_set")
        dve_link = sem("dve_link")
        counted = sem("counted")
        summed = sem("summed")
        tiles_known = sem("tiles_known")
        rows_in = sem("rows_in")
        rows_ready = sem("rows_ready")
        rows_turned = sem("rows_turned")
        items_ready = sem("items_ready")
        bucket_out = sem("bucket_out")
        bucket_in = sem("bucket_in")
        key_out = sem("key_out")
        key_in = sem("key_in")
        key_free = sem("key_free")
        weights_turned = sem("weights_turned")
        weights_ready = sem("weights_ready")
        staged = sem("staged")
        begun = sem("begun")
        got = [sem(f"got{k}") for k in range(SLOTS)]
        zeros_set = sem("zeros_set")
        scores_done = sem("scores_done")
        tails_out = sem("tails_out")
        sums_out = sem("sums_out")
        gcn_done = sem("gcn_done")
        msgs_ready = sem("msgs_ready")
        groups_done = sem("groups_done")
        step_link = sem("step_link")
        var_ready = sem("var_ready")
        std_ready = sem("std_ready")
        logs_ready = sem("logs_ready")
        h_ready = sem("h_ready")
        turned = sem("turned")
        turned_out = sem("turned_out")
        proj_done = sem("proj_done")
        proj_out = sem("proj_out")
        table_ready = sem("table_ready")
        table_out = sem("table_out")
        score_turned = sem("score_turned")
        score_out = sem("score_out")
        ends_ready = sem("ends_ready")
        ends_turned = sem("ends_turned")
        carry_ready = sem("carry_ready")
        carry_turned = sem("carry_turned")
        shifted = sem("shifted")
        exps_ready = sem("exps_ready")
        exp_turned = sem("exp_turned")
        exp_out = sem("exp_out")
        ff1_done = sem("ff1_done")
        ff1_out = sem("ff1_out")
        ff2_done = sem("ff2_done")
        ff2_out = sem("ff2_out")
        x_again = sem("x_again")
        y_ready = sem("y_ready")
        y_out = sem("y_out")

        DEG, SCORE, HOP0, CONV0 = 0, 1, 2, 2 + HOPS
        PASSES = CONV0 + LAYERS

        def got_before(p):
            return 0 if p <= SCORE else 16 * G * ITERS * (p - SCORE + 1)

        def staged_before(p):
            return 0 if p == SCORE else (p - SCORE + 1) * GROUPS

        def msgs_before(s):
            return 0 if s == 0 else (2 * s - 1) * GROUPS

        def proj_view(n, col):
            return ps[0:BN, 0:n * BANK].rearrange("p (k n) -> p k n", n=BANK)[:, :, col * F:(col + 1) * F]

        def sums_pass(p):
            return 0 if p == DEG else p - 1

        def nodes_of(table):
            return table.rearrange("(b p) f -> p b f", p=BN)

        LOADS = 3 + 3 + LAYERS + 9

        block = ctx.enter_context(nc.Block())

        @block.sync
        def _(sp):
            sp.dma_start(dst_all, a["dst"].rearrange("(p t) -> p t", p=P)).then_inc(dst_in, 16)
            sp.dma_start(h0[0:BN], nodes_of(a["x"])).then_inc(x_in, 16)
            loads = [(w_raw[:, k, :], a[n]) for k, n in enumerate(("L0_gnn_W_head", "L0_gnn_W_tail", "L0_gnn_W_ent"))]
            loads += [(ff1_raw[:], a["L0_gnn_W_ff1"].rearrange("(c p) f -> p c f", p=P)),
                      (ff2_raw[:], a["L0_gnn_W_ff2"]),
                      (b_ff1[:], a["L0_gnn_b_ff1"].rearrange("(c p) -> p c", p=P))]
            loads += [(w_gcn[:, k, :], a[f"L1_gnn_W{k}"]) for k in range(LAYERS)]
            for k, n in ((G1, "L0_gnn_ln1_g"), (B1, "L0_gnn_ln1_b"), (G2, "L0_gnn_ln2_g"), (B2, "L0_gnn_ln2_b"),
                         (BFF2, "L0_gnn_b_ff2"), (BG0, "L1_gnn_b0"), (BG1, "L1_gnn_b1"), (BG2, "L1_gnn_b2")):
                loads.append((rowvec[:, k, :], a[n].partition_broadcast(P)))
            loads.append((rowvec[:, ATTN, :], a["L0_gnn_attn"].rearrange("a h d -> (a h d)").partition_broadcast(P)))
            assert len(loads) == LOADS
            for to, of in loads:
                sp.dma_start(to, of, allow_slow_non_contiguous=True).then_inc(consts_in, 16)
            sp.wait_ge(tiles_known, 1)
            sp.dma_start(item_bucket_d.rearrange("(k p) -> p k", p=P), item_b[:],
                         allow_slow_non_contiguous=True).then_inc(bucket_out, 16)
            sp.wait_ge(bucket_out, 16)
            sp.dma_start(bucket_row[:], item_bucket_d.rearrange("(a n) -> a n", a=1)).then_inc(bucket_in, 16)
            sp.wait_ge(rows_in, 3 * KB * 16)
            sp.dma_start(item_dst_d.rearrange("(k p) e -> p k e", p=P), row_i[1]).then_inc(key_out, 16)
            for k, (table, rows_) in enumerate(((tab_head, na), (tab_tail, nb_), (tab_f, x_sb))):
                sp.wait_ge(table_ready, k + 1)
                sp.dma_start(nodes_of(table), rows_[0:BN]).then_inc(table_out, 16)
            sp.wait_ge(key_out, 16)
            sp.wait_ge(key_free, 1)
            chunks = item_dst_d.rearrange("(r c) e -> c r e", c=CHUNKS)[:, 0:CI, :]
            for c in range(CHUNKS):
                sp.dma_start(key[c * HEADS:(c + 1) * HEADS, :].rearrange("p (r e) -> p r e", e=P),
                             chunks[c].partition_broadcast(HEADS)).then_inc(key_in, 16)
            sp.wait_ge(exp_out, -(-CI // BPB))
            sp.dma_start(x_sb[0:BN], nodes_of(a["x"])).then_inc(x_again, 16)
            for k in range(HOPS - 1 + LAYERS):
                sp.wait_ge(table_ready, 4 + k)
                sp.dma_start(nodes_of(tab_f), (na if k < HOPS - 1 else nb_)[0:BN]).then_inc(table_out, 16)
            sp.wait_ge(y_ready, 1)
            sp.dma_start(nodes_of(out), na[0:BN]).then_inc(y_out, 16)
            sp.wait_ge(y_out, 16)
            sp.wait_ge(table_out, 16 * (2 + HOPS + LAYERS))

        @block.gpsimd
        def _(pool):
            pool.memset(ident[:], 0.0).then_inc(masks_set, 1)
            pool.wait_ge(masks_set, 1)
            pool.affine_select(out=ident[:], in_=ident[:], compare_op=ALU.not_equal, fill=1.0, base=0,
                               pattern=[[-1, P]], channel_multiplier=1).then_inc(masks_set, 1)
            pool.iota(iota_bn[:], pattern=[[1, BN]], base=0, channel_multiplier=0,
                      allow_small_or_imprecise_dtypes=True).then_inc(masks_set, 1)
            pool.iota(item_t[:], pattern=[[P, KB]], base=0, channel_multiplier=1).then_inc(masks_set, 1)
            pool.iota(thr[:, 0, :], pattern=[[1, NB]], base=1, channel_multiplier=0,
                      allow_small_or_imprecise_dtypes=True).then_inc(masks_set, 1)
            pool.wait_ge(tiles_known, 1)
            for k in range(KB):
                for name, to in zip(("src", "dst", "edge_weight"), row_i):
                    pool.indirect_dma_start(to[:, k, :], None, a[name].rearrange("(t e) -> t e", e=P),
                                            bass.IndirectOffsetOnAxis(ap=item_t[:, k:k + 1], axis=0)).then_inc(rows_in, 16)

            def gather_pass(p, tables):
                with pool.Fori(0, ITERS) as r:
                    for k in range(SLOTS):
                        n = len(tables)
                        pool.wait_ge(staged, r * (n * SLOTS) + (staged_before(p) + n * (k + 1)))
                        pool.sem_inc(begun, 1)
                        for table, stage, to in tables:
                            for j in range(G):
                                pool.indirect_dma_start(
                                    to[:, k, j, :], None, table,
                                    bass.IndirectOffsetOnAxis(ap=stage[:, k, j:j + 1], axis=0)).then_inc(got[k], 16)

            pool.wait_ge(table_out, 3 * 16)
            gather_pass(SCORE, ((tab_head, stage_a, ga), (tab_tail, stage_b, gb)))
            for n in range(HOPS + LAYERS):
                pool.wait_ge(table_out, 16 * (3 + n))
                gather_pass(HOP0 + n, ((tab_f, stage_a, ga),))

        @block.scalar
        def _(act):
            def std(n):
                act.wait_ge(var_ready, n)
                nc.scalar.activation(stat[0:BN, 2, :], stat[0:BN, 1, :], ACT.Sqrt).then_inc(std_ready, 1)

            def turn_out(n):
                for k in range(BANKS):
                    b0, b1 = bank_buckets(k)
                    act.wait_ge(turned, n * BANKS + k + 1)
                    nc.scalar.copy(hT[:, b0 * BN:b1 * BN], bank(k, (b1 - b0) * BN)).then_inc(turned_out, 1)

            def stage_pass(p, lists):
                with act.Fori(0, ITERS) as r:
                    for k in range(SLOTS):
                        if p == SCORE:
                            act.wait_ge(scores_done, r * SLOTS + (k + 1))
                        else:
                            act.wait_ge(groups_done, r * SLOTS + (sums_pass(p) * GROUPS + k + 1))
                        for stage, index in lists:
                            nc.scalar.copy(stage[:, k, :],
                                           index[:, bass.ds(r * PER_ITER + k * G, G)]).then_inc(staged, 1)

            act.wait_ge(logs_ready, 1)
            nc.scalar.activation(log_deg[0:BN], log_deg[0:BN], ACT.Ln).then_inc(logs_ready, 1)
            act.wait_ge(var_ready, 1)
            nc.scalar.activation(dinv[0:BN], dinv[0:BN], ACT.Sqrt).then_inc(std_ready, 1)
            std(2)
            std(3)
            turn_out(0)
            for q in range(PROJ_BATCHES):
                b0, b1 = q * BANKS, min(NB, (q + 1) * BANKS)
                act.wait_ge(proj_done, q + 1)
                for col, to in ((0, na), (2, x_sb)):
                    nc.scalar.copy(to[0:BN, b0:b1, :], proj_view(b1 - b0, col)).then_inc(proj_out, 1)
            act.wait_ge(items_ready, 3)
            stage_pass(SCORE, ((stage_a, src_it), (stage_b, dst_it)))
            act.wait_ge(table_out, 3 * 16)
            for n in range(-(-CI // BPB)):
                j0, j1 = n * BPB, min(CI, (n + 1) * BPB)
                act.wait_ge(score_turned, n + 1)
                nc.scalar.copy(e_sc[:, j0 * P:j1 * P], bank(n % BANKS, (j1 - j0) * P)).then_inc(score_out, 1)
            act.wait_ge(shifted, 1)
            for n in range(EXP_PARTS):
                w = L // EXP_PARTS
                nc.scalar.activation(e_sc[:, n * w:(n + 1) * w], e_sc[:, n * w:(n + 1) * w],
                                     ACT.Exp).then_inc(exps_ready, 1)
            act.wait_ge(exp_out, -(-CI // BPB))
            for n in range(HOPS):
                stage_pass(HOP0 + n, ((stage_a, src_it),))
            std(4)
            turn_out(1)
            for q in range(BANKS):
                b0, b1 = bank_buckets(q)
                n = (b1 - b0) * BN
                if q:
                    act.wait_ge(ff2_done, q)
                for c in range(FFC):
                    act.wait_ge(ff1_done, q * FFC + c + 1)
                    nc.scalar.activation(ffa[:, c, 0:n], bank(c, n), ACT.Relu,
                                         bias=b_ff1[:, c:c + 1]).then_inc(ff1_out, 1)
            std(5)
            for n in range(LAYERS):
                turn_out(2 + n)
                stage_pass(CONV0 + n, ((stage_a, src_it),))

        @block.tensor
        def _(pe):
            def clear(banks):
                for k in banks:
                    nc.tensor.matmul(bank(k), zeros[:, 0:P], zeros[:], start=True, stop=False, skip_group_check=True)

            def sum_pass(p):
                s = sums_pass(p)
                with pe.Fori(0, ITERS) as r:
                    for k in range(SLOTS):
                        per = 1 if p == DEG else 2
                        pe.wait_ge(msgs_ready, r * (per * SLOTS) + (msgs_before(s) + per * (k + 1)))
                        for j in range(G):
                            i = r * PER_ITER + (k * G + j)
                            b = pe.value_load(bucket_row[0:1, bass.ds(i, 1)], min_val=0, max_val=NB)
                            if p == DEG:
                                mm = nc.tensor.matmul(ps[0:BN, bass.ds(b * 2 + 7 * BANK, 2)], hot[:, k, j, :],
                                                      w_it[:, bass.ds(i, 1), :].rearrange("p i c -> p (i c)"),
                                                      start=False, stop=False, skip_group_check=True)
                                continue
                            if p == HOP0:
                                nc.tensor.matmul(ps[0:BN, bass.ds(b * HEADS + 7 * BANK, HEADS)], hot[:, k, j, :],
                                                 ex_it[:, bass.ds(i, 1), :].rearrange("p i c -> p (i c)"),
                                                 start=False, stop=False, skip_group_check=True)
                            mm = nc.tensor.matmul(ps[0:BN, bass.ds(b * F, F)], hot[:, k, j, :], ga[:, k, j, :],
                                                  start=False, stop=False, skip_group_check=True)
                        mm.then_inc(groups_done, 1)

            def turn(n, rows_):
                pe.wait_ge(h_ready, n + 1)
                for k in range(BANKS):
                    b0, b1 = bank_buckets(k)
                    for b in range(b0, b1):
                        t = nc.tensor.transpose(bank(k)[:, (b - b0) * BN:(b - b0 + 1) * BN], rows_[0:BN, b, :],
                                                ident[0:BN, 0:BN])
                    t.then_inc(turned, 1)

            pe.sem_inc(groups_done, SLOTS)
            pe.wait_ge(masks_set, MASKS)
            pe.wait_ge(zeros_set, 2)
            pe.wait_ge(counted, 1)
            nc.tensor.matmul(small[:, 0:NB], ones[:], thr[:, 1, :], start=True, stop=True).then_inc(summed, 1)
            pe.wait_ge(consts_in, 16 * LOADS)
            for k in range(3):
                nc.tensor.transpose(bank(0)[:, k * F:(k + 1) * F], w_raw[:, k, :], ident[:])
            for c in range(FFC):
                nc.tensor.transpose(bank(1)[:, c * P:(c + 1) * P], ff1_raw[:, c, :], ident[:])
            for c in range(FFC):
                t = nc.tensor.transpose(bank(2)[:, c * F:(c + 1) * F], ff2_raw[:, c * P:(c + 1) * P], ident[:])
            t.then_inc(weights_turned, 1)
            pe.wait_ge(weights_ready, 3)
            pe.wait_ge(rows_ready, 3)
            for v in range(4):
                rows_ = (row_f[0], row_f[1], row_f[2], row_raw[2])[v]
                if v >= 1:
                    pe.wait_ge(items_ready, v)
                for k in range(KB):
                    t = nc.tensor.transpose(bank(k, P), rows_[:, k, :], ident[:])
                t.then_inc(rows_turned, 1)
            pe.wait_ge(items_ready, 4)
            pe.wait_ge(bucket_in, 16)
            clear([7])
            sum_pass(DEG)
            turn(0, na)
            pe.wait_ge(turned_out, BANKS)
            for q in range(PROJ_BATCHES):
                b0, b1 = q * BANKS, min(NB, (q + 1) * BANKS)
                if q:
                    pe.wait_ge(proj_out, 2 * q)
                    pe.wait_ge(tails_out, 2 * q)
                for b in range(b0, b1):
                    mm = nc.tensor.matmul(bank(b - b0, 3 * F)[0:BN], hT[:, b * BN:(b + 1) * BN], w_qkv[:],
                                          start=True, stop=True)
                mm.then_inc(proj_done, 1)
            pe.wait_ge(proj_out, 2 * PROJ_BATCHES)
            pe.wait_ge(tails_out, 2 * PROJ_BATCHES)
            pe.wait_ge(scores_done, SLOTS + GROUPS)
            by_chunk = ex_it[:].rearrange("p (j c) h -> p j (c h)", c=CHUNKS)
            for n in range(-(-CI // BPB)):
                if n >= BANKS:
                    pe.wait_ge(score_out, n - BANKS + 1)
                for j in range(n * BPB, min(CI, (n + 1) * BPB)):
                    t = nc.tensor.transpose(bank(n % BANKS)[:, (j % BPB) * P:(j % BPB + 1) * P], by_chunk[:, j, :], ident[:])
                t.then_inc(score_turned, 1)
            for n in range(2):
                pe.wait_ge(ends_ready, n + 1)
                for k in range(4):
                    t = nc.tensor.matmul(small[0:1, k * P:(k + 1) * P], ends[:, k:k + 1], ident[:],
                                         start=True, stop=True)
                t.then_inc(ends_turned, 1)
                pe.wait_ge(carry_ready, n + 1)
                nc.tensor.matmul(bank(0, 1), carry[0:1, 4, :], ones[0:1, 0:1], start=True,
                                 stop=True).then_inc(carry_turned, 1)
            for n in range(-(-CI // BPB)):
                pe.wait_ge(exps_ready, -(-min(CI, (n + 1) * BPB) * EXP_PARTS // CI))
                if n == 0:
                    pe.wait_ge(score_out, -(-CI // BPB))
                if n >= BANKS:
                    pe.wait_ge(exp_out, n - BANKS + 1)
                for j in range(n * BPB, min(CI, (n + 1) * BPB)):
                    t = nc.tensor.transpose(bank(n % BANKS)[:, (j % BPB) * P:(j % BPB + 1) * P],
                                            e_sc[:, j * P:(j + 1) * P], ident[:])
                t.then_inc(exp_turned, 1)
            pe.wait_ge(exp_out, -(-CI // BPB))
            clear([7])
            for n in range(HOPS):
                if n:
                    pe.wait_ge(sums_out, n)
                clear(range(BANKS))
                sum_pass(HOP0 + n)
            turn(1, nb_)
            pe.wait_ge(turned_out, 2 * BANKS)
            for q in range(BANKS):
                b0, b1 = bank_buckets(q)
                n = (b1 - b0) * BN
                for c in range(FFC):
                    if q:
                        pe.wait_ge(ff1_out, (q - 1) * FFC + c + 1)
                    nc.tensor.matmul(bank(c, n), ff1_t[:, c * P:(c + 1) * P], hT[:, b0 * BN:b1 * BN],
                                     start=True, stop=True).then_inc(ff1_done, 1)
                pe.wait_ge(ff1_out, (q + 1) * FFC)
                if q >= 2:
                    pe.wait_ge(ff2_out, q - 1)
                for b in range(b0, b1):
                    for c in range(FFC):
                        mm = nc.tensor.matmul(bank(4 + q % 2)[0:BN, (b - b0) * F:(b - b0 + 1) * F],
                                              ffa[:, c, (b - b0) * BN:(b - b0 + 1) * BN], ff2_t[:, c, :],
                                              start=(c == 0), stop=(c == FFC - 1))
                mm.then_inc(ff2_done, 1)
            for n in range(LAYERS):
                turn(2 + n, na)
                for k in range(BANKS):
                    pe.wait_ge(turned_out, (2 + n) * BANKS + k + 1)
                    b0, b1 = bank_buckets(k)
                    for b in range(b0, b1):
                        mm = nc.tensor.matmul(bank(k)[0:BN, (b - b0) * F:(b - b0 + 1) * F],
                                              hT[:, b * BN:(b + 1) * BN], w_gcn[:, n, :], start=True, stop=True)
                    mm.then_inc(gcn_done, 1)
                pe.wait_ge(table_ready, 3 + HOPS + n)
                clear(range(BANKS))
                sum_pass(CONV0 + n)

        @block.vector
        def _(dve):
            count = [0]

            def link(ins):
                count[0] += 1
                ins.then_inc(dve_link, 1)
                dve.wait_ge(dve_link, count[0])

            v = nc.vector

            def tt(to, x, y, op):
                link(v.tensor_tensor(to, x, y, op))

            def layernorm(to, x, scratch, n):
                link(v.tensor_reduce(stat[0:BN, 0, :], x[0:BN], AX.X, ALU.add))
                link(v.tensor_scalar(stat[0:BN, 0, :], stat[0:BN, 0, :], 1.0 / F, None, ALU.mult))
                tt(to[0:BN], x[0:BN], over_f(stat[0:BN, 0, :]), ALU.subtract)
                tt(scratch[0:BN], to[0:BN], to[0:BN], ALU.mult)
                link(v.tensor_reduce(stat[0:BN, 3, :], scratch[0:BN], AX.X, ALU.add))
                v.tensor_scalar(stat[0:BN, 1, :], stat[0:BN, 3, :], 1.0 / F, EPS, ALU.mult,
                                ALU.add).then_inc(var_ready, 1)
                dve.wait_ge(std_ready, n)
                link(v.reciprocal(stat[0:BN, 3, :], stat[0:BN, 2, :]))
                tt(to[0:BN], to[0:BN], over_f(stat[0:BN, 3, :]), ALU.mult)

            def over_f(x):
                return x.unsqueeze(2).to_broadcast([BN, NB, F])

            def over_nodes(k):
                return rowvec[0:BN, k:k + 1, :].to_broadcast([BN, NB, F])

            def onehots(r, k):
                i = r * PER_ITER + k * G
                return v.tensor_tensor(hot[:, k], dloc[:, bass.ds(i, G)].unsqueeze(2).to_broadcast([P, G, BN]),
                                       iota_bn[:].unsqueeze(1).to_broadcast([P, G, BN]), ALU.is_equal)

            def message_pass(p):
                s = sums_pass(p)
                with dve.Fori(0, ITERS) as r:
                    for k in range(SLOTS):
                        if p == DEG:
                            dve.wait_ge(groups_done, r * SLOTS + (s * GROUPS + k + 1))
                            onehots(r, k).then_inc(msgs_ready, 1)
                            continue
                        dve.wait_ge(got[k], r * (16 * G) + (got_before(p) + 16 * G))
                        onehots(r, k).then_inc(msgs_ready, 1)
                        i = r * PER_ITER + k * G
                        if p < CONV0:
                            rows_ = ga[:, k].rearrange("p g (h d) -> p (g h) d", h=HEADS)
                            by = ex_it[:, bass.ds(i, G), :].rearrange("p g h -> p (g h)").unsqueeze(2).to_broadcast(
                                [P, G * HEADS, HD])
                        else:
                            rows_ = ga[:, k]
                            by = w_it[:, bass.ds(i, G), 1:2].to_broadcast([P, G, F])
                        v.tensor_tensor(rows_, rows_, by, ALU.mult).then_inc(msgs_ready, 1)
                dve.wait_ge(groups_done, SLOTS + (s + 1) * GROUPS)

            dve.sem_inc(scores_done, SLOTS)
            v.memset(zeros[:], 0.0).then_inc(zeros_set, 1)
            v.memset(ones[:], 1.0).then_inc(zeros_set, 1)
            link(v.memset(w_it[:, :, 0:1], 1.0))
            dve.wait_ge(masks_set, MASKS)
            dve.wait_ge(dst_in, 16)
            link(v.tensor_copy(dst_allf, dst_all))
            for b in range(NB):
                link(v.tensor_scalar(nb_.rearrange("p b f -> p (b f)")[:, 0:TILES], dst_allf, float(BN * (b + 1)),
                                     0.0, ALU.is_lt, ALU.add, accum_out=thr[:, 1, b:b + 1]))
            dve.sem_inc(counted, 1)
            dve.wait_ge(summed, 1)
            link(v.tensor_copy(thr_i[:], small[:, 0:NB]))
            link(v.tensor_scalar(thr_i[:], thr_i[:], P.bit_length() - 1, None, ALU.arith_shift_right))
            link(v.tensor_copy(thr[:, 2, :], thr_i[:]))
            tt(thr[:, 2, :], thr[:, 2, :], thr[:, 0, :], ALU.add)
            link(v.tensor_scalar(item_b[:], item_t[:], CHUNKS - 1, None, ALU.bitwise_and))
            link(v.tensor_scalar(item_t[:], item_t[:], CHUNKS.bit_length() - 1, None, ALU.arith_shift_right))
            link(v.tensor_copy(item_f[:, 1, :], item_b[:]))
            link(v.tensor_copy(item_f[:, 2, :], item_t[:]))
            link(v.scalar_tensor_tensor(out=item_f[:, 0, :], in0=item_f[:, 1, :], scalar=float(CI),
                                        in1=item_f[:, 2, :], op0=ALU.mult, op1=ALU.add))
            tt(ge[:], item_f[:, 0, :].unsqueeze(2).to_broadcast([P, KB, NB]),
               thr[:, 2, :].unsqueeze(1).to_broadcast([P, KB, NB]), ALU.is_ge)
            link(v.tensor_reduce(item_f[:, 1, :], ge[:], AX.X, ALU.add))
            tt(item_f[:, 2, :], item_f[:, 0, :], item_f[:, 1, :], ALU.subtract)
            link(v.tensor_copy(item_b[:], item_f[:, 1, :]))
            link(v.tensor_scalar(item_f[:, 3, :], item_f[:, 1, :], float(BN), None, ALU.mult))
            v.tensor_scalar(item_t[:], item_f[:, 2, :], float(TILES - 1), None, ALU.min).then_inc(tiles_known, 1)
            dve.wait_ge(weights_turned, 1)
            v.tensor_copy(w_qkv[:], bank(0, 3 * F)).then_inc(weights_ready, 1)
            v.tensor_copy(ff1_t[:], bank(1)).then_inc(weights_ready, 1)
            v.tensor_copy(ff2_t[:].rearrange("p c f -> p (c f)"), bank(2)).then_inc(weights_ready, 1)
            dve.wait_ge(rows_in, 3 * KB * 16)
            v.tensor_copy(row_f[0], row_i[0]).then_inc(rows_ready, 1)
            v.tensor_scalar(row_f[1], row_i[1], float(N_NODES - 1), None, ALU.min).then_inc(rows_ready, 1)
            v.tensor_tensor(row_f[2], row_i[1], item_f[:, 3, :].unsqueeze(2).to_broadcast([P, KB, P]),
                            ALU.subtract).then_inc(rows_ready, 1)
            turned_rows = ps[:, 0:KB * BANK].rearrange("p (k n) -> p k n", n=BANK)[:, :, 0:P]
            for n, to in enumerate((src_it[:], dst_it[:], dloc[:], w_it[:, :, 1])):
                dve.wait_ge(rows_turned, n + 1)
                v.tensor_copy(to.rearrange("p (k e) -> p k e", e=P), turned_rows).then_inc(items_ready, 1)
            dve.wait_ge(items_ready, 4)
            message_pass(DEG)
            link(v.tensor_copy(deg[0:BN], ps[0:BN, 7 * BANK:7 * BANK + 2 * NB].rearrange("p (b c) -> p b c", c=2)))
            v.tensor_scalar(log_deg[0:BN], deg[0:BN, :, 0], 1.0, None, ALU.max).then_inc(logs_ready, 1)
            link(v.tensor_scalar(stat[0:BN, 0, :], deg[0:BN, :, 1], 1.0, None, ALU.add))
            link(v.tensor_scalar(stat[0:BN, 1, :], stat[0:BN, 0, :], 0.0, None, ALU.is_gt))
            v.tensor_scalar(dinv[0:BN], stat[0:BN, 0, :], 1e-30, None, ALU.max).then_inc(var_ready, 1)
            dve.wait_ge(std_ready, 1)
            link(v.reciprocal(dinv[0:BN], dinv[0:BN]))
            tt(dinv[0:BN], dinv[0:BN], stat[0:BN, 1, :], ALU.mult)
            dve.wait_ge(logs_ready, 2)
            link(v.tensor_scalar(log_deg[0:BN], log_deg[0:BN], 1.0 / HD, None, ALU.mult))
            dve.wait_ge(x_in, 16)
            dve.wait_ge(key_out, 16)
            layernorm(h0, h0, na, 2)
            link(v.tensor_scalar(h0[0:BN], h0[0:BN], 0.0, None, ALU.max))
            layernorm(na, h0, nb_, 3)
            tt(na[0:BN], na[0:BN], over_nodes(G1), ALU.mult)
            v.tensor_tensor(na[0:BN], na[0:BN], over_nodes(B1), ALU.add).then_inc(h_ready, 1)
            dve.wait_ge(turned_out, BANKS)
            for q in range(PROJ_BATCHES):
                b0, b1 = q * BANKS, min(NB, (q + 1) * BANKS)
                dve.wait_ge(proj_out, 2 * (q + 1))
                v.tensor_tensor(nb_[0:BN, b0:b1, :], proj_view(b1 - b0, 1),
                                log_deg[0:BN, b0:b1].unsqueeze(2).to_broadcast([BN, b1 - b0, F]),
                                ALU.mult).then_inc(tails_out, 1)
                v.tensor_scalar(fe_a[0:BN, b0:b1, :], proj_view(b1 - b0, 2), ALPHA, None,
                                ALU.mult).then_inc(tails_out, 1)
            dve.wait_ge(proj_out, 2 * PROJ_BATCHES)
            dve.wait_ge(tails_out, 2 * PROJ_BATCHES)
            dve.sem_inc(table_ready, 3)
            with dve.Fori(0, ITERS) as r:
                for k in range(SLOTS):
                    dve.wait_ge(got[k], r * (2 * 16 * G) + 2 * 16 * G)
                    v.tensor_tensor(gb[:, k], ga[:, k], gb[:, k], ALU.mult).then_inc(step_link, 1)
                    dve.wait_ge(step_link, r * (3 * SLOTS) + (3 * k + 1))
                    v.scalar_tensor_tensor(out=ga[:, k], in0=gb[:, k], scalar=SLOPE, in1=gb[:, k], op0=ALU.mult,
                                           op1=ALU.max).then_inc(step_link, 1)
                    dve.wait_ge(step_link, r * (3 * SLOTS) + (3 * k + 2))
                    v.tensor_tensor(ga[:, k], ga[:, k], rowvec[:, ATTN:ATTN + 1, :].to_broadcast([P, G, F]),
                                    ALU.mult).then_inc(step_link, 1)
                    dve.wait_ge(step_link, r * (3 * SLOTS) + (3 * k + 3))
                    v.tensor_reduce(ex_it[:, bass.ds(r * PER_ITER + k * G, G), :].rearrange("p g h -> p (g h)"),
                                    ga[:, k].rearrange("p g (h d) -> p (g h) d", h=HEADS),
                                    AX.X, ALU.add).then_inc(scores_done, 1)
            dve.wait_ge(scores_done, SLOTS + GROUPS)
            dve.wait_ge(table_out, 3 * 16)
            dve.sem_inc(key_free, 1)
            dve.wait_ge(key_in, 16 * CHUNKS)
            link(v.memset(gap[:], 0.0))
            tt(gap[:, 1:L], key[:, 1:L], key[:, 0:L - 1], ALU.not_equal)
            link(v.tensor_scalar(gap[:], gap[:], -BIG, None, ALU.mult))
            link(v.tensor_reduce(ends[:, 1:2], gap[:, 0:L], AX.X, ALU.min))
            link(v.tensor_copy(ends[:, 2:3], key[:, 0:1]))
            link(v.tensor_copy(ends[:, 3:4], key[:, L - 1:L]))
            dve.wait_ge(score_out, -(-CI // BPB))

            def scan_carried(n, to, gaps, data, last, back):
                link(v.tensor_tensor_scan(to, gaps, data, -BIG, ALU.add, ALU.max))
                v.tensor_copy(ends[:, 0:1], last).then_inc(ends_ready, 1)
                dve.wait_ge(ends_turned, n + 1)
                link(v.tensor_copy(rows[:], small[0:1, 0:4 * P].rearrange("o (k c h) -> o k h c", k=4, h=HEADS)))
                way = slice(None, None, -1) if back else slice(None)
                row = [rows[0:1, k, :, way] for k in range(4)]
                final, gate, first, last_ = (row[0], row[1], row[3], row[2]) if back else row
                gates, new, run, cut = (carry[0:1, k, :].rearrange("o (h c) -> o h c", h=HEADS) for k in range(4))
                link(v.memset(carry[0:1, 3, :], 1.0))
                link(v.memset(carry[0:1, 0:2, :], -BIG))
                tt(cut[:, :, 1:], first[:, :, 1:], last_[:, :, :-1], ALU.not_equal)
                link(v.scalar_tensor_tensor(out=gates[:, :, 1:], in0=cut[:, :, :-1], scalar=-BIG,
                                            in1=gate[:, :, :-1], op0=ALU.mult, op1=ALU.add))
                link(v.tensor_copy(new[:, :, 1:], final[:, :, :-1]))
                link(v.tensor_tensor_scan(carry[0:1, 2, :], carry[0:1, 0, :], carry[0:1, 1, :], -BIG, ALU.add,
                                          ALU.max))
                to_col = carry[0:1, 4, :].rearrange("o (c h) -> o h c", h=HEADS)[:, :, way]
                v.scalar_tensor_tensor(out=to_col, in0=cut, scalar=-BIG, in1=run, op0=ALU.mult,
                                       op1=ALU.add).then_inc(carry_ready, 1)
                dve.wait_ge(carry_turned, n + 1)
                link(v.tensor_copy(carry_col[:, n:n + 1], bank(0, 1)))
                link(v.tensor_tensor_scan(to, gaps, data, carry_col[:, n:n + 1], ALU.add, ALU.max))

            scan_carried(0, fw, gap[:, 0:L], e_sc, fw[:, L - 1:L], False)
            scan_carried(1, bw[:, ::-1], gap[:, 1:L + 1][:, ::-1], fw[:, ::-1], bw[:, 0:1], True)
            v.tensor_tensor(e_sc, e_sc, bw, ALU.subtract).then_inc(shifted, 1)
            for n in range(-(-CI // BPB)):
                j0, j1 = n * BPB, min(CI, (n + 1) * BPB)
                dve.wait_ge(exp_turned, n + 1)
                v.tensor_copy(ex_it[:, j0 * CHUNKS:j1 * CHUNKS, :].rearrange("p i h -> p (i h)"),
                              bank(n % BANKS, (j1 - j0) * P)).then_inc(exp_out, 1)
            dve.wait_ge(exp_out, -(-CI // BPB))
            for n in range(HOPS):
                message_pass(HOP0 + n)
                if n == 0:
                    link(v.tensor_scalar(inv_sum[0:BN], ps[0:BN, 7 * BANK:7 * BANK + NB * HEADS].rearrange(
                        "p (b h) -> p b h", h=HEADS), 1e-30, None, ALU.max))
                    link(v.reciprocal(inv_sum[0:BN], inv_sum[0:BN]))
                    link(v.tensor_scalar(inv_sum[0:BN], inv_sum[0:BN], 1.0 - ALPHA, None, ALU.mult))
                for k in range(BANKS):
                    b0, b1 = bank_buckets(k)
                    ins = v.tensor_tensor(
                        na[0:BN, b0:b1, :].rearrange("p b (h d) -> p (b h) d", h=HEADS),
                        bank(k, (b1 - b0) * F)[0:BN].rearrange("p (q d) -> p q d", d=HD),
                        inv_sum[0:BN, b0:b1, :].rearrange("p b h -> p (b h)").unsqueeze(2).to_broadcast(
                            [BN, (b1 - b0) * HEADS, HD]), ALU.mult)
                    link(ins)
                if n < HOPS - 1:
                    dve.sem_inc(sums_out, 1)
                    v.tensor_tensor(na[0:BN], na[0:BN], fe_a[0:BN], ALU.add).then_inc(table_ready, 1)
                else:
                    tt(na[0:BN], na[0:BN], fe_a[0:BN], ALU.add)
            tt(na[0:BN], na[0:BN], h0[0:BN], ALU.add)
            dve.wait_ge(x_again, 16)
            tt(h0[0:BN], na[0:BN], x_sb[0:BN], ALU.add)
            tt(h0[0:BN], h0[0:BN], over_nodes(BFF2), ALU.add)
            layernorm(nb_, na, x_sb, 4)
            tt(nb_[0:BN], nb_[0:BN], over_nodes(G2), ALU.mult)
            v.tensor_tensor(nb_[0:BN], nb_[0:BN], over_nodes(B2), ALU.add).then_inc(h_ready, 1)
            for q in range(BANKS):
                b0, b1 = bank_buckets(q)
                dve.wait_ge(ff2_done, q + 1)
                v.tensor_tensor(h0[0:BN, b0:b1, :], h0[0:BN, b0:b1, :],
                                bank(4 + q % 2, (b1 - b0) * F)[0:BN].rearrange("p (b f) -> p b f", f=F),
                                ALU.add).then_inc(ff2_out, 1)
            dve.wait_ge(ff2_out, BANKS)
            layernorm(na, h0, nb_, 5)
            v.tensor_scalar(na[0:BN], na[0:BN], 0.0, None, ALU.max).then_inc(h_ready, 1)
            for n in range(LAYERS):
                for k in range(BANKS):
                    b0, b1 = bank_buckets(k)
                    dve.wait_ge(gcn_done, n * BANKS + k + 1)
                    link(v.tensor_tensor(nb_[0:BN, b0:b1, :],
                                         bank(k, (b1 - b0) * F)[0:BN].rearrange("p (b f) -> p b f", f=F),
                                         dinv[0:BN, b0:b1].unsqueeze(2).to_broadcast([BN, b1 - b0, F]), ALU.mult))
                dve.sem_inc(table_ready, 1)
                message_pass(CONV0 + n)
                for k in range(BANKS):
                    b0, b1 = bank_buckets(k)
                    link(v.tensor_tensor(na[0:BN, b0:b1, :],
                                         bank(k, (b1 - b0) * F)[0:BN].rearrange("p (b f) -> p b f", f=F),
                                         nb_[0:BN, b0:b1, :], ALU.add))
                tt(na[0:BN], na[0:BN], over_f(dinv[0:BN]), ALU.mult)
                tt(na[0:BN], na[0:BN], over_nodes(BG0 + n), ALU.add)
                if n < LAYERS - 1:
                    v.tensor_scalar(na[0:BN], na[0:BN], 0.0, None, ALU.max).then_inc(h_ready, 1)
                else:
                    v.tensor_tensor(na[0:BN], na[0:BN], h0[0:BN], ALU.add).then_inc(y_ready, 1)


_EDGE = {"src": 0, "dst": N_NODES + BN, "edge_weight": 0}


def kernel(**inputs):
    import numpy as np
    import concourse.bacc as bacc
    from concourse.bass_utils import run_bass_kernel_spmd

    nc = bacc.Bacc("TRN2", target_bir_lowering=False, num_devices=1)
    arrays, args = {}, {}
    for name, value in inputs.items():
        x = np.ascontiguousarray(value)
        if name in _EDGE:
            x = np.pad(x, (0, TILES * P - N_EDGES), constant_values=_EDGE[name])
        arrays["in_" + name] = x
        args[name] = nc.dram_tensor("in_" + name, x.shape, mybir.dt.from_np(x.dtype), kind="ExternalInput").ap()
    out = nc.dram_tensor("out_0", (N_NODES, F), F32, kind="ExternalOutput").ap()
    gnn_stack(nc, args, out)
    r = run_bass_kernel_spmd(nc, [arrays], core_ids=[0])
    return r.results[0]["out_0"]
```

```python
from contextlib import ExitStack

import concourse.bass as bass
from concourse import mybir

F32 = mybir.dt.float32
BF16 = mybir.dt.bfloat16
I32 = mybir.dt.int32
ALU = mybir.AluOpType
ACT = mybir.ActivationFunctionType
AX = mybir.AxisListType

P = 128
N_NODES = 3125
N_EDGES = 100000
F = 128
BN = 125
NB = N_NODES // BN
HEADS, HD = 8, 16
D_FF = 4 * F
FFC = D_FF // P
HOPS, ALPHA, SLOPE, EPS = 5, 0.15, 0.2, 1e-5
LAYERS = 3
TILES = -(-N_EDGES // P)
CHUNKS = 16
ITEM_COUNT = N_EDGES // P + NB
G = 4
SLOTS = 4
PER_ITER = G * SLOTS
ITEMS = -(-ITEM_COUNT // PER_ITER) * PER_ITER
ITERS = ITEMS // PER_ITER
GROUPS = ITERS * SLOTS
CI = ITEMS // CHUNKS
L = CI * P
KB = -(-ITEMS // P)
BANK = 512
BPB = BANK // F
BANKS = -(-NB // BPB)
BIG = 1e30
AHEAD = SLOTS - 1
TABLES = HOPS - 1
WN = 5
WINDOWS = N_NODES // WN
WPB = BN // WN
WIN_ITEM_COUNT = N_EDGES // P + WINDOWS
BG = 2
BUILD_HOPS = HOPS - 1
KW = -(-WIN_ITEM_COUNT // P)
WIN_ITEMS = KW * P
BUILD_ITERS = WIN_ITEMS // (BUILD_HOPS * SLOTS * BG)
CELL = NB * WN
ROW = P
WIN_SPARE = SLOTS * BG
RING = 5
assert WINDOWS * WN == N_NODES and WPB * WN == BN and BUILD_ITERS * BUILD_HOPS * SLOTS * BG == WIN_ITEMS
NEXT_BANK = (5, 6, 5, 6, 7)
assert NB % RING == 0 and len(NEXT_BANK) == RING
ROUND = 1.5 * 2.0 ** 23
PROJ_BATCHES = -(-NB // BANKS)
EXP_PARTS = 3
RADIX_BITS = 6
RADIX = 1 << RADIX_BITS
SORT_PASSES = 2
assert N_NODES + BN < RADIX ** SORT_PASSES
EX_SUMS = 7 * BANK
W_SUMS = EX_SUMS
MASKS = 8
assert PER_ITER == CHUNKS and ITEMS % CHUNKS == 0 and CHUNKS * HEADS == P and NB * BN == N_NODES
assert (NB + 1) * F <= BANKS * BANK and BANKS < 8


def bank_buckets(k):
    return k * BPB, min(NB, (k + 1) * BPB)


def gnn_stack(nc, a, out):
    ctx = ExitStack()
    with ctx:
        def sb(name, shape, dt=F32):
            return ctx.enter_context(nc.sbuf_tensor(name, shape, dt))

        def sem(name):
            return ctx.enter_context(nc.semaphore(name))

        def dram(name, shape, dt=F32):
            return nc.dram_tensor(name, shape, dt, kind="Internal").ap()

        tab_he = dram("tab_he", (N_NODES, 2 * F))
        edge_fe = dram("edge_fe", (P, ITEMS, F))
        tab_f = dram("tab_f", (N_NODES, F))
        srt = {n: dram("sorted_" + n, (TILES, P), d)
               for n, d in (("src", I32), ("dst", I32), ("edge_weight", F32))}
        packed = [dram(f"packed{k}", (TILES * P, 4)) for k in range(SORT_PASSES)]
        item_bucket_d = dram("item_bucket_d", (KB * P,), I32)
        item_dst_d = dram("item_dst_d", (KB * P, P), I32)
        adj = dram("adj", (P, WINDOWS + WIN_SPARE, ROW))
        win_d = dram("win_d", (WIN_ITEMS,))
        cols_d = dram("cols_d", (P, 3 * WIN_ITEMS))
        dinv_d = dram("dinv_d", (N_NODES,))

        ps = ctx.enter_context(nc.psum_tensor("ps", [P, 8 * BANK], F32))

        def bank(k, n=BANK):
            return ps[:, k * BANK:k * BANK + n]

        small = bank(7)

        h0 = sb("h0", [P, NB, F])
        fe_a = sb("fe_a", [P, NB, F])
        src_it = sb("src_it", [P, KB * P], I32)
        dloc = sb("dloc", [P, KB * P])
        w_it = sb("w_it", [P, KB * P])
        ex_it = sb("ex_it", [P, ITEMS, HEADS])
        bucket_row = sb("bucket_row", [1, KB * P], I32)
        stage = sb("stage", [P, SLOTS, G], I32)
        slide = sb("slide", [P, 2 * P - 1], BF16)
        ident = sb("ident", [P, P])
        iota_p = sb("iota_p", [P, P])
        iota_bn = iota_p[:, 0:BN]
        ones = sb("ones", [P, P])
        zeros = sb("zeros", [1, BANK])
        raw = sb("raw", [P, WIN_ITEMS])
        w_raw = raw[:, 0:3 * F].rearrange("p (k f) -> p k f", f=F)
        w_qkv = sb("w_qkv", [P, 3 * F])
        ff1_raw = raw[:, 3 * F:3 * F + D_FF].rearrange("p (c f) -> p c f", f=F)
        ff1_t = sb("ff1_t", [P, D_FF])
        ff2_raw = raw[:, 3 * F + D_FF:3 * F + 2 * D_FF]
        ff2_t = sb("ff2_t", [P, FFC, F])
        w_gcn = sb("w_gcn", [P, LAYERS, F])
        b_ff1 = sb("b_ff1", [P, FFC])
        rowvec = sb("rowvec", [P, 6, F])
        G1, B1, G2, B2, BFF2, ATTN = range(6)
        b_gcn = sb("b_gcn", [P, LAYERS])
        step5 = sb("step5", [P, WPB])
        deg_n = sb("deg_n", [P, NB])
        win_it = sb("win_it", [P, KW])
        win_f = sb("win_f", [P, 2, KW])
        win_t = sb("win_t", [P, KW], I32)
        target = sb("target", [1, WIN_ITEMS], I32)
        w_deg = sb("w_deg", [P, NB])
        log_deg = sb("log_deg", [P, NB])
        dinv = sb("dinv", [P, NB])
        inv_sum = sb("inv_sum", [P, NB, HEADS])
        stat = sb("stat", [P, 4, NB])
        thr = sb("thr", [P, 3, NB + 1])
        disorder = sb("disorder", [P, 1], I32)
        thr_i = sb("thr_i", [P, NB + 1], I32)
        item_f = sb("item_f", [P, 4, KB])
        item_t = sb("item_t", [P, KB], I32)
        item_b = sb("item_b", [P, KB], I32)
        ge = sb("ge", [P, KB, NB])
        ge_rev = sb("ge_rev", [P, KB, NB])
        anti = sb("anti", [P, P])
        ends = sb("ends", [P, 4])
        rows = sb("rows", [1, 4, HEADS, CHUNKS])
        carry = sb("carry", [1, 5, HEADS * CHUNKS])
        carry_col = sb("carry_col", [P, 2])

        U = sb("U", [P, 3 * L])
        gap = sb("gap", [P, L + 2], BF16)
        e_sc, fw, bw = (U[:, k * L:(k + 1) * L] for k in range(3))
        key = bw.bitcast(I32)
        at = [0]

        def part(n):
            at[0] += n
            assert at[0] <= 3 * L
            return U[:, at[0] - n:at[0]]

        node = [part(n * F).rearrange("p (b f) -> p b f", f=F) for n in (NB, NB, NB + 1)]
        x_sb, na, nb_pad = node
        nb_ = nb_pad[:, 0:NB]
        turned_flat = part(NB * BN)
        hT = turned_flat
        hot_t = turned_flat[0:BN, 0:2 * G * P].rearrange("p (s g e) -> p s g e", s=2, g=G)
        ga_flat = part(SLOTS * G * 2 * F)
        ga_wide = ga_flat.rearrange("p (s g f) -> p s g f", s=SLOTS, g=G)
        ga = ga_flat.rearrange("p (s n) -> p s n", s=SLOTS)[:, :, 0:G * F].rearrange("p s (g f) -> p s g f", g=G)
        ffa = ga_flat[:, 0:FFC * BPB * BN].rearrange("p (c n) -> p c n", c=FFC)
        hot_flat = part(SLOTS * G * BN)
        hot = hot_flat.rearrange("p (s g f) -> p s g f", s=SLOTS, g=G)
        hot_b = hot_flat[:, 0:SLOTS * G * BN // 2].bitcast(BF16).rearrange("p (s g f) -> p s g f", s=SLOTS, g=G)
        item_deg = ex_it[:].rearrange("p i h -> p (i h)")[:, 0:KB * BN].rearrange("p (k n) -> p k n", k=KB)
        dst_all = ga_flat[:, 0:TILES].bitcast(I32)
        dst_next = hT[:, TILES:2 * TILES].bitcast(I32)
        dst_allf = hT[:, 0:TILES]
        dst_allw = hT[:, 2 * TILES:3 * TILES]
        row_raw = [node[k].rearrange("p b f -> p (b f)")[:, 0:KB * P].rearrange("p (k e) -> p k e", e=P)
                   for k in range(3)]
        row_i = [row_raw[0].bitcast(I32), row_raw[1].bitcast(I32), row_raw[2]]
        row_f = [node[k].rearrange("p b f -> p (b f)")[:, KB * P:2 * KB * P].rearrange("p (k e) -> p k e", e=P)
                 for k in range(3)]

        sort_at = [0]

        def sort_part(*shape):
            n = shape[0] if len(shape) == 1 else shape[0] * shape[1]
            sort_at[0] += n
            assert sort_at[0] <= 2 * NB * F
            v = U[:, sort_at[0] - n:sort_at[0]]
            return v if len(shape) == 1 else v.rearrange("p (t c) -> p t c", c=shape[1])

        edges = sort_part(TILES, 4)
        s_raw = sort_part(TILES)
        s_digit = sort_part(TILES)
        s_hot = sort_part(RADIX)
        s_tmp = sort_part(RADIX)
        s_base = sort_part(RADIX)
        s_count = sort_part(RADIX)
        s_iota = sort_part(RADIX)
        s_rank = sort_part(4)
        s_move = sort_part(4)
        s_lower = sort_part(P)

        win_rows = [U[:, k * WIN_ITEMS:(k + 1) * WIN_ITEMS] for k in range(3)] + [raw[:]]
        win_tmp = [U[:, 3 * WIN_ITEMS + k * WINDOWS:3 * WIN_ITEMS + (k + 1) * WINDOWS] for k in range(3)]
        assert 3 * WIN_ITEMS + 3 * WINDOWS <= 2 * NB * F and 3 * F + 2 * D_FF <= WIN_ITEMS
        cols_at = 2 * NB * F
        assert 4 * WIN_ITEMS <= (NB + 1) * F + NB * BN
        win_p, win_b, win_dd, win_same = (U[:, cols_at + k * WIN_ITEMS:cols_at + (k + 1) * WIN_ITEMS] for k in range(4))
        win_w = raw
        wrow = na.rearrange("p b f -> p (b f)")[:, 0:WIN_ITEMS]
        wtmp = na.rearrange("p b f -> p (b f)")[0:1, WIN_ITEMS:2 * WIN_ITEMS]
        gap_f = gap[:].bitcast(F32)
        gap_at = [0]

        def gap_part(s_, j, n):
            gap_at[0] += s_ * j * n
            return gap_f[:, gap_at[0] - s_ * j * n:gap_at[0]].rearrange("p (s j n) -> p s j n", s=s_, j=j)

        hot_p = gap_part(2, BG, P)
        prod = gap_part(2, BG, CELL)
        win_acc = gap_part(SLOTS, BG, ROW)
        hot_bk = gap_part(2, BG, NB)
        hot_d = gap_part(2, BG, WN)
        spare0 = gap_part(1, 1, WIN_SPARE)[0:1, 0, 0, :]
        dinv_row = gap_f[:, 0:N_NODES]
        wide = WPB * ROW
        ex_flat = ex_it[:].rearrange("p i h -> p (i h)")
        ring = [ex_flat[:, 0:wide], ex_flat[:, wide:2 * wide], fe_a[:].rearrange("p b f -> p (b f)")[:, 0:wide],
                x_sb.rearrange("p b f -> p (b f)")[:, 0:wide], ga_flat[:, 0:wide]]

        def cells_of(u):
            return ring[u][0:BN].rearrange("p (w n) -> p w n", n=ROW)[:, :, 0:CELL].rearrange(
                "p w (b d) -> p w b d", b=NB)

        turned_q = hot_flat[:, 0:RING * BN].rearrange("p (u n) -> p u n", n=BN)

        win_counted = sem("win_counted")
        win_summed = sem("win_summed")
        win_known = sem("win_known")
        win_rows_in = sem("win_rows_in")
        win_rows_ready = sem("win_rows_ready")
        win_turned = sem("win_turned")
        win_cols = sem("win_cols")
        win_out = sem("win_out")
        wrow_in = sem("wrow_in")
        cols_in = sem("cols_in")
        targets_ready = sem("targets_ready")
        pool_link = sem("pool_link")
        w_summed = sem("w_summed")
        prod_ready = sem("prod_ready")
        cell_sums = sem("cell_sums")
        acc_ready = sem("acc_ready")
        acc_out = [sem(f"acc_out{k}") for k in range(SLOTS)]
        build_link = sem("build_link")
        hops_done = sem("hops_done")
        sum_link = sem("sum_link")
        dinv_ready = sem("dinv_ready")
        dinv_out = sem("dinv_out")
        dinv_in = sem("dinv_in")
        adj_in = [sem(f"adj_in{u}") for u in range(RING)]
        loops_in = sem("loops_in")
        conv_done = sem("conv_done")
        conv_scaled = sem("conv_scaled")
        conv_out = sem("conv_out")
        next_done = sem("next_done")
        next_out = sem("next_out")
        consts_in = sem("consts_in")
        dst_in = sem("dst_in")
        x_in = sem("x_in")
        masks_set = sem("masks_set")
        dve_link = sem("dve_link")
        counted = sem("counted")
        summed = sem("summed")
        tiles_known = sem("tiles_known")
        rows_in = sem("rows_in")
        rows_ready = sem("rows_ready")
        rows_turned = sem("rows_turned")
        items_ready = sem("items_ready")
        bucket_out = sem("bucket_out")
        bucket_in = sem("bucket_in")
        key_out = sem("key_out")
        key_in = sem("key_in")
        key_free = sem("key_free")
        weights_turned = sem("weights_turned")
        weights_ready = sem("weights_ready")
        staged = sem("staged")
        hots_ready = sem("hots_ready")
        hots_used = sem("hots_used")
        item_degs = sem("item_degs")
        item_degs_out = sem("item_degs_out")
        degs_ready = sem("degs_ready")
        hot_turned = sem("hot_turned")
        hot_t_out = sem("hot_t_out")
        tails_ready = sem("tails_ready")
        scaled = sem("scaled")
        stored = [sem(f"stored{k}") for k in range(SLOTS)]
        loaded = [sem(f"loaded{k}") for k in range(SLOTS)]
        edges_copied = sem("edges_copied")
        edges_sorted = sem("edges_sorted")
        order_known = sem("order_known")
        sort_masks = sem("sort_masks")
        sort_in = sem("sort_in")
        sort_counted = sem("sort_counted")
        sort_summed = sem("sort_summed")
        sort_hot = sem("sort_hot")
        sort_prefix = sem("sort_prefix")
        sort_link = sem("sort_link")
        sort_ranked = sem("sort_ranked")
        sort_begun = sem("sort_begun")
        sort_moved = sem("sort_moved")
        sort_split = sem("sort_split")
        begun = sem("begun")
        got = [sem(f"got{k}") for k in range(SLOTS)]
        zeros_set = sem("zeros_set")
        slide_set = sem("slide_set")
        reversed_ = sem("reversed_")
        scores_done = sem("scores_done")
        tails_out = sem("tails_out")
        sums_out = sem("sums_out")
        gcn_done = sem("gcn_done")
        msgs_ready = sem("msgs_ready")
        groups_done = sem("groups_done")
        step_link = sem("step_link")
        var_ready = sem("var_ready")
        std_ready = sem("std_ready")
        logs_ready = sem("logs_ready")
        h_ready = sem("h_ready")
        turned = sem("turned")
        turned_out = sem("turned_out")
        proj_done = sem("proj_done")
        proj_out = sem("proj_out")
        table_ready = sem("table_ready")
        table_out = sem("table_out")
        score_turned = sem("score_turned")
        score_out = sem("score_out")
        ends_ready = sem("ends_ready")
        ends_turned = sem("ends_turned")
        carry_ready = sem("carry_ready")
        carry_turned = sem("carry_turned")
        shifted = sem("shifted")
        exps_ready = sem("exps_ready")
        exp_turned = sem("exp_turned")
        exp_out = sem("exp_out")
        ff1_done = sem("ff1_done")
        ff1_out = sem("ff1_out")
        ff2_done = sem("ff2_done")
        ff2_out = sem("ff2_out")
        x_again = sem("x_again")
        y_out = sem("y_out")

        def staged_before(s):
            return GROUPS + AHEAD + (s - 1) * GROUPS

        def got_before(s):
            return 16 * G * ITERS * s

        def msgs_before(s):
            return GROUPS + 1 + 2 * s * GROUPS

        def item_of(r, k, ahead=0):
            return r * PER_ITER + (k + ahead) * G

        def win_item(s, r, k, j=0):
            return r * (SLOTS * BG) + ((s - 1) * BUILD_ITERS * SLOTS * BG + k * BG + j)

        def steps_before(s):
            return (s - 1) * BUILD_ITERS * SLOTS

        WIN_COUNT_AT, WIN_GATHER_AT, WIN_ROWS_AT, WIN_TURN_AT = 8, 14, 22, 26

        WHY_BOUNDED = "a count of the NB bounds at or below the item"

        def buckets_of(pe, i):
            _, b = nc.values_load_multi_w_load_instructions(bucket_row[0:1, bass.ds(i, G)], engines=(pe.engine,),
                                                            min_val=0, max_val=NB,
                                                            skip_runtime_bounds_check_because=WHY_BOUNDED)
            return b

        def proj_view(n, col):
            return ps[0:BN, 0:n * BANK].rearrange("p (k n) -> p k n", n=BANK)[:, :, col * F:(col + 1) * F]

        def nodes_of(table):
            return table.rearrange("(b p) f -> p b f", p=BN)

        LOADS = 3 + 3 + LAYERS + 6 + LAYERS

        block = ctx.enter_context(nc.Block())

        @block.sync
        def _(sp):
            in_rows = {n: a[n][0:TILES * P].rearrange("(p t) -> p t", p=P) for n in srt}
            sp.dma_start(dst_all, in_rows["dst"]).then_inc(dst_in, 16)
            sp.dma_start(dst_next, a["dst"][1:TILES * P + 1].rearrange("(p t) -> p t", p=P)).then_inc(dst_in, 16)
            for n in srt:
                sp.dma_start(srt[n].rearrange("(a t) e -> a (t e)", a=2),
                             a[n][0:TILES * P].rearrange("(a n) -> a n", a=2)).then_inc(edges_copied, 16)
            sp.dma_start(h0[0:BN], nodes_of(a["x"])).then_inc(x_in, 16)
            loads = [(w_raw[:, k, :], a[n]) for k, n in enumerate(("L0_gnn_W_head", "L0_gnn_W_tail", "L0_gnn_W_ent"))]
            loads += [(ff1_raw[:], a["L0_gnn_W_ff1"].rearrange("(c p) f -> p c f", p=P)),
                      (ff2_raw[:], a["L0_gnn_W_ff2"]),
                      (b_ff1[:], a["L0_gnn_b_ff1"].rearrange("(c p) -> p c", p=P))]
            loads += [(w_gcn[:, k, :], a[f"L1_gnn_W{k}"]) for k in range(LAYERS)]
            for k, n in ((G1, "L0_gnn_ln1_g"), (B1, "L0_gnn_ln1_b"), (G2, "L0_gnn_ln2_g"), (B2, "L0_gnn_ln2_b"),
                         (BFF2, "L0_gnn_b_ff2")):
                loads.append((rowvec[:, k, :], a[n].partition_broadcast(P)))
            loads.append((rowvec[:, ATTN, :], a["L0_gnn_attn"].rearrange("a h d -> (a h d)").partition_broadcast(P)))
            loads += [(b_gcn[:, k:k + 1], a[f"L1_gnn_b{k}"].rearrange("(p o) -> p o", o=1)) for k in range(LAYERS)]
            assert len(loads) == LOADS
            for to, of in loads:
                sp.dma_start(to, of, allow_slow_non_contiguous=True).then_inc(consts_in, 16)
            sp.wait_ge(order_known, 1)
            sp.wait_ge(edges_copied, 16 * 3)
            with sp.If(sp.value_load(disorder[0:1, 0:1], min_val=0, max_val=TILES * P) != 0):
                sp.dma_start(s_raw.bitcast(I32), in_rows["src"]).then_inc(sort_in, 16)
                sp.dma_start(s_digit, in_rows["edge_weight"]).then_inc(sort_in, 16)
                for n in range(SORT_PASSES):
                    sp.wait_ge(sort_moved, 16 * TILES * (n + 1))
                    sp.dma_start(edges, packed[n].rearrange("(p t) c -> p t c", p=P)).then_inc(sort_in, 16)
                sp.wait_ge(sort_split, 1)
                for n, v in (("src", s_raw.bitcast(I32)), ("dst", s_digit.bitcast(I32)), ("edge_weight", dst_allw)):
                    sp.dma_start(srt[n].rearrange("t e -> (t e)").rearrange("(p t) -> p t", p=P),
                                 v).then_inc(edges_copied, 16)
                sp.wait_ge(edges_copied, 16 * 6)
            sp.sem_inc(edges_sorted, 1)
            sp.wait_ge(tiles_known, 1)
            sp.dma_start(item_bucket_d.rearrange("(k p) -> p k", p=P), item_b[:],
                         allow_slow_non_contiguous=True).then_inc(bucket_out, 16)
            sp.wait_ge(bucket_out, 16)
            sp.dma_start(bucket_row[:], item_bucket_d.rearrange("(a n) -> a n", a=1)).then_inc(bucket_in, 16)
            sp.wait_ge(rows_in, 3 * KB * 16)
            sp.dma_start(item_dst_d.rearrange("(k p) e -> p k e", p=P), row_i[1]).then_inc(key_out, 16)
            sp.sem_inc(stored[SLOTS - 1], 16)
            sp.wait_ge(table_ready, 1)
            sp.dma_start(nodes_of(tab_he[:, 0:F]), na[0:BN]).then_inc(table_out, 16)
            sp.dma_start(nodes_of(tab_he[:, F:2 * F]), x_sb[0:BN]).then_inc(table_out, 16)
            with sp.Fori(0, ITERS) as r:
                for k in range(SLOTS):
                    sp.wait_ge(got[k], r * (16 * G) + 16 * G)
                    sp.dma_start(edge_fe[:, bass.ds(item_of(r, k), G), :], ga_wide[:, k, :, F:2 * F]).then_inc(stored[k], 16)
            sp.wait_ge(win_known, 1)
            sp.dma_start(win_d.rearrange("(k p) -> p k", p=P), win_f[:, 0, :],
                         allow_slow_non_contiguous=True).then_inc(win_out, 16)
            sp.wait_ge(win_cols, 4)
            sp.dma_start(cols_d, U[:, 0:3 * WIN_ITEMS]).then_inc(win_out, 16)
            sp.wait_ge(key_out, 16)
            sp.wait_ge(key_free, 1)
            chunks = item_dst_d.rearrange("(r c) e -> c r e", c=CHUNKS)[:, 0:CI, :]
            for c in range(CHUNKS):
                sp.dma_start(key[c * HEADS:(c + 1) * HEADS, :].rearrange("p (r e) -> p r e", e=P),
                             chunks[c].partition_broadcast(HEADS)).then_inc(key_in, 16)
            sp.wait_ge(exp_out, -(-CI // BPB))
            sp.dma_start(x_sb[0:BN], nodes_of(a["x"])).then_inc(x_again, 16)
            sp.wait_ge(win_out, 32)
            sp.dma_start(wrow, win_d.partition_broadcast(P)).then_inc(wrow_in, 16)
            sp.dma_start(U[:, cols_at:cols_at + 3 * WIN_ITEMS], cols_d).then_inc(cols_in, 16)
            for k in range(SLOTS):
                sp.wait_ge(stored[k], 16 * (ITERS + (k == SLOTS - 1)))
            with sp.Fori(0, ITERS) as r:
                for k in range(SLOTS):
                    sp.wait_ge(groups_done, r * SLOTS + (k + 1))
                    sp.dma_start(ga[:, k], edge_fe[:, bass.ds(item_of(r, k), G), :]).then_inc(loaded[k], 16)
            for k in range(SLOTS):
                sp.sem_inc(acc_out[k], 16 * BG)
            sp.wait_ge(targets_ready, 1)
            for n in range(HOPS):
                if n:
                    with sp.Fori(0, BUILD_ITERS) as r:
                        for k in range(SLOTS):
                            sp.wait_ge(acc_ready, r * SLOTS + (steps_before(n) + k + 2))
                            for j in range(BG):
                                to = sp.value_load(target[0:1, bass.ds(win_item(n, r, k, j), 1)], min_val=0,
                                                   max_val=WINDOWS + WIN_SPARE - 1)
                                sp.dma_start(adj[:, bass.ds(to, 1), :].rearrange("p w c -> p (w c)"),
                                             win_acc[:, k, j, :]).then_inc(acc_out[k], 16)
                if n < HOPS - 1:
                    for k in range(BANKS):
                        b0, b1 = bank_buckets(k)
                        sp.wait_ge(table_ready, 1 + n * BANKS + k + 1)
                        sp.dma_start(nodes_of(tab_f)[:, b0:b1], na[0:BN, b0:b1]).then_inc(table_out, 16)
            for k in range(SLOTS):
                sp.wait_ge(acc_out[k], 16 * BG * (BUILD_HOPS * BUILD_ITERS + 1))
            sp.wait_ge(dinv_ready, 1)
            sp.dma_start(dinv_d.rearrange("(b p) -> p b", p=BN), dinv[0:BN],
                         allow_slow_non_contiguous=True).then_inc(dinv_out, 16)
            buckets_d = adj[:, 0:WINDOWS, :].rearrange("p (q w) c -> p q (w c)", q=NB)

            def load_bucket(u, q):
                sp.dma_start(ring[u], buckets_d[:, bass.ds(q, 1), :].rearrange("p q c -> p (q c)")
                             ).then_inc(adj_in[u], 16)

            sp.wait_ge(hops_done, 1)
            for u in range(RING):
                if u == 3:
                    sp.wait_ge(dinv_out, 16)
                    sp.dma_start(dinv_row, dinv_d.partition_broadcast(P)).then_inc(dinv_in, 16)
                    sp.wait_ge(h_ready, 2)
                if u == 4:
                    sp.wait_ge(ff2_done, BANKS)
                load_bucket(u, u)
            for n in range(LAYERS):
                last = n == LAYERS - 1
                if not last:
                    passes = [(0, NB // RING - 1, RING), (NB // RING - 1, NB // RING, RING - NB)]
                else:
                    passes = [(0, NB // RING - 1, RING)]
                for r0, r1, ahead in passes:
                    with sp.Fori(r0, r1) as r:
                        for u in range(RING):
                            sp.wait_ge(conv_done, r * RING + (n * NB + u + 1))
                            load_bucket(u, r * RING + (u + ahead))
            for k in range(BANKS):
                b0, b1 = bank_buckets(k)
                sp.wait_ge(next_out, (LAYERS - 1) * NB + b1)
                sp.dma_start(nodes_of(out)[:, b0:b1], na[0:BN, b0:b1]).then_inc(y_out, 16)
            sp.wait_ge(y_out, 16 * BANKS)
            sp.wait_ge(table_out, 16 * (2 + TABLES * BANKS))

        @block.gpsimd
        def _(pool):
            pool.memset(ident[:], 0.0).then_inc(masks_set, 1)
            pool.wait_ge(masks_set, 1)
            pool.affine_select(out=ident[:], in_=ident[:], compare_op=ALU.not_equal, fill=1.0, base=0,
                               pattern=[[-1, P]], channel_multiplier=1).then_inc(masks_set, 1)
            pool.iota(iota_p[:], pattern=[[1, P]], base=0, channel_multiplier=0,
                      allow_small_or_imprecise_dtypes=True).then_inc(masks_set, 1)
            pool.iota(item_t[:], pattern=[[P, KB]], base=0, channel_multiplier=1).then_inc(masks_set, 1)
            pool.iota(thr[:, 0, :], pattern=[[1, NB + 1]], base=1, channel_multiplier=0,
                      allow_small_or_imprecise_dtypes=True).then_inc(masks_set, 1)
            pool.iota(step5[:], pattern=[[WN, WPB]], base=WN - 1, channel_multiplier=-1,
                      allow_small_or_imprecise_dtypes=True).then_inc(masks_set, 1)
            pool.iota(win_it[:], pattern=[[P, KW]], base=0, channel_multiplier=1,
                      allow_small_or_imprecise_dtypes=True).then_inc(masks_set, 1)
            pool.memset(slide[:], 0.0).then_inc(masks_set, 1)
            pool.wait_ge(masks_set, MASKS)
            pool.memset(slide[:, P - 1:P], 1.0).then_inc(slide_set, 1)
            pool.wait_ge(order_known, 1)
            with pool.If(pool.value_load(disorder[0:1, 0:1], min_val=0, max_val=TILES * P) != 0):
                pool.iota(s_iota, pattern=[[1, RADIX]], base=0, channel_multiplier=0,
                          allow_small_or_imprecise_dtypes=True).then_inc(sort_masks, 1)
                pool.memset(s_lower, 1.0).then_inc(sort_masks, 1)
                pool.wait_ge(sort_masks, 2)
                pool.affine_select(out=s_lower, in_=s_lower, compare_op=ALU.is_gt, fill=0.0, base=0,
                                   pattern=[[1, P]], channel_multiplier=-1).then_inc(sort_masks, 1)
                for n in range(SORT_PASSES):
                    with pool.Fori(0, TILES) as r:
                        pool.wait_ge(sort_ranked, r + (n * TILES + 1))
                        pool.sem_inc(sort_begun, 1)
                        pool.indirect_dma_start(packed[n], bass.IndirectOffsetOnAxis(
                            ap=s_rank[:, 3:4].bitcast(I32), axis=0), s_move, None).then_inc(sort_moved, 16)
                pool.wait_ge(sort_moved, 16 * TILES * SORT_PASSES)
            pool.wait_ge(edges_sorted, 1)
            pool.wait_ge(tiles_known, 1)
            for k in range(KB):
                for name, to in zip(("src", "dst", "edge_weight"), row_i):
                    pool.indirect_dma_start(to[:, k, :], None, srt[name],
                                            bass.IndirectOffsetOnAxis(ap=item_t[:, k:k + 1], axis=0)).then_inc(rows_in, 16)

            def gather_pass(before, table, to, r0=0, r1=ITERS):
                with pool.Fori(r0, r1) as r:
                    for k in range(SLOTS):
                        pool.wait_ge(staged, r * SLOTS + (before + k + 1))
                        pool.sem_inc(begun, 1)
                        for j in range(G):
                            pool.indirect_dma_start(
                                to[:, k, j, :], None, table,
                                bass.IndirectOffsetOnAxis(ap=stage[:, k, j:j + 1], axis=0)).then_inc(got[k], 16)

            pool.wait_ge(table_out, 2 * 16)
            gather_pass(0, tab_he, ga_wide, 0, WIN_GATHER_AT)
            pool.wait_ge(win_known, 1)
            for k in range(KW):
                for name, to in zip(("src", "dst", "edge_weight"), (win_rows[0], win_rows[2], win_rows[3])):
                    to = to[:, k * P:(k + 1) * P]
                    pool.indirect_dma_start(to if name == "edge_weight" else to.bitcast(I32), None, srt[name],
                                            bass.IndirectOffsetOnAxis(ap=win_t[:, k:k + 1], axis=0)
                                            ).then_inc(win_rows_in, 16)
            gather_pass(0, tab_he, ga_wide, WIN_GATHER_AT, ITERS)
            links = [0]

            def chain(ins):
                links[0] += 1
                ins.then_inc(pool_link, 1)
                pool.wait_ge(pool_link, links[0])

            g = nc.gpsimd
            pool.wait_ge(wrow_in, 16)
            pool.wait_ge(exp_out, -(-CI // BPB))
            chain(g.memset(win_acc, 0.0))
            chain(g.memset(win_same[:, 0:1], 0.0))
            chain(g.tensor_tensor(win_same[:, 1:], wrow[:, :-1], wrow[:, 1:], ALU.subtract))
            chain(g.tensor_tensor(win_same[:, 1:], win_same[:, 1:],
                                  ones[:, 0:1].to_broadcast([P, WIN_ITEMS - 1]), ALU.add))
            chain(g.iota(spare0, pattern=[[1, WIN_SPARE]], base=WINDOWS, channel_multiplier=0,
                         allow_small_or_imprecise_dtypes=True))
            spares = spare0.unsqueeze(1).to_broadcast([1, WIN_ITEMS // WIN_SPARE, WIN_SPARE])
            of_steps = [x_.rearrange("o (i s) -> o i s", s=WIN_SPARE) for x_ in (wrow[0:1], wtmp, target[:])]
            chain(g.tensor_tensor(of_steps[1], of_steps[0], spares, ALU.subtract))
            chain(g.tensor_tensor(wrow[0:1, :-1], win_same[0:1, 1:], wtmp[:, :-1], ALU.mult))
            chain(g.tensor_copy(wrow[0:1, WIN_ITEMS - 1:], wtmp[:, WIN_ITEMS - 1:]))
            chain(g.tensor_tensor(wtmp, wtmp, wrow[0:1], ALU.subtract))
            chain(g.tensor_tensor(of_steps[1], of_steps[1], spares, ALU.add))
            g.tensor_copy(target[:], wtmp).then_inc(targets_ready, 1)
            for s in range(1, HOPS):
                pool.wait_ge(table_out, 16 * (2 + s * BANKS))
                gather_pass(staged_before(s), tab_f, ga)

        @block.scalar
        def _(act):
            def std(n):
                act.wait_ge(var_ready, n)
                nc.scalar.activation(stat[0:BN, 2, :], stat[0:BN, 1, :], ACT.Sqrt).then_inc(std_ready, 1)

            def turn_out(n):
                for k in range(BANKS):
                    b0, b1 = bank_buckets(k)
                    act.wait_ge(turned, n * BANKS + k + 1)
                    nc.scalar.copy(hT[:, b0 * BN:b1 * BN], bank(k, (b1 - b0) * BN)).then_inc(turned_out, 1)

            def stage_group(r, k, ahead=0):
                to = (k + ahead) % SLOTS
                nc.scalar.copy(stage[:, to, :], src_it[:, bass.ds(item_of(r, k, ahead), G)]).then_inc(staged, 1)

            def stage_pass(s):
                with act.Fori(0, ITERS) as r:
                    for k in range(SLOTS):
                        act.wait_ge(groups_done, r * SLOTS + (s * GROUPS + k + 1))
                        stage_group(r, k)

            std(1)
            std(2)
            turn_out(0)
            for q in range(PROJ_BATCHES):
                b0, b1 = q * BANKS, min(NB, (q + 1) * BANKS)
                act.wait_ge(proj_done, q + 1)
                for col, to in ((0, na), (2, x_sb)):
                    nc.scalar.copy(to[0:BN, b0:b1, :], proj_view(b1 - b0, col)).then_inc(proj_out, 1)
            act.wait_ge(items_ready, 1)
            for k in range(AHEAD):
                stage_group(0, k)
            act.wait_ge(item_degs, 1)
            nc.scalar.copy(item_deg, ps[:, 0:KB * BANK].rearrange("p (k n) -> p k n", n=BANK)[:, :, 0:BN]
                           ).then_inc(item_degs_out, 1)
            act.wait_ge(logs_ready, 1)
            nc.scalar.activation(log_deg[0:BN], log_deg[0:BN], ACT.Ln).then_inc(logs_ready, 1)
            def score_groups(r0, r1):
                with act.Fori(r0, r1) as r:
                    for k in range(SLOTS):
                        act.wait_ge(hot_turned, r * SLOTS + (k + 1))
                        nc.scalar.copy(hot_t[:, k % 2], bank(k % 2)[0:BN].rearrange("p (g e) -> p g e", g=G)
                                       ).then_inc(hot_t_out, 1)
                        act.wait_ge(scores_done, r * SLOTS + (SLOTS + k))
                        act.wait_ge(stored[(k + AHEAD) % SLOTS], r * 16 + 16)
                        stage_group(r, k, AHEAD)

            score_groups(0, WIN_TURN_AT)
            for n in range(4):
                act.wait_ge(win_turned, n + 1)
                nc.scalar.copy(win_rows[n], ps[:, 4 * BANK:4 * BANK + WIN_ITEMS]).then_inc(win_cols, 1)
            score_groups(WIN_TURN_AT, ITERS)
            act.wait_ge(key_free, 1)
            act.wait_ge(win_out, 32)
            for n in range(-(-CI // BPB)):
                j0, j1 = n * BPB, min(CI, (n + 1) * BPB)
                act.wait_ge(score_turned, n + 1)
                nc.scalar.copy(e_sc[:, j0 * P:j1 * P], bank(n % BANKS, (j1 - j0) * P)).then_inc(score_out, 1)
            act.wait_ge(var_ready, 3)
            nc.scalar.activation(dinv[0:BN], dinv[0:BN], ACT.Sqrt).then_inc(std_ready, 1)
            act.wait_ge(shifted, 1)
            for n in range(EXP_PARTS):
                w = L // EXP_PARTS
                nc.scalar.activation(e_sc[:, n * w:(n + 1) * w], e_sc[:, n * w:(n + 1) * w],
                                     ACT.Exp).then_inc(exps_ready, 1)
            act.wait_ge(exp_out, -(-CI // BPB))
            for s in range(1, HOPS):
                stage_pass(s)
            std(4)
            turn_out(1)
            for q in range(BANKS):
                b0, b1 = bank_buckets(q)
                n = (b1 - b0) * BN
                if q:
                    act.wait_ge(ff2_done, q)
                for c in range(FFC):
                    act.wait_ge(ff1_done, q * FFC + c + 1)
                    nc.scalar.activation(ffa[:, c, 0:n], bank(c, n), ACT.Relu,
                                         bias=b_ff1[:, c:c + 1]).then_inc(ff1_out, 1)
            std(5)
            turn_out(2)
            for n in range(LAYERS):
                with act.Fori(0, NB // RING) as r:
                    for u in range(RING):
                        act.wait_ge(conv_scaled, r * RING + (n * NB + u + 1))
                        nc.scalar.activation(turned_q[:, u, :], turned_q[:, u, :],
                                             ACT.Relu if n < LAYERS - 1 else ACT.Identity,
                                             bias=b_gcn[:, n:n + 1]).then_inc(conv_out, 1)

        @block.tensor
        def _(pe):
            def clear(banks):
                for k in banks:
                    nc.tensor.matmul(bank(k), zeros[:, 0:P], zeros[:], start=True, stop=False, skip_group_check=True)

            def sum_pass(s):
                for r0, r1 in ((0, BUILD_ITERS), (BUILD_ITERS, ITERS)) if s else ((0, ITERS),):
                    sum_groups(s, r0, r1, s > 0 and r0 == 0)

            def sum_groups(s, r0, r1, building):
                with pe.Fori(r0, r1) as r:
                    for k in range(SLOTS):
                        if building:
                            pe.wait_ge(prod_ready, r * SLOTS + (steps_before(s) + k + 1))
                            pe.wait_ge(acc_ready, r * SLOTS + (steps_before(s) + k + 1))
                            for j in range(BG):
                                mm = nc.tensor.matmul(ps[:, 7 * BANK + j * CELL:7 * BANK + (j + 1) * CELL],
                                                      hot_p[:, k % 2, j, :], prod[:, k % 2, j, :],
                                                      start=True, stop=True)
                            mm.then_inc(cell_sums, 1)
                        pe.wait_ge(msgs_ready, r * (2 * SLOTS) + (msgs_before(s) + 2 * (k + 1)))
                        for j, b in enumerate(buckets_of(pe, item_of(r, k))):
                            i = r * PER_ITER + (k * G + j)
                            if s == 0:
                                nc.tensor.matmul(ps[0:BN, bass.ds(b * HEADS + EX_SUMS, HEADS)], hot[:, k, j, :],
                                                 ex_it[:, bass.ds(i, 1), :].rearrange("p i c -> p (i c)"),
                                                 start=False, stop=False, skip_group_check=True)
                            mm = nc.tensor.matmul(ps[0:BN, bass.ds(b * F, F)], hot[:, k, j, :], ga[:, k, j, :],
                                                  start=False, stop=False, skip_group_check=True)
                        mm.then_inc(groups_done, 1)

            def turn(n, rows_):
                pe.wait_ge(h_ready, n + 1)
                for k in range(BANKS):
                    b0, b1 = bank_buckets(k)
                    for b in range(b0, b1):
                        t = nc.tensor.transpose(bank(k)[:, (b - b0) * BN:(b - b0 + 1) * BN], rows_[0:BN, b, :],
                                                ident[0:BN, 0:BN])
                    t.then_inc(turned, 1)

            pe.sem_inc(groups_done, SLOTS)
            pe.sem_inc(hots_used, SLOTS)
            pe.wait_ge(masks_set, MASKS)
            pe.wait_ge(zeros_set, 3)
            pe.wait_ge(counted, 1)
            nc.tensor.matmul(small[:, 0:NB + 1], ones[:], thr[:, 1, :], start=True, stop=True).then_inc(summed, 1)
            pe.wait_ge(order_known, 1)
            with pe.If(pe.value_load(disorder[0:1, 0:1], min_val=0, max_val=TILES * P) != 0):
                pe.wait_ge(sort_masks, 3)
                for n in range(SORT_PASSES):
                    pe.wait_ge(sort_counted, n + 1)
                    nc.tensor.matmul(bank(0, RADIX), ones[:], s_count, start=True, stop=True).then_inc(sort_summed, 1)
                    with pe.Fori(0, TILES) as r:
                        pe.wait_ge(sort_hot, r + (n * TILES + 1))
                        nc.tensor.matmul(bank(1, RADIX), s_lower, s_hot, start=True, stop=True)
                        nc.tensor.matmul(bank(2, RADIX), ones[:], s_hot, start=True, stop=True).then_inc(sort_prefix, 1)
                pe.wait_ge(sort_ranked, TILES * SORT_PASSES)
            pe.wait_ge(consts_in, 16 * LOADS)
            for k in range(3):
                nc.tensor.transpose(bank(0)[:, k * F:(k + 1) * F], w_raw[:, k, :], ident[:])
            for c in range(FFC):
                nc.tensor.transpose(bank(1)[:, c * P:(c + 1) * P], ff1_raw[:, c, :], ident[:])
            for c in range(FFC):
                t = nc.tensor.transpose(bank(2)[:, c * F:(c + 1) * F], ff2_raw[:, c * P:(c + 1) * P], ident[:])
            t.then_inc(weights_turned, 1)
            pe.wait_ge(weights_ready, 3)
            pe.wait_ge(rows_ready, 2)
            for v in range(3):
                rows_ = (row_f[0], row_f[2], row_raw[2])[v]
                if v >= 1:
                    pe.wait_ge(items_ready, v)
                for k in range(KB):
                    t = nc.tensor.transpose(bank(k, P), rows_[:, k, :], ident[:])
                t.then_inc(rows_turned, 1)
            turn(0, na)
            pe.wait_ge(turned_out, BANKS)
            for q in range(PROJ_BATCHES):
                b0, b1 = q * BANKS, min(NB, (q + 1) * BANKS)
                if q:
                    pe.wait_ge(proj_out, 2 * q)
                    pe.wait_ge(tails_out, 2 * q)
                for b in range(b0, b1):
                    mm = nc.tensor.matmul(bank(b - b0, 3 * F)[0:BN], hT[:, b * BN:(b + 1) * BN], w_qkv[:],
                                          start=True, stop=True)
                mm.then_inc(proj_done, 1)
            pe.wait_ge(proj_out, 2 * PROJ_BATCHES)
            pe.wait_ge(tails_out, 2 * PROJ_BATCHES)
            pe.wait_ge(slide_set, 1)
            nc.tensor.matmul(small[:, 0:KB * NB], anti[:], ge[:].rearrange("p k b -> p (k b)"), start=True,
                             stop=True).then_inc(reversed_, 1)
            clear(range(KB))
            per_block = P // PER_ITER
            for kb in range(KB):
                with pe.Fori(0, min(per_block, ITERS - kb * per_block)) as r:
                    for k in range(SLOTS):
                        pe.wait_ge(hots_ready, r * SLOTS + (kb * per_block * SLOTS + k + 1))
                        for j in range(G):
                            mm = nc.tensor.matmul(bank(kb, BN), slide[:, bass.ds(r * PER_ITER + (k * G + j), P)],
                                                  hot_b[:, k, j, :],
                                                  start=False, stop=False, skip_group_check=True)
                        mm.then_inc(hots_used, 1)
            pe.drain().then_inc(item_degs, 1)
            pe.wait_ge(item_degs_out, 1)
            for k in range(KB):
                mm = nc.tensor.matmul(small[0:BN, 0:NB], item_deg[:, k, :], ge_rev[:, k, :], start=(k == 0),
                                      stop=(k == KB - 1))
            mm.then_inc(degs_ready, 1)
            pe.wait_ge(scaled, 1)
            pe.wait_ge(bucket_in, 16)
            clear([7])

            def score_groups(r0, r1):
                with pe.Fori(r0, r1) as r:
                    for k in range(SLOTS):
                        pe.wait_ge(msgs_ready, r * SLOTS + (k + 1))
                        for j in range(G):
                            t = nc.tensor.transpose(bank(k % 2)[0:BN, j * P:(j + 1) * P], hot[:, k, j, :], ident[:])
                        t.then_inc(hot_turned, 1)
                        buckets = buckets_of(pe, item_of(r, k))
                        pe.wait_ge(hot_t_out, r * SLOTS + (k + 1))
                        pe.wait_ge(scores_done, r * SLOTS + (SLOTS + k - 1))
                        for j, b in enumerate(buckets):
                            nc.tensor.matmul(ps[0:BN, bass.ds(b + W_SUMS, 1)], hot[:, k, j, :],
                                             w_it[:, bass.ds(r * PER_ITER + (k * G + j), 1)],
                                             start=False, stop=False, skip_group_check=True)
                            mm = nc.tensor.matmul(bank(2 + k % 2)[:, j * F:(j + 1) * F], hot_t[:, k % 2, j, :],
                                                  nb_pad[0:BN, bass.ds(b, 1), :].rearrange("p b f -> p (b f)"),
                                                  start=True, stop=True)
                        mm.then_inc(tails_ready, 1)

            score_groups(0, WIN_COUNT_AT)
            pe.wait_ge(win_counted, 1)
            half = -(-NB // 2)
            nc.tensor.matmul(bank(4, half * WPB), ones[0:BN, :], win_tmp[0][0:BN, 0:half * WPB], start=True, stop=True)
            nc.tensor.matmul(bank(5, (NB - half) * WPB), ones[0:BN, :], win_tmp[0][0:BN, half * WPB:],
                             start=True, stop=True).then_inc(win_summed, 1)
            score_groups(WIN_COUNT_AT, WIN_TURN_AT)
            for n in range(4):
                pe.wait_ge(win_rows_ready, n + 1)
                if n:
                    pe.wait_ge(win_cols, n)
                for k in range(KW):
                    t = nc.tensor.transpose(ps[:, 4 * BANK + k * P:4 * BANK + (k + 1) * P],
                                            win_rows[n][:, k * P:(k + 1) * P], ident[:])
                t.then_inc(win_turned, 1)
            score_groups(WIN_TURN_AT, ITERS)
            pe.drain().then_inc(w_summed, 1)
            pe.wait_ge(scores_done, SLOTS + GROUPS)
            by_chunk = ex_it[:].rearrange("p (j c) h -> p j (c h)", c=CHUNKS)
            for n in range(-(-CI // BPB)):
                if n >= BANKS:
                    pe.wait_ge(score_out, n - BANKS + 1)
                for j in range(n * BPB, min(CI, (n + 1) * BPB)):
                    t = nc.tensor.transpose(bank(n % BANKS)[:, (j % BPB) * P:(j % BPB + 1) * P], by_chunk[:, j, :], ident[:])
                t.then_inc(score_turned, 1)
            for n in range(2):
                pe.wait_ge(ends_ready, n + 1)
                for k in range(4):
                    t = nc.tensor.matmul(small[0:1, k * P:(k + 1) * P], ends[:, k:k + 1], ident[:],
                                         start=True, stop=True)
                t.then_inc(ends_turned, 1)
                pe.wait_ge(carry_ready, n + 1)
                nc.tensor.matmul(bank(0, 1), carry[0:1, 4, :], ones[0:1, 0:1], start=True,
                                 stop=True).then_inc(carry_turned, 1)
            for n in range(-(-CI // BPB)):
                pe.wait_ge(exps_ready, -(-min(CI, (n + 1) * BPB) * EXP_PARTS // CI))
                if n == 0:
                    pe.wait_ge(score_out, -(-CI // BPB))
                if n >= BANKS:
                    pe.wait_ge(exp_out, n - BANKS + 1)
                for j in range(n * BPB, min(CI, (n + 1) * BPB)):
                    t = nc.tensor.transpose(bank(n % BANKS)[:, (j % BPB) * P:(j % BPB + 1) * P],
                                            e_sc[:, j * P:(j + 1) * P], ident[:])
                t.then_inc(exp_turned, 1)
            pe.wait_ge(exp_out, -(-CI // BPB))
            clear([7])
            for n in range(HOPS):
                if n:
                    pe.wait_ge(sums_out, n * BANKS)
                clear(range(BANKS))
                sum_pass(n)
            turn(1, nb_)
            pe.wait_ge(turned_out, 2 * BANKS)
            for q in range(BANKS):
                b0, b1 = bank_buckets(q)
                n = (b1 - b0) * BN
                for c in range(FFC):
                    if q:
                        pe.wait_ge(ff1_out, (q - 1) * FFC + c + 1)
                    nc.tensor.matmul(bank(c, n), ff1_t[:, c * P:(c + 1) * P], hT[:, b0 * BN:b1 * BN],
                                     start=True, stop=True).then_inc(ff1_done, 1)
                pe.wait_ge(ff1_out, (q + 1) * FFC)
                if q >= 2:
                    pe.wait_ge(ff2_out, q - 1)
                for b in range(b0, b1):
                    for c in range(FFC):
                        mm = nc.tensor.matmul(bank(4 + q % 2)[0:BN, (b - b0) * F:(b - b0 + 1) * F],
                                              ffa[:, c, (b - b0) * BN:(b - b0 + 1) * BN], ff2_t[:, c, :],
                                              start=(c == 0), stop=(c == FFC - 1))
                mm.then_inc(ff2_done, 1)
            turn(2, na)
            for k in range(BANKS):
                pe.wait_ge(turned_out, 2 * BANKS + k + 1)
                b0, b1 = bank_buckets(k)
                for b in range(b0, b1):
                    mm = nc.tensor.matmul(bank(k)[0:BN, (b - b0) * F:(b - b0 + 1) * F],
                                          hT[:, b * BN:(b + 1) * BN], w_gcn[:, 0, :], start=True, stop=True)
                mm.then_inc(gcn_done, 1)
            pe.wait_ge(table_ready, 1 + HOPS * BANKS)

            def next_product(n, r, u):
                pe.wait_ge(conv_out, r * RING + (n * NB + u + 1))
                if n or u >= 2:
                    pe.wait_ge(next_out, r * RING + (n * NB + u - 1))
                nc.tensor.matmul(bank(NEXT_BANK[u], F)[0:BN], turned_q[:, u, :],
                                 w_gcn[:, n + 1, :] if n < LAYERS - 1 else ident[:],
                                 start=True, stop=True).then_inc(next_done, 1)

            for n in range(LAYERS):
                rows_ = (nb_, na)[n % 2]
                if n:
                    pe.wait_ge(next_out, n * NB)
                with pe.Fori(0, NB // RING) as r:
                    for u in range(RING):
                        pe.wait_ge(loops_in, r * RING + (n * NB + u + 1))
                        cells = cells_of(u)
                        for b in range(NB):
                            mm = nc.tensor.matmul(bank(u, BN).rearrange("p (w d) -> p w d", d=WN), rows_[0:BN, b, :],
                                                  cells[:, :, b, :], start=(b == 0), stop=(b == NB - 1))
                        mm.then_inc(conv_done, 1)
                        if u:
                            next_product(n, r, u - 1)
                    next_product(n, r, RING - 1)

        @block.vector
        def _(dve):
            count = [0]

            def link(ins):
                count[0] += 1
                ins.then_inc(dve_link, 1)
                dve.wait_ge(dve_link, count[0])

            v = nc.vector

            def tt(to, x, y, op):
                link(v.tensor_tensor(to, x, y, op))

            def layernorm(to, x, scratch, n):
                link(v.tensor_reduce(stat[0:BN, 0, :], x[0:BN], AX.X, ALU.add))
                link(v.tensor_scalar(stat[0:BN, 0, :], stat[0:BN, 0, :], 1.0 / F, None, ALU.mult))
                tt(to[0:BN], x[0:BN], over_f(stat[0:BN, 0, :]), ALU.subtract)
                tt(scratch[0:BN], to[0:BN], to[0:BN], ALU.mult)
                link(v.tensor_reduce(stat[0:BN, 3, :], scratch[0:BN], AX.X, ALU.add))
                v.tensor_scalar(stat[0:BN, 1, :], stat[0:BN, 3, :], 1.0 / F, EPS, ALU.mult,
                                ALU.add).then_inc(var_ready, 1)
                dve.wait_ge(std_ready, n)
                link(v.reciprocal(stat[0:BN, 3, :], stat[0:BN, 2, :]))
                tt(to[0:BN], to[0:BN], over_f(stat[0:BN, 3, :]), ALU.mult)

            def over_f(x):
                return x.unsqueeze(2).to_broadcast([BN, NB, F])

            def over_nodes(k):
                return rowvec[0:BN, k:k + 1, :].to_broadcast([BN, NB, F])

            def onehots(to, r, k, ahead=0):
                return v.tensor_tensor(to[:, (k + ahead) % SLOTS],
                                       dloc[:, bass.ds(item_of(r, k, ahead), G)].unsqueeze(2).to_broadcast([P, G, BN]),
                                       iota_bn.unsqueeze(1).to_broadcast([P, G, BN]), ALU.is_equal)

            def message_pass(s):
                for r0, r1 in ((0, BUILD_ITERS), (BUILD_ITERS, ITERS)) if s else ((0, ITERS),):
                    message_groups(s, r0, r1, s > 0 and r0 == 0)
                dve.wait_ge(groups_done, SLOTS + (s + 1) * GROUPS)

            def build_factors(s, r, k):
                i = win_item(s, r, k)
                v.tensor_tensor(hot_p[:, k % 2], win_p[:, bass.ds(i, BG)].unsqueeze(2).to_broadcast([P, BG, P]),
                                iota_p[:].unsqueeze(1).to_broadcast([P, BG, P]), ALU.is_equal)
                v.tensor_tensor(hot_bk[:, k % 2], win_b[:, bass.ds(i, BG)].unsqueeze(2).to_broadcast([P, BG, NB]),
                                iota_bn[:, 0:NB].unsqueeze(1).to_broadcast([P, BG, NB]),
                                ALU.is_equal).then_inc(build_link, 1)
                for j in range(BG):
                    v.tensor_scalar(hot_d[:, k % 2, j, :], iota_bn[:, 0:WN], win_dd[:, bass.ds(win_item(s, r, k, j), 1)],
                                    win_w[:, bass.ds(win_item(s, r, k, j), 1)], ALU.is_equal,
                                    ALU.mult).then_inc(build_link, 1)
                dve.wait_ge(build_link, r * (SLOTS * (BG + 1)) + (steps_before(s) + k + 1) * (BG + 1))
                v.tensor_tensor(prod[:, k % 2].rearrange("p j (b d) -> p j b d", d=WN),
                                hot_bk[:, k % 2].unsqueeze(3).to_broadcast([P, BG, NB, WN]),
                                hot_d[:, k % 2].unsqueeze(2).to_broadcast([P, BG, NB, WN]),
                                ALU.mult).then_inc(prod_ready, 1)

            def build_sums(s, r, k):
                dve.wait_ge(cell_sums, r * SLOTS + (steps_before(s) + k + 1))
                dve.wait_ge(acc_out[k], r * (16 * BG) + 16 * BG * ((s - 1) * BUILD_ITERS + 1))
                for j in range(BG):
                    before = win_acc[:, k, j - 1, 0:CELL] if j else win_acc[:, (k - 1) % SLOTS, BG - 1, 0:CELL]
                    ins = v.scalar_tensor_tensor(
                        out=win_acc[:, k, j, 0:CELL], in0=before,
                        scalar=win_same[:, bass.ds(win_item(s, r, k, j), 1)],
                        in1=ps[:, 7 * BANK + j * CELL:7 * BANK + (j + 1) * CELL], op0=ALU.mult, op1=ALU.add)
                    if j < BG - 1:
                        ins.then_inc(sum_link, 1)
                        dve.wait_ge(sum_link, r * (SLOTS * (BG - 1)) + ((steps_before(s) + k) * (BG - 1) + j + 1))
                ins.then_inc(acc_ready, 1)
                dve.wait_ge(acc_ready, r * SLOTS + (steps_before(s) + k + 2))

            def message_groups(s, r0, r1, building):
                with dve.Fori(r0, r1) as r:
                    for k in range(SLOTS):
                        if building:
                            build_factors(s, r, k)
                        if s == 0:
                            dve.wait_ge(loaded[k], r * 16 + 16)
                        else:
                            dve.wait_ge(got[k], r * (16 * G) + (got_before(s) + 16 * G))
                        onehots(hot, r, k).then_inc(msgs_ready, 1)
                        i = item_of(r, k)
                        rows_ = ga[:, k].rearrange("p g (h d) -> p (g h) d", h=HEADS)
                        by = ex_it[:, bass.ds(i, G), :].rearrange("p g h -> p (g h)").unsqueeze(2).to_broadcast(
                            [P, G * HEADS, HD])
                        v.tensor_tensor(rows_, rows_, by, ALU.mult).then_inc(msgs_ready, 1)
                        if building:
                            build_sums(s, r, k)

            def sort_edges():
                sort_count = [0]

                def chain(ins):
                    sort_count[0] += 1
                    ins.then_inc(sort_link, 1)
                    dve.wait_ge(sort_link, sort_count[0])

                dve.wait_ge(sort_in, 32)
                chain(v.memset(edges, 0.0))
                chain(v.tensor_copy(edges[:, :, 0], s_raw.bitcast(I32)))
                chain(v.tensor_copy(edges[:, :, 1], dst_allf))
                chain(v.tensor_copy(edges[:, :, 2], s_digit))
                dve.wait_ge(sort_masks, 3)
                for n in range(SORT_PASSES):
                    if n:
                        dve.wait_ge(sort_in, 32 + 16 * n)
                    chain(v.tensor_copy(s_raw.bitcast(I32), edges[:, :, 1]))
                    chain(v.tensor_scalar(s_raw.bitcast(I32), s_raw.bitcast(I32), *(
                        (RADIX - 1, None, ALU.bitwise_and) if n == 0 else (RADIX_BITS, None, ALU.arith_shift_right))))
                    chain(v.tensor_copy(s_digit, s_raw.bitcast(I32)))
                    for d in range(RADIX):
                        chain(v.tensor_scalar(s_raw, s_digit, float(d), 0.0, ALU.is_lt, ALU.add,
                                              accum_out=s_count[:, d:d + 1]))
                    dve.sem_inc(sort_counted, 1)
                    dve.wait_ge(sort_summed, n + 1)
                    chain(v.tensor_copy(s_base, bank(0, RADIX)))
                    steps, before = [0], sort_count[0]
                    STEPS = 8 + 4 * (n == 0)

                    with dve.Fori(0, TILES) as r:
                        def step(ins):
                            steps[0] += 1
                            ins.then_inc(sort_link, 1)
                            dve.wait_ge(sort_link, r * STEPS + (before + steps[0]))

                        v.tensor_tensor(s_hot, s_iota, s_digit[:, bass.ds(r, 1)].to_broadcast([P, RADIX]),
                                        ALU.is_equal).then_inc(sort_hot, 1)
                        step(v.tensor_copy(s_move, edges[:, bass.ds(r, 1), :].rearrange("p t c -> p (t c)")))
                        dve.wait_ge(sort_prefix, r + (n * TILES + 1))
                        step(v.tensor_tensor(s_tmp, s_base, bank(1, RADIX), ALU.add))
                        step(v.tensor_tensor(s_tmp, s_tmp, s_hot, ALU.mult))
                        step(v.tensor_reduce(s_rank[:, 0:1], s_tmp, AX.X, ALU.add))
                        step(v.tensor_tensor(s_base, s_base, bank(2, RADIX), ALU.add))
                        step(v.tensor_copy(s_rank[:, 1:2].bitcast(I32), s_rank[:, 0:1]))
                        if n == 0:
                            step(v.tensor_scalar(s_rank[:, 2:3].bitcast(I32), s_rank[:, 1:2].bitcast(I32),
                                                 P.bit_length() - 1, None, ALU.arith_shift_right))
                            step(v.tensor_scalar(s_rank[:, 1:2].bitcast(I32), s_rank[:, 1:2].bitcast(I32),
                                                 P - 1, None, ALU.bitwise_and))
                            step(v.tensor_copy(s_rank[:, 0:1], s_rank[:, 1:2].bitcast(I32)))
                            step(v.tensor_copy(s_tmp[:, 0:1], s_rank[:, 2:3].bitcast(I32)))
                            step(v.scalar_tensor_tensor(out=s_rank[:, 1:2], in0=s_rank[:, 0:1], scalar=float(TILES),
                                                        in1=s_tmp[:, 0:1], op0=ALU.mult, op1=ALU.add))
                            step(v.tensor_copy(s_rank[:, 3:4].bitcast(I32), s_rank[:, 1:2]))
                        else:
                            step(v.tensor_copy(s_tmp[:, 0:1], s_rank[:, 0:1]))
                            step(v.tensor_copy(s_rank[:, 3:4].bitcast(I32), s_rank[:, 0:1]))
                        dve.sem_inc(sort_ranked, 1)
                        dve.wait_ge(sort_moved, r * 16 + 16 * (n * TILES + 1))
                    assert steps[0] == STEPS, steps
                    sort_count[0] = before + STEPS * TILES
                dve.wait_ge(sort_in, 32 + 16 * SORT_PASSES)
                chain(v.tensor_copy(s_raw.bitcast(I32), edges[:, :, 0]))
                chain(v.tensor_copy(s_digit.bitcast(I32), edges[:, :, 1]))
                chain(v.tensor_copy(dst_allw, edges[:, :, 2]))
                dve.sem_inc(sort_split, 1)

            dve.sem_inc(scores_done, SLOTS)
            v.memset(zeros[:], 0.0).then_inc(zeros_set, 1)
            v.memset(ones[:], 1.0).then_inc(zeros_set, 1)
            v.memset(nb_pad[:, NB, :], 0.0).then_inc(zeros_set, 1)
            dve.wait_ge(masks_set, MASKS)
            dve.wait_ge(dst_in, 32)
            link(v.tensor_scalar(step5[:], step5[:], 0.0, None, ALU.is_ge))
            link(v.tensor_copy(dst_allf, dst_all))
            link(v.scalar_tensor_tensor(out=nb_.rearrange("p b f -> p (b f)")[:, 0:TILES], in0=dst_allf, scalar=0.0,
                                        in1=dst_next, op0=ALU.add, op1=ALU.is_gt, accum_out=thr[:, 1, NB:NB + 1]))
            for b in range(NB):
                link(v.tensor_scalar(nb_.rearrange("p b f -> p (b f)")[:, 0:TILES], dst_allf, float(BN * (b + 1)),
                                     0.0, ALU.is_lt, ALU.add, accum_out=thr[:, 1, b:b + 1]))
            dve.sem_inc(counted, 1)
            dve.wait_ge(summed, 1)
            v.tensor_copy(disorder[:], small[:, NB:NB + 1]).then_inc(order_known, 1)
            dve.wait_ge(order_known, 1)
            with dve.If(dve.value_load(disorder[0:1, 0:1], min_val=0, max_val=TILES * P) != 0):
                sort_edges()
            link(v.tensor_copy(thr_i[:], small[:, 0:NB + 1]))
            link(v.tensor_scalar(thr_i[:], thr_i[:], P.bit_length() - 1, None, ALU.arith_shift_right))
            link(v.tensor_copy(thr[:, 2, :], thr_i[:]))
            tt(thr[:, 2, :], thr[:, 2, :], thr[:, 0, :], ALU.add)
            link(v.tensor_scalar(thr[:, 0, :], thr[:, 0, :], -1.0, None, ALU.add))
            link(v.tensor_scalar(item_b[:], item_t[:], CHUNKS - 1, None, ALU.bitwise_and))
            link(v.tensor_scalar(item_t[:], item_t[:], CHUNKS.bit_length() - 1, None, ALU.arith_shift_right))
            link(v.tensor_copy(item_f[:, 1, :], item_b[:]))
            link(v.tensor_copy(item_f[:, 2, :], item_t[:]))
            link(v.scalar_tensor_tensor(out=item_f[:, 0, :], in0=item_f[:, 1, :], scalar=float(CI),
                                        in1=item_f[:, 2, :], op0=ALU.mult, op1=ALU.add))
            tt(ge[:], item_f[:, 0, :].unsqueeze(2).to_broadcast([P, KB, NB]),
               thr[:, 2, 0:NB].unsqueeze(1).to_broadcast([P, KB, NB]), ALU.is_ge)
            link(v.tensor_reduce(item_f[:, 1, :], ge[:], AX.X, ALU.add))
            tt(item_f[:, 2, :], item_f[:, 0, :], item_f[:, 1, :], ALU.subtract)
            link(v.tensor_copy(item_b[:], item_f[:, 1, :]))
            link(v.tensor_scalar(item_f[:, 3, :], item_f[:, 1, :], float(BN), None, ALU.mult))
            v.tensor_scalar(item_t[:], item_f[:, 2, :], float(TILES - 1), None, ALU.min).then_inc(tiles_known, 1)
            link(v.tensor_copy(anti[:], ident[:, ::-1]))
            tt(ge[:], item_f[:, 1, :].unsqueeze(2).to_broadcast([P, KB, NB]),
               thr[:, 0, 0:NB].unsqueeze(1).to_broadcast([P, KB, NB]), ALU.is_equal)
            dve.wait_ge(weights_turned, 1)
            v.tensor_copy(w_qkv[:], bank(0, 3 * F)).then_inc(weights_ready, 1)
            v.tensor_copy(ff1_t[:], bank(1)).then_inc(weights_ready, 1)
            v.tensor_copy(ff2_t[:].rearrange("p c f -> p (c f)"), bank(2)).then_inc(weights_ready, 1)
            dve.wait_ge(rows_in, 3 * KB * 16)
            v.tensor_copy(row_f[0], row_i[0]).then_inc(rows_ready, 1)
            v.tensor_tensor(row_f[2], row_i[1], item_f[:, 3, :].unsqueeze(2).to_broadcast([P, KB, P]),
                            ALU.subtract).then_inc(rows_ready, 1)
            turned_rows = ps[:, 0:KB * BANK].rearrange("p (k n) -> p k n", n=BANK)[:, :, 0:P]
            for n, to in enumerate((src_it[:], dloc[:], w_it[:])):
                dve.wait_ge(rows_turned, n + 1)
                v.tensor_copy(to.rearrange("p (k e) -> p k e", e=P), turned_rows).then_inc(items_ready, 1)
            dve.wait_ge(items_ready, 3)
            dve.wait_ge(x_in, 16)
            dve.wait_ge(key_out, 16)
            layernorm(h0, h0, na, 1)
            link(v.tensor_scalar(h0[0:BN], h0[0:BN], 0.0, None, ALU.max))
            layernorm(na, h0, nb_, 2)
            tt(na[0:BN], na[0:BN], over_nodes(G1), ALU.mult)
            v.tensor_tensor(na[0:BN], na[0:BN], over_nodes(B1), ALU.add).then_inc(h_ready, 1)
            dve.wait_ge(turned_out, BANKS)
            for q in range(PROJ_BATCHES):
                b0, b1 = q * BANKS, min(NB, (q + 1) * BANKS)
                dve.wait_ge(proj_out, 2 * (q + 1))
                v.tensor_copy(nb_[0:BN, b0:b1, :], proj_view(b1 - b0, 1)).then_inc(tails_out, 1)
                v.tensor_scalar(fe_a[0:BN, b0:b1, :], proj_view(b1 - b0, 2), ALPHA, None,
                                ALU.mult).then_inc(tails_out, 1)
            dve.wait_ge(tails_out, 2 * PROJ_BATCHES)
            dve.sem_inc(table_ready, 1)
            dve.wait_ge(reversed_, 1)
            link(v.tensor_copy(ge_rev[:].rearrange("p k b -> p (k b)"), small[:, 0:KB * NB]))
            with dve.Fori(0, ITERS) as r:
                for k in range(SLOTS):
                    dve.wait_ge(hots_used, r * SLOTS + (k + 1))
                    onehots(hot_b, r, k).then_inc(hots_ready, 1)
            dve.wait_ge(degs_ready, 1)
            v.tensor_scalar(log_deg[0:BN], small[0:BN, 0:NB], 1.0, None, ALU.max).then_inc(logs_ready, 1)
            link(v.tensor_copy(deg_n[0:BN], small[0:BN, 0:NB]))
            dve.wait_ge(logs_ready, 2)
            link(v.tensor_scalar(log_deg[0:BN], log_deg[0:BN], 1.0 / HD, None, ALU.mult))
            v.tensor_tensor(nb_[0:BN, 0:NB], nb_[0:BN, 0:NB], over_f(log_deg[0:BN]), ALU.mult).then_inc(scaled, 1)
            onehots(hot, 0, 0).then_inc(msgs_ready, 1)

            def score_groups(r0, r1):
                with dve.Fori(r0, r1) as r:
                    for k in range(SLOTS):
                        onehots(hot, r, k, 1).then_inc(msgs_ready, 1)
                        heads = ga_wide[:, k, :, 0:F]
                        dve.wait_ge(got[k], r * (16 * G) + 16 * G)
                        dve.wait_ge(tails_ready, r * SLOTS + (k + 1))
                        v.tensor_tensor(heads, heads, bank(2 + k % 2).rearrange("p (g f) -> p g f", g=G),
                                        ALU.mult).then_inc(step_link, 1)
                        dve.wait_ge(step_link, r * (3 * SLOTS) + (3 * k + 1))
                        v.scalar_tensor_tensor(out=heads, in0=heads, scalar=SLOPE, in1=heads, op0=ALU.mult,
                                               op1=ALU.max).then_inc(step_link, 1)
                        dve.wait_ge(step_link, r * (3 * SLOTS) + (3 * k + 2))
                        v.tensor_tensor(heads, heads, rowvec[:, ATTN:ATTN + 1, :].to_broadcast([P, G, F]),
                                        ALU.mult).then_inc(step_link, 1)
                        dve.wait_ge(step_link, r * (3 * SLOTS) + (3 * k + 3))
                        v.tensor_reduce(ex_it[:, bass.ds(item_of(r, k), G), :],
                                        heads.rearrange("p g (h d) -> p g h d", h=HEADS),
                                        AX.X, ALU.add).then_inc(scores_done, 1)

            score_groups(0, WIN_COUNT_AT)
            ends_at, ends_i, junk = win_tmp
            dve.wait_ge(table_out, 32)
            by_window = ends_at.rearrange("p (b j) -> p b j", j=WPB)
            run_deg, before_deg = stat[0:BN, 0, :], stat[0:BN, 1, :]
            link(v.tensor_tensor_scan(run_deg, ones[0:BN, 0:NB], deg_n[0:BN], 0.0, ALU.mult, ALU.add))
            tt(before_deg, run_deg, deg_n[0:BN], ALU.subtract)
            tt(by_window[0:BN], deg_n[0:BN].unsqueeze(2).to_broadcast([BN, NB, WPB]),
               step5[0:BN].unsqueeze(1).to_broadcast([BN, NB, WPB]), ALU.mult)
            v.tensor_tensor(by_window[0:BN], by_window[0:BN], before_deg.unsqueeze(2).to_broadcast([BN, NB, WPB]),
                            ALU.add).then_inc(win_counted, 1)
            dve.wait_ge(win_summed, 1)
            half = -(-NB // 2) * WPB
            link(v.tensor_copy(ends_i.bitcast(I32)[:, 0:half], bank(4, half)))
            link(v.tensor_copy(ends_i.bitcast(I32)[:, half:], bank(5, WINDOWS - half)))
            link(v.tensor_scalar(ends_i.bitcast(I32), ends_i.bitcast(I32), P.bit_length() - 1, None,
                                 ALU.arith_shift_right))
            link(v.tensor_copy(ends_at, ends_i.bitcast(I32)))
            link(v.tensor_scalar(stat[:, 2, :], iota_bn[:, 0:NB], float(WPB), 1.0, ALU.mult, ALU.add))
            tt(by_window, by_window, stat[:, 2, :].unsqueeze(2).to_broadcast([P, NB, WPB]), ALU.add)
            tt(by_window, by_window, iota_bn[:, 0:WPB].unsqueeze(1).to_broadcast([P, NB, WPB]), ALU.add)
            for k in range(KW):
                link(v.tensor_scalar(junk, ends_at, win_it[:, k:k + 1], 0.0, ALU.is_le, ALU.add,
                                     accum_out=win_f[:, 0, k:k + 1]))
            link(v.tensor_scalar(win_f[:, 1, :], win_f[:, 0, :], float(WN), None, ALU.mult))
            tt(win_it[:], win_it[:], win_f[:, 0, :], ALU.subtract)
            v.tensor_scalar(win_t[:], win_it[:], float(TILES - 1), None, ALU.min).then_inc(win_known, 1)
            score_groups(WIN_COUNT_AT, WIN_ROWS_AT)
            dve.wait_ge(win_rows_in, 16 * 3 * KW)
            w_src, w_bkt, w_dst = win_rows[0:3]
            link(v.tensor_copy(w_src, w_src.bitcast(I32)))
            link(v.tensor_scalar(w_bkt, w_src, -(BN - 1) / 2, 1.0 / BN, ALU.add, ALU.mult))
            link(v.tensor_scalar(w_bkt, w_bkt, ROUND, None, ALU.add))
            link(v.tensor_scalar(w_bkt, w_bkt, -ROUND, None, ALU.add))
            v.scalar_tensor_tensor(out=w_src, in0=w_bkt, scalar=-float(BN), in1=w_src, op0=ALU.mult,
                                   op1=ALU.add).then_inc(win_rows_ready, 2)
            v.tensor_tensor(w_dst.rearrange("p (k e) -> p k e", e=P), w_dst.bitcast(I32).rearrange("p (k e) -> p k e", e=P),
                            win_f[:, 1, :].unsqueeze(2).to_broadcast([P, KW, P]),
                            ALU.subtract).then_inc(win_rows_ready, 2)
            score_groups(WIN_ROWS_AT, ITERS)
            dve.wait_ge(scores_done, SLOTS + GROUPS)
            for k in range(SLOTS):
                dve.wait_ge(stored[k], 16 * (ITERS + (k == SLOTS - 1)))
            dve.sem_inc(key_free, 1)
            dve.wait_ge(w_summed, 1)
            link(v.tensor_scalar(stat[0:BN, 0, :], ps[0:BN, W_SUMS:W_SUMS + NB], 1.0, None, ALU.add))
            link(v.tensor_scalar(w_deg[0:BN], stat[0:BN, 0, :], 0.0, None, ALU.is_gt))
            v.tensor_scalar(dinv[0:BN], stat[0:BN, 0, :], 1e-30, None, ALU.max).then_inc(var_ready, 1)
            dve.wait_ge(key_in, 16 * CHUNKS)
            link(v.memset(gap[:], 0.0))
            tt(gap[:, 1:L], key[:, 1:L], key[:, 0:L - 1], ALU.not_equal)
            link(v.tensor_scalar(gap[:], gap[:], -BIG, None, ALU.mult))
            link(v.tensor_reduce(ends[:, 1:2], gap[:, 0:L], AX.X, ALU.min))
            link(v.tensor_copy(ends[:, 2:3], key[:, 0:1]))
            link(v.tensor_copy(ends[:, 3:4], key[:, L - 1:L]))
            dve.wait_ge(score_out, -(-CI // BPB))

            def scan_carried(n, to, gaps, data, last, back):
                link(v.tensor_tensor_scan(to, gaps, data, -BIG, ALU.add, ALU.max))
                v.tensor_copy(ends[:, 0:1], last).then_inc(ends_ready, 1)
                dve.wait_ge(ends_turned, n + 1)
                link(v.tensor_copy(rows[:], small[0:1, 0:4 * P].rearrange("o (k c h) -> o k h c", k=4, h=HEADS)))
                way = slice(None, None, -1) if back else slice(None)
                row = [rows[0:1, k, :, way] for k in range(4)]
                final, gate, first, last_ = (row[0], row[1], row[3], row[2]) if back else row
                gates, new, run, cut = (carry[0:1, k, :].rearrange("o (h c) -> o h c", h=HEADS) for k in range(4))
                link(v.memset(carry[0:1, 3, :], 1.0))
                link(v.memset(carry[0:1, 0:2, :], -BIG))
                tt(cut[:, :, 1:], first[:, :, 1:], last_[:, :, :-1], ALU.not_equal)
                link(v.scalar_tensor_tensor(out=gates[:, :, 1:], in0=cut[:, :, :-1], scalar=-BIG,
                                            in1=gate[:, :, :-1], op0=ALU.mult, op1=ALU.add))
                link(v.tensor_copy(new[:, :, 1:], final[:, :, :-1]))
                link(v.tensor_tensor_scan(carry[0:1, 2, :], carry[0:1, 0, :], carry[0:1, 1, :], -BIG, ALU.add,
                                          ALU.max))
                to_col = carry[0:1, 4, :].rearrange("o (c h) -> o h c", h=HEADS)[:, :, way]
                v.scalar_tensor_tensor(out=to_col, in0=cut, scalar=-BIG, in1=run, op0=ALU.mult,
                                       op1=ALU.add).then_inc(carry_ready, 1)
                dve.wait_ge(carry_turned, n + 1)
                link(v.tensor_copy(carry_col[:, n:n + 1], bank(0, 1)))
                link(v.tensor_tensor_scan(to, gaps, data, carry_col[:, n:n + 1], ALU.add, ALU.max))

            scan_carried(0, fw, gap[:, 0:L], e_sc, fw[:, L - 1:L], False)
            scan_carried(1, bw[:, ::-1], gap[:, 1:L + 1][:, ::-1], fw[:, ::-1], bw[:, 0:1], True)
            v.tensor_tensor(e_sc, e_sc, bw, ALU.subtract).then_inc(shifted, 1)
            for n in range(-(-CI // BPB)):
                j0, j1 = n * BPB, min(CI, (n + 1) * BPB)
                dve.wait_ge(exp_turned, n + 1)
                v.tensor_copy(ex_it[:, j0 * CHUNKS:j1 * CHUNKS, :].rearrange("p i h -> p (i h)"),
                              bank(n % BANKS, (j1 - j0) * P)).then_inc(exp_out, 1)
            dve.wait_ge(exp_out, -(-CI // BPB))
            dve.sem_inc(acc_ready, 1)
            for n in range(HOPS):
                message_pass(n)
                if n == 0:
                    dve.wait_ge(targets_ready, 1)
                    dve.wait_ge(cols_in, 16)
                    link(v.tensor_scalar(inv_sum[0:BN], ps[0:BN, EX_SUMS:EX_SUMS + NB * HEADS].rearrange(
                        "p (b h) -> p b h", h=HEADS), 1e-30, None, ALU.max))
                    link(v.reciprocal(inv_sum[0:BN], inv_sum[0:BN]))
                    link(v.tensor_scalar(inv_sum[0:BN], inv_sum[0:BN], 1.0 - ALPHA, None, ALU.mult))
                for k in range(BANKS):
                    b0, b1 = bank_buckets(k)
                    v.tensor_tensor(
                        na[0:BN, b0:b1, :].rearrange("p b (h d) -> p (b h) d", h=HEADS),
                        bank(k, (b1 - b0) * F)[0:BN].rearrange("p (q d) -> p q d", d=HD),
                        inv_sum[0:BN, b0:b1, :].rearrange("p b h -> p (b h)").unsqueeze(2).to_broadcast(
                            [BN, (b1 - b0) * HEADS, HD]), ALU.mult).then_inc(sums_out, 1)
                    dve.wait_ge(sums_out, n * BANKS + k + 1)
                    ins = v.tensor_tensor(na[0:BN, b0:b1], na[0:BN, b0:b1], fe_a[0:BN, b0:b1], ALU.add)
                    if n < HOPS - 1:
                        ins.then_inc(table_ready, 1)
                    else:
                        link(ins)
                if n == HOPS - 2:
                    dve.wait_ge(std_ready, 3)
                    link(v.reciprocal(dinv[0:BN], dinv[0:BN]))
                    v.tensor_tensor(dinv[0:BN], dinv[0:BN], w_deg[0:BN], ALU.mult).then_inc(dinv_ready, 1)
            dve.sem_inc(hops_done, 1)
            tt(na[0:BN], na[0:BN], h0[0:BN], ALU.add)
            dve.wait_ge(x_again, 16)
            tt(h0[0:BN], na[0:BN], x_sb[0:BN], ALU.add)
            tt(h0[0:BN], h0[0:BN], over_nodes(BFF2), ALU.add)
            layernorm(nb_, na, x_sb, 4)
            tt(nb_[0:BN], nb_[0:BN], over_nodes(G2), ALU.mult)
            v.tensor_tensor(nb_[0:BN], nb_[0:BN], over_nodes(B2), ALU.add).then_inc(h_ready, 1)
            for q in range(BANKS):
                b0, b1 = bank_buckets(q)
                dve.wait_ge(ff2_done, q + 1)
                v.tensor_tensor(h0[0:BN, b0:b1, :], h0[0:BN, b0:b1, :],
                                bank(4 + q % 2, (b1 - b0) * F)[0:BN].rearrange("p (b f) -> p b f", f=F),
                                ALU.add).then_inc(ff2_out, 1)
            dve.wait_ge(ff2_out, BANKS)
            layernorm(na, h0, nb_, 5)
            v.tensor_scalar(na[0:BN], na[0:BN], 0.0, None, ALU.max).then_inc(h_ready, 1)
            for k in range(BANKS):
                b0, b1 = bank_buckets(k)
                dve.wait_ge(gcn_done, k + 1)
                v.tensor_tensor(nb_[0:BN, b0:b1, :],
                                bank(k, (b1 - b0) * F)[0:BN].rearrange("p (b f) -> p b f", f=F),
                                dinv[0:BN, b0:b1].unsqueeze(2).to_broadcast([BN, b1 - b0, F]),
                                ALU.mult).then_inc(table_ready, 1)
            dve.wait_ge(dinv_in, 16)

            def add_loops(n, r, u):
                dve.wait_ge(adj_in[u % RING], r * 16 + 16 * (n * (NB // RING) + u // RING + 1))
                own = cells_of(u % RING)[:, :, bass.ds(r * RING + u, 1), :].rearrange("p w b d -> p w (b d)")
                v.tensor_tensor(own, own, ident[0:BN, 0:BN].rearrange("p (w d) -> p w d", d=WN),
                                ALU.add).then_inc(loops_in, 1)

            def scale_bucket(n, r, u):
                dve.wait_ge(conv_done, r * RING + (n * NB + u + 1))
                v.tensor_tensor(turned_q[:, u, :], bank(u, BN), dinv_row[:, bass.ds(r * (RING * BN) + u * BN, BN)],
                                ALU.mult).then_inc(conv_scaled, 1)

            def next_rows(n, r, u):
                dve.wait_ge(next_done, r * RING + (n * NB + u + 1))
                to = (na, nb_)[n % 2][0:BN, bass.ds(r * RING + u, 1), :].rearrange("p b f -> p (b f)")
                if n < LAYERS - 1:
                    ins = v.tensor_scalar(to, bank(NEXT_BANK[u], F)[0:BN], dinv[0:BN, bass.ds(r * RING + u, 1)], None,
                                          ALU.mult)
                else:
                    ins = v.tensor_tensor(to, bank(NEXT_BANK[u], F)[0:BN],
                                          h0[0:BN, bass.ds(r * RING + u, 1), :].rearrange("p b f -> p (b f)"), ALU.add)
                ins.then_inc(next_out, 1)

            for n in range(LAYERS):
                add_loops(n, 0, 0)
                for r0, r1 in ((0, NB // RING - 1), (NB // RING - 1, NB // RING)):
                    with dve.Fori(r0, r1) as r:
                        for u in range(RING):
                            if u < RING - 1 or r0 == 0:
                                add_loops(n, r, u + 1)
                            scale_bucket(n, r, u)
                            if u:
                                next_rows(n, r, u - 1)
                        next_rows(n, r, RING - 1)


_EDGE = {"src": 0, "dst": N_NODES + BN, "edge_weight": 0}


def kernel(**inputs):
    import numpy as np
    import concourse.bacc as bacc
    from concourse.bass_utils import run_bass_kernel_spmd

    nc = bacc.Bacc("TRN2", target_bir_lowering=False, num_devices=1)
    arrays, args = {}, {}
    for name, value in inputs.items():
        x = np.ascontiguousarray(value)
        if name in _EDGE:
            x = np.pad(x, (0, (TILES + 1) * P - N_EDGES), constant_values=_EDGE[name])
        arrays["in_" + name] = x
        args[name] = nc.dram_tensor("in_" + name, x.shape, mybir.dt.from_np(x.dtype), kind="ExternalInput").ap()
    out = nc.dram_tensor("out_0", (N_NODES, F), F32, kind="ExternalOutput").ap()
    gnn_stack(nc, args, out)
    r = run_bass_kernel_spmd(nc, [arrays], core_ids=[0])
    return r.results[0]["out_0"]
```

```python
from contextlib import ExitStack

import concourse.bass as bass
from concourse import mybir

F32 = mybir.dt.float32
BF16 = mybir.dt.bfloat16
I32 = mybir.dt.int32
ALU = mybir.AluOpType
ACT = mybir.ActivationFunctionType
AX = mybir.AxisListType

P = 128
N_NODES = 3125
N_EDGES = 100000
F = 128
BN = 125
NB = N_NODES // BN
HEADS, HD = 8, 16
D_FF = 4 * F
FFC = D_FF // P
HOPS, ALPHA, SLOPE, EPS = 5, 0.15, 0.2, 1e-5
LAYERS = 3
TILES = -(-N_EDGES // P)
CHUNKS = 16
ITEM_COUNT = N_EDGES // P + NB
G = 4
SLOTS = 4
PER_ITER = G * SLOTS
ITEMS = -(-ITEM_COUNT // PER_ITER) * PER_ITER
ITERS = ITEMS // PER_ITER
GROUPS = ITERS * SLOTS
CI = ITEMS // CHUNKS
L = CI * P
GB = -(-GROUPS // P)
KB = -(-ITEMS // P)
BANK = 512
BPB = BANK // F
BANKS = -(-NB // BPB)
BIG = 1e30
PAD_ITEMS = ITEMS - ITEM_COUNT
FULL_ITERS = ITERS - PAD_ITEMS
assert PAD_ITEMS < CI and CI == ITERS
AHEAD = SLOTS - 1
TABLES = HOPS - 1
WN = 5
WINDOWS = N_NODES // WN
WPB = BN // WN
WIN_ITEM_COUNT = N_EDGES // P + WINDOWS
BG = 2
BUILD_HOPS = HOPS - 1
KW = -(-WIN_ITEM_COUNT // P)
WIN_ITEMS = KW * P
BUILD_ITERS = WIN_ITEMS // (BUILD_HOPS * SLOTS * BG)
CELL = NB * WN
ROW = P
WIN_SPARE = SLOTS * BG
RING = 5
assert FULL_ITERS < BUILD_ITERS < ITERS
assert WINDOWS * WN == N_NODES and WPB * WN == BN and BUILD_ITERS * BUILD_HOPS * SLOTS * BG == WIN_ITEMS
NEXT_BANK = (5, 6, 5, 6, 7)
assert NB % RING == 0 and len(NEXT_BANK) == RING
KEY = 32
assert KEY > NB
ROUND = 1.5 * 2.0 ** 23
PROJ_BATCHES = -(-NB // BANKS)
SCANS = 4
EXP_PARTS = 3
RADIX_BITS = 6
RADIX = 1 << RADIX_BITS
SORT_PASSES = 2
assert N_NODES + BN < RADIX ** SORT_PASSES
W_SUMS = (NB + 1) * F
MASKS = 9
assert PER_ITER == CHUNKS and ITEMS % CHUNKS == 0 and CHUNKS * HEADS == P and NB * BN == N_NODES
assert W_SUMS + NB + 1 <= BANKS * BANK and BANKS < 8


def bank_buckets(k):
    return k * BPB, min(NB, (k + 1) * BPB)


PARTS = ((0, (BANKS + 1) // 2), ((BANKS + 1) // 2, BANKS))


def part_buckets(part):
    return part[0] * BPB, min(NB, part[1] * BPB)


def gnn_stack(nc, a, out):
    ctx = ExitStack()
    with ctx:
        def sb(name, shape, dt=F32):
            return ctx.enter_context(nc.sbuf_tensor(name, shape, dt))

        def sem(name):
            return ctx.enter_context(nc.semaphore(name))

        def dram(name, shape, dt=F32):
            return nc.dram_tensor(name, shape, dt, kind="Internal").ap()

        tab_he = dram("tab_he", (N_NODES, 2 * F))
        edge_fe = dram("edge_fe", (P, ITEMS, F))
        tab_f = dram("tab_f", (N_NODES, F))
        srt = {n: dram("sorted_" + n, (TILES, P), d)
               for n, d in (("src", I32), ("dst", I32), ("edge_weight", F32))}
        packed = [dram(f"packed{k}", (TILES * P, 4)) for k in range(SORT_PASSES)]
        item_bucket_d = dram("item_bucket_d", (KB * P,), I32)
        item_key_d = dram("item_key_d", (KB * P, P))
        adj = dram("adj", (P, WINDOWS + WIN_SPARE, ROW))
        win_d = dram("win_d", (WIN_ITEMS,))
        cols_d = dram("cols_d", (P, 3 * WIN_ITEMS))
        dinv_d = dram("dinv_d", (N_NODES,))

        ps = ctx.enter_context(nc.psum_tensor("ps", [P, 8 * BANK], F32))

        def bank(k, n=BANK):
            return ps[:, k * BANK:k * BANK + n]

        small = bank(7)

        h0 = sb("h0", [P, NB, F])
        fe_a = sb("fe_a", [P, NB, F])
        src_it = sb("src_it", [P, KB * P], I32)
        dloc = sb("dloc", [P, KB * P])
        w_it = sb("w_it", [P, KB * P])
        ex_it = sb("ex_it", [P, ITEMS, HEADS])
        bucket_row = sb("bucket_row", [1, KB * P], I32)
        stage = sb("stage", [P, SLOTS, G], I32)
        slide = sb("slide", [P, 2 * P - 1], BF16)
        ident = sb("ident", [P, P])
        iota_p = sb("iota_p", [P, P])
        iota_bn = iota_p[:, 0:BN]
        ones = sb("ones", [P, P])
        zeros = sb("zeros", [1, BANK], BF16)
        raw = sb("raw", [P, WIN_ITEMS])
        w_raw = raw[:, 0:3 * F].rearrange("p (k f) -> p k f", f=F)
        w_qkv = sb("w_qkv", [P, 3 * F])
        ff1_raw = raw[:, 3 * F:3 * F + D_FF].rearrange("p (c f) -> p c f", f=F)
        ff1_t = sb("ff1_t", [P, D_FF])
        ff2_raw = raw[:, 3 * F + D_FF:3 * F + 2 * D_FF]
        ff2_t = sb("ff2_t", [P, FFC, F])
        w_gcn = sb("w_gcn", [P, LAYERS, F])
        b_ff1 = sb("b_ff1", [P, FFC])
        rowvec = sb("rowvec", [P, 6, F])
        G1, B1, G2, B2, BFF2, ATTN = range(6)
        b_gcn = sb("b_gcn", [P, LAYERS])
        step5 = sb("step5", [P, WPB])
        deg_n = sb("deg_n", [P, NB])
        win_it = sb("win_it", [P, KW])
        win_f = sb("win_f", [P, 2, KW])
        win_t = sb("win_t", [P, KW], I32)
        target = sb("target", [1, WIN_ITEMS], I32)
        w_deg = sb("w_deg", [P, NB])
        log_deg = sb("log_deg", [P, NB])
        dinv = sb("dinv", [P, NB])
        stat = sb("stat", [P, 4, NB])
        thr = sb("thr", [P, 3, NB + 1])
        disorder = sb("disorder", [P, 1], I32)
        thr_i = sb("thr_i", [P, NB + 1], I32)
        item_f = sb("item_f", [P, 4, KB])
        item_t = sb("item_t", [P, KB], I32)
        item_b = sb("item_b", [P, KB], I32)
        ge = sb("ge", [P, KB, NB])
        grp_i = sb("grp_i", [P, 2, GB * G], I32)
        grp_f = sb("grp_f", [P, 2, GB * G])
        grp_hot = sb("grp_hot", [P, GB * G, NB])
        ends = sb("ends", [P, 4])
        rows = sb("rows", [1, 4, HEADS, CHUNKS])
        carry = sb("carry", [1, 5, HEADS * CHUNKS])
        carry_col = sb("carry_col", [P, 4])

        U = sb("U", [P, 3 * L])
        gap = sb("gap", [P, L + 2], BF16)
        e_sc, fw, bw = (U[:, k * L:(k + 1) * L] for k in range(3))
        KEY_MAIN = L - P
        key = U[:, 0:KEY_MAIN]
        key_last = sb("key_last", [P, P])
        at = [0]

        def part(n):
            at[0] += n
            assert at[0] <= 3 * L
            return U[:, at[0] - n:at[0]]

        node = [part(n * F).rearrange("p (b f) -> p b f", f=F) for n in (NB, NB, NB + 1)]
        x_sb, na, nb_pad = node
        nb_ = nb_pad[:, 0:NB]
        turned_flat = part(NB * BN)
        hT = turned_flat
        hot_t = turned_flat[0:BN, 0:2 * G * P].rearrange("p (s g e) -> p s g e", s=2, g=G)
        ga_flat = part(SLOTS * G * 2 * F)
        ga_wide = ga_flat.rearrange("p (s g f) -> p s g f", s=SLOTS, g=G)
        ga = ga_flat.rearrange("p (s n) -> p s n", s=SLOTS)[:, :, 0:G * F].rearrange("p s (g f) -> p s g f", g=G)
        ffa = ga_flat[:, 0:FFC * BPB * BN].rearrange("p (c n) -> p c n", c=FFC)
        hot_flat = part(SLOTS * G * BN)
        hot = hot_flat.rearrange("p (s g f) -> p s g f", s=SLOTS, g=G)
        hot_b = hot_flat[:, 0:SLOTS * G * BN // 2].bitcast(BF16).rearrange("p (s f g) -> p s f g", s=SLOTS, g=G)
        iota_g = hT[:, 0:BN * G // 2].bitcast(BF16).rearrange("p (f g) -> p f g", g=G)
        dloc_b = hT[:, BN * G // 2:BN * G // 2 + KB * P // 2].bitcast(BF16)
        item_deg = ex_it[:].rearrange("p i h -> p (i h)")[:, 0:GB * BN * G].rearrange("p (k n g) -> p k n g", k=GB, g=G)
        dst_all = ga_flat[:, 0:TILES].bitcast(I32)
        dst_next = hT[:, TILES:2 * TILES].bitcast(I32)
        dst_allf = hT[:, 0:TILES]
        dst_allw = hT[:, 2 * TILES:3 * TILES]
        row_raw = [node[k].rearrange("p b f -> p (b f)")[:, 0:KB * P].rearrange("p (k e) -> p k e", e=P)
                   for k in range(3)]
        row_i = [row_raw[0].bitcast(I32), row_raw[1].bitcast(I32), row_raw[2]]
        row_f = [node[k].rearrange("p b f -> p (b f)")[:, KB * P:2 * KB * P].rearrange("p (k e) -> p k e", e=P)
                 for k in range(3)]

        sort_at = [0]

        def sort_part(*shape):
            n = shape[0] if len(shape) == 1 else shape[0] * shape[1]
            sort_at[0] += n
            assert sort_at[0] <= 2 * NB * F
            v = U[:, sort_at[0] - n:sort_at[0]]
            return v if len(shape) == 1 else v.rearrange("p (t c) -> p t c", c=shape[1])

        edges = sort_part(TILES, 4)
        s_raw = sort_part(TILES)
        s_digit = sort_part(TILES)
        s_hot = sort_part(RADIX)
        s_tmp = sort_part(RADIX)
        s_base = sort_part(RADIX)
        s_count = sort_part(RADIX)
        s_iota = sort_part(RADIX)
        s_rank = sort_part(4)
        s_move = sort_part(4)
        s_lower = sort_part(P)

        win_rows = [U[:, k * WIN_ITEMS:(k + 1) * WIN_ITEMS] for k in range(3)] + [raw[:]]
        win_tmp = [U[:, 3 * WIN_ITEMS + k * WINDOWS:3 * WIN_ITEMS + (k + 1) * WINDOWS] for k in range(3)]
        assert 3 * WIN_ITEMS + 3 * WINDOWS <= 2 * NB * F and 3 * F + 2 * D_FF <= WIN_ITEMS
        cols_at = 2 * NB * F
        assert 4 * WIN_ITEMS <= (NB + 1) * F + NB * BN
        win_p, win_b, win_dd, win_same = (U[:, cols_at + k * WIN_ITEMS:cols_at + (k + 1) * WIN_ITEMS] for k in range(4))
        win_w = raw
        wrow = na.rearrange("p b f -> p (b f)")[:, 0:WIN_ITEMS]
        wtmp = na.rearrange("p b f -> p (b f)")[0:1, WIN_ITEMS:2 * WIN_ITEMS]
        gap_f = gap[:].bitcast(F32)
        gap_at = [0]

        def gap_part(s_, j, n):
            gap_at[0] += s_ * j * n
            return gap_f[:, gap_at[0] - s_ * j * n:gap_at[0]].rearrange("p (s j n) -> p s j n", s=s_, j=j)

        hot_p = gap_part(2, BG, P)
        prod = gap_part(2, BG, CELL)
        win_acc = gap_part(SLOTS, BG, ROW)
        hot_bk = gap_part(2, BG, NB)
        hot_d = gap_part(2, BG, WN)
        spare0 = gap_part(1, 1, WIN_SPARE)[0:1, 0, 0, :]
        dinv_row = gap_f[:, 0:N_NODES]
        wide = WPB * ROW
        ex_flat = ex_it[:].rearrange("p i h -> p (i h)")
        ring = [ex_flat[:, 0:wide], ex_flat[:, wide:2 * wide], fe_a[:].rearrange("p b f -> p (b f)")[:, 0:wide],
                x_sb.rearrange("p b f -> p (b f)")[:, 0:wide], ga_flat[:, 0:wide]]

        def cells_of(u):
            return ring[u][0:BN].rearrange("p (w n) -> p w n", n=ROW)[:, :, 0:CELL].rearrange(
                "p w (b d) -> p w b d", b=NB)

        turned_q = hot_flat[:, 0:RING * BN].rearrange("p (u n) -> p u n", n=BN)

        win_counted = sem("win_counted")
        win_summed = sem("win_summed")
        win_known = sem("win_known")
        win_rows_in = sem("win_rows_in")
        win_rows_ready = sem("win_rows_ready")
        win_turned = sem("win_turned")
        win_cols = sem("win_cols")
        win_out = sem("win_out")
        wrow_in = sem("wrow_in")
        cols_in = sem("cols_in")
        targets_ready = sem("targets_ready")
        pool_link = sem("pool_link")
        prod_ready = sem("prod_ready")
        cell_sums = sem("cell_sums")
        acc_ready = sem("acc_ready")
        acc_out = [sem(f"acc_out{k}") for k in range(SLOTS)]
        build_link = sem("build_link")
        hops_done = sem("hops_done")
        sum_link = sem("sum_link")
        dinv_ready = sem("dinv_ready")
        dinv_out = sem("dinv_out")
        dinv_in = sem("dinv_in")
        adj_in = [sem(f"adj_in{u}") for u in range(RING)]
        loops_in = sem("loops_in")
        conv_done = sem("conv_done")
        conv_scaled = sem("conv_scaled")
        conv_out = sem("conv_out")
        next_done = sem("next_done")
        next_out = sem("next_out")
        consts_in = sem("consts_in")
        dst_in = sem("dst_in")
        x_in = sem("x_in")
        masks_set = sem("masks_set")
        dve_link = sem("dve_link")
        counted = sem("counted")
        summed = sem("summed")
        tiles_known = sem("tiles_known")
        rows_in = sem("rows_in")
        rows_ready = sem("rows_ready")
        rows_turned = sem("rows_turned")
        items_ready = sem("items_ready")
        bucket_out = sem("bucket_out")
        bucket_in = sem("bucket_in")
        key_out = sem("key_out")
        key_in = sem("key_in")
        key_free = sem("key_free")
        weights_turned = sem("weights_turned")
        weights_ready = sem("weights_ready")
        staged = sem("staged")
        hots_ready = sem("hots_ready")
        hots_used = sem("hots_used")
        item_degs = sem("item_degs")
        item_degs_out = sem("item_degs_out")
        degs_ready = sem("degs_ready")
        hot_turned = sem("hot_turned")
        hot_t_out = sem("hot_t_out")
        tails_ready = sem("tails_ready")
        scaled = sem("scaled")
        stored = [sem(f"stored{k}") for k in range(SLOTS)]
        loaded = [sem(f"loaded{k}") for k in range(SLOTS)]
        edges_copied = sem("edges_copied")
        edges_sorted = sem("edges_sorted")
        order_known = sem("order_known")
        sort_masks = sem("sort_masks")
        sort_in = sem("sort_in")
        sort_counted = sem("sort_counted")
        sort_summed = sem("sort_summed")
        sort_hot = sem("sort_hot")
        sort_prefix = sem("sort_prefix")
        sort_link = sem("sort_link")
        sort_ranked = sem("sort_ranked")
        sort_begun = sem("sort_begun")
        sort_moved = sem("sort_moved")
        sort_split = sem("sort_split")
        begun = sem("begun")
        got = [sem(f"got{k}") for k in range(SLOTS)]
        zeros_set = sem("zeros_set")
        slide_set = sem("slide_set")
        scores_done = sem("scores_done")
        tails_out = sem("tails_out")
        sums_out = sem("sums_out")
        gcn_done = sem("gcn_done")
        msgs_ready = sem("msgs_ready")
        groups_done = sem("groups_done")
        step_link = sem("step_link")
        var_ready = sem("var_ready")
        std_ready = sem("std_ready")
        logs_ready = sem("logs_ready")
        h_ready = sem("h_ready")
        turned = sem("turned")
        turned_out = sem("turned_out")
        proj_done = sem("proj_done")
        proj_out = sem("proj_out")
        table_ready = sem("table_ready")
        table_out = sem("table_out")
        score_turned = sem("score_turned")
        score_out = sem("score_out")
        ends_ready = sem("ends_ready")
        ends_turned = sem("ends_turned")
        carry_ready = sem("carry_ready")
        carry_turned = sem("carry_turned")
        shifted = sem("shifted")
        exps_ready = sem("exps_ready")
        shares_ready = sem("shares_ready")
        exp_turned = sem("exp_turned")
        exp_out = sem("exp_out")
        ff1_done = sem("ff1_done")
        ff1_out = sem("ff1_out")
        ff2_done = sem("ff2_done")
        ff2_out = sem("ff2_out")
        x_again = sem("x_again")
        x_used = sem("x_used")
        y_out = sem("y_out")

        def staged_before(s):
            return GROUPS + AHEAD + (s - 1) * GROUPS

        def got_at(s, r, k, r0):
            if k < SLOTS - 1:
                return r * (16 * G) + 16 * G * (ITERS * s + 1)
            skipped = PAD_ITEMS * s
            if r0 < FULL_ITERS:
                return r * (16 * G) + 16 * (G * (ITERS * s + 1) - skipped)
            return r * (16 * (G - 1)) + 16 * (G * ITERS * s - skipped + FULL_ITERS + G - 1)

        def cut(*at):
            return list(zip(at[:-1], at[1:]))

        def msgs_before(s):
            return GROUPS + 1 + 2 * s * GROUPS

        def item_of(r, k, ahead=0):
            return r * PER_ITER + (k + ahead) * G

        def win_item(s, r, k, j=0):
            return r * (SLOTS * BG) + ((s - 1) * BUILD_ITERS * SLOTS * BG + k * BG + j)

        def steps_before(s):
            return (s - 1) * BUILD_ITERS * SLOTS

        WIN_COUNT_AT, WIN_GATHER_AT, WIN_ROWS_AT, WIN_TURN_AT, WIN_OUT_AT = 8, 14, 22, 26, 31
        KEY_LOAD_AT, KEY_AT, KEY_AT2 = 33, 36, 39

        WHY_BOUNDED = "a count of the NB bounds at or below the item"

        def buckets_of(pe, i):
            _, b = nc.values_load_multi_w_load_instructions(bucket_row[0:1, bass.ds(i, G)], engines=(pe.engine,),
                                                            min_val=0, max_val=NB,
                                                            skip_runtime_bounds_check_because=WHY_BOUNDED)
            return b

        def proj_view(n, col):
            return ps[0:BN, 0:n * BANK].rearrange("p (k n) -> p k n", n=BANK)[:, :, col * F:(col + 1) * F]

        def nodes_of(table):
            return table.rearrange("(b p) f -> p b f", p=BN)

        LOADS = 3 + 3 + LAYERS + 6 + LAYERS

        block = ctx.enter_context(nc.Block())

        @block.sync
        def _(sp):
            in_rows = {n: a[n][0:TILES * P].rearrange("(p t) -> p t", p=P) for n in srt}
            sp.dma_start(dst_all, in_rows["dst"]).then_inc(dst_in, 16)
            sp.dma_start(dst_next, a["dst"][1:TILES * P + 1].rearrange("(p t) -> p t", p=P)).then_inc(dst_in, 16)
            for n in srt:
                sp.dma_start(srt[n].rearrange("(a t) e -> a (t e)", a=2),
                             a[n][0:TILES * P].rearrange("(a n) -> a n", a=2)).then_inc(edges_copied, 16)
            sp.dma_start(h0[0:BN], nodes_of(a["x"])).then_inc(x_in, 16)
            loads = [(w_raw[:, k, :], a[n]) for k, n in enumerate(("L0_gnn_W_head", "L0_gnn_W_tail", "L0_gnn_W_ent"))]
            loads += [(ff1_raw[:], a["L0_gnn_W_ff1"].rearrange("(c p) f -> p c f", p=P)),
                      (ff2_raw[:], a["L0_gnn_W_ff2"]),
                      (b_ff1[:], a["L0_gnn_b_ff1"].rearrange("(c p) -> p c", p=P))]
            loads += [(w_gcn[:, k, :], a[f"L1_gnn_W{k}"]) for k in range(LAYERS)]
            for k, n in ((G1, "L0_gnn_ln1_g"), (B1, "L0_gnn_ln1_b"), (G2, "L0_gnn_ln2_g"), (B2, "L0_gnn_ln2_b"),
                         (BFF2, "L0_gnn_b_ff2")):
                loads.append((rowvec[:, k, :], a[n].partition_broadcast(P)))
            loads.append((rowvec[:, ATTN, :], a["L0_gnn_attn"].rearrange("a h d -> (a h d)").partition_broadcast(P)))
            loads += [(b_gcn[:, k:k + 1], a[f"L1_gnn_b{k}"].rearrange("(p o) -> p o", o=1)) for k in range(LAYERS)]
            assert len(loads) == LOADS
            for to, of in loads:
                sp.dma_start(to, of, allow_slow_non_contiguous=True).then_inc(consts_in, 16)
            sp.wait_ge(order_known, 1)
            sp.wait_ge(edges_copied, 16 * 3)
            with sp.If(sp.value_load(disorder[0:1, 0:1], min_val=0, max_val=TILES * P) != 0):
                sp.dma_start(s_raw.bitcast(I32), in_rows["src"]).then_inc(sort_in, 16)
                sp.dma_start(s_digit, in_rows["edge_weight"]).then_inc(sort_in, 16)
                for n in range(SORT_PASSES):
                    sp.wait_ge(sort_moved, 16 * TILES * (n + 1))
                    sp.dma_start(edges, packed[n].rearrange("(p t) c -> p t c", p=P)).then_inc(sort_in, 16)
                sp.wait_ge(sort_split, 1)
                for n, v in (("src", s_raw.bitcast(I32)), ("dst", s_digit.bitcast(I32)), ("edge_weight", dst_allw)):
                    sp.dma_start(srt[n].rearrange("t e -> (t e)").rearrange("(p t) -> p t", p=P),
                                 v).then_inc(edges_copied, 16)
                sp.wait_ge(edges_copied, 16 * 6)
            sp.sem_inc(edges_sorted, 1)
            sp.wait_ge(tiles_known, 1)
            sp.dma_start(item_bucket_d.rearrange("(k p) -> p k", p=P), item_b[:],
                         allow_slow_non_contiguous=True).then_inc(bucket_out, 16)
            sp.wait_ge(bucket_out, 16)
            sp.dma_start(bucket_row[:], item_bucket_d.rearrange("(a n) -> a n", a=1)).then_inc(bucket_in, 16)
            sp.wait_ge(rows_ready, 3)
            sp.dma_start(item_key_d.rearrange("(k p) e -> p k e", p=P), row_f[1]).then_inc(key_out, 16)
            sp.sem_inc(stored[SLOTS - 1], 16)
            sp.wait_ge(table_ready, 1)
            sp.dma_start(nodes_of(tab_he[:, 0:F]), na[0:BN]).then_inc(table_out, 16)
            sp.dma_start(nodes_of(tab_he[:, F:2 * F]), x_sb[0:BN]).then_inc(table_out, 16)
            for r0, r1 in cut(0, WIN_OUT_AT, KEY_LOAD_AT, FULL_ITERS, ITERS):
                if r0 == WIN_OUT_AT:
                    sp.wait_ge(win_known, 1)
                    sp.dma_start(win_d.rearrange("(k p) -> p k", p=P), win_f[:, 0, :],
                                 allow_slow_non_contiguous=True).then_inc(win_out, 16)
                    sp.wait_ge(win_cols, 4)
                    sp.dma_start(cols_d, U[:, 0:3 * WIN_ITEMS]).then_inc(win_out, 16)
                if r0 == KEY_LOAD_AT:
                    sp.wait_ge(key_out, 16)
                    sp.wait_ge(win_out, 32)
                    chunks = item_key_d.rearrange("(r c) e -> c r e", c=CHUNKS)
                    for c in range(CHUNKS):
                        sp.dma_start(key[c * HEADS:(c + 1) * HEADS, :].rearrange("p (r e) -> p r e", e=P),
                                     chunks[c, 0:CI - 1].partition_broadcast(HEADS)).then_inc(key_in, 16)
                    for c in range(CHUNKS):
                        sp.dma_start(key_last[c * HEADS:(c + 1) * HEADS, :],
                                     chunks[c, CI - 1].partition_broadcast(HEADS)).then_inc(key_in, 16)
                with sp.Fori(r0, r1) as r:
                    for k in range(SLOTS):
                        sp.wait_ge(got[k], got_at(0, r, k, r0))
                        sp.dma_start(edge_fe[:, bass.ds(item_of(r, k), G), :],
                                     ga_wide[:, k, :, F:2 * F]).then_inc(stored[k], 16)
            sp.wait_ge(exp_out, -(-CI // BPB))
            sp.dma_start(x_sb[0:BN], nodes_of(a["x"])).then_inc(x_again, 16)
            sp.wait_ge(win_out, 32)
            sp.dma_start(wrow, win_d.partition_broadcast(P)).then_inc(wrow_in, 16)
            sp.dma_start(U[:, cols_at:cols_at + 3 * WIN_ITEMS], cols_d).then_inc(cols_in, 16)
            for k in range(SLOTS):
                sp.wait_ge(stored[k], 16 * (ITERS + (k == SLOTS - 1)))
            with sp.Fori(0, ITERS) as r:
                for k in range(SLOTS):
                    sp.wait_ge(groups_done, r * SLOTS + (k + 1))
                    sp.dma_start(ga[:, k], edge_fe[:, bass.ds(item_of(r, k), G), :]).then_inc(loaded[k], 16)
            for k in range(SLOTS):
                sp.sem_inc(acc_out[k], 16 * BG)
            sp.wait_ge(targets_ready, 1)
            for n in range(HOPS):
                if n:
                    with sp.Fori(0, BUILD_ITERS) as r:
                        for k in range(SLOTS):
                            sp.wait_ge(acc_ready, r * SLOTS + (steps_before(n) + k + 2))
                            for j in range(BG):
                                to = sp.value_load(target[0:1, bass.ds(win_item(n, r, k, j), 1)], min_val=0,
                                                   max_val=WINDOWS + WIN_SPARE - 1)
                                sp.dma_start(adj[:, bass.ds(to, 1), :].rearrange("p w c -> p (w c)"),
                                             win_acc[:, k, j, :]).then_inc(acc_out[k], 16)
                if n < HOPS - 1:
                    for k in range(BANKS):
                        b0, b1 = bank_buckets(k)
                        sp.wait_ge(sums_out, n * BANKS + k + 1)
                        sp.dma_start(nodes_of(tab_f)[:, b0:b1], na[0:BN, b0:b1]).then_inc(table_out, 16)
            for k in range(SLOTS):
                sp.wait_ge(acc_out[k], 16 * BG * (BUILD_HOPS * BUILD_ITERS + 1))
            sp.wait_ge(dinv_ready, 1)
            sp.dma_start(dinv_d.rearrange("(b p) -> p b", p=BN), dinv[0:BN],
                         allow_slow_non_contiguous=True).then_inc(dinv_out, 16)
            buckets_d = adj[:, 0:WINDOWS, :].rearrange("p (q w) c -> p q (w c)", q=NB)

            def load_bucket(u, q):
                sp.dma_start(ring[u], buckets_d[:, bass.ds(q, 1), :].rearrange("p q c -> p (q c)")
                             ).then_inc(adj_in[u], 16)

            sp.wait_ge(hops_done, 1)
            for u in range(RING):
                if u == 3:
                    sp.wait_ge(dinv_out, 16)
                    sp.dma_start(dinv_row, dinv_d.partition_broadcast(P)).then_inc(dinv_in, 16)
                    sp.wait_ge(x_used, 1)
                if u == 4:
                    sp.wait_ge(ff2_done, BANKS)
                load_bucket(u, u)
            for n in range(LAYERS):
                last = n == LAYERS - 1
                if not last:
                    passes = [(0, NB // RING - 1, RING), (NB // RING - 1, NB // RING, RING - NB)]
                else:
                    passes = [(0, NB // RING - 1, RING)]
                for r0, r1, ahead in passes:
                    with sp.Fori(r0, r1) as r:
                        for u in range(RING):
                            sp.wait_ge(conv_done, r * RING + (n * NB + u + 1))
                            load_bucket(u, r * RING + (u + ahead))
            for k in range(BANKS):
                b0, b1 = bank_buckets(k)
                sp.wait_ge(next_out, (LAYERS - 1) * NB + b1)
                sp.dma_start(nodes_of(out)[:, b0:b1], na[0:BN, b0:b1]).then_inc(y_out, 16)
            sp.wait_ge(y_out, 16 * BANKS)
            sp.wait_ge(table_out, 16 * (2 + TABLES * BANKS))

        @block.gpsimd
        def _(pool):
            pool.memset(ident[:], 0.0).then_inc(masks_set, 1)
            pool.wait_ge(masks_set, 1)
            pool.affine_select(out=ident[:], in_=ident[:], compare_op=ALU.not_equal, fill=1.0, base=0,
                               pattern=[[-1, P]], channel_multiplier=1).then_inc(masks_set, 1)
            pool.iota(iota_p[:], pattern=[[1, P]], base=0, channel_multiplier=0,
                      allow_small_or_imprecise_dtypes=True).then_inc(masks_set, 1)
            pool.iota(item_t[:], pattern=[[P, KB]], base=0, channel_multiplier=1).then_inc(masks_set, 1)
            pool.iota(thr[:, 0, :], pattern=[[1, NB + 1]], base=1, channel_multiplier=0,
                      allow_small_or_imprecise_dtypes=True).then_inc(masks_set, 1)
            pool.iota(step5[:], pattern=[[WN, WPB]], base=WN - 1, channel_multiplier=-1,
                      allow_small_or_imprecise_dtypes=True).then_inc(masks_set, 1)
            pool.iota(win_it[:], pattern=[[P, KW]], base=0, channel_multiplier=1,
                      allow_small_or_imprecise_dtypes=True).then_inc(masks_set, 1)
            pool.iota(grp_i[:, 0, :].rearrange("p (k g) -> p k g", g=G), pattern=[[G * P, GB], [1, G]],
                      base=G * (P - 1), channel_multiplier=-G).then_inc(masks_set, 1)
            pool.memset(slide[:], 0.0).then_inc(masks_set, 1)
            pool.wait_ge(masks_set, MASKS)
            pool.memset(slide[:, P - 1:P], 1.0).then_inc(slide_set, 1)
            pool.wait_ge(order_known, 1)
            with pool.If(pool.value_load(disorder[0:1, 0:1], min_val=0, max_val=TILES * P) != 0):
                pool.iota(s_iota, pattern=[[1, RADIX]], base=0, channel_multiplier=0,
                          allow_small_or_imprecise_dtypes=True).then_inc(sort_masks, 1)
                pool.memset(s_lower, 1.0).then_inc(sort_masks, 1)
                pool.wait_ge(sort_masks, 2)
                pool.affine_select(out=s_lower, in_=s_lower, compare_op=ALU.is_gt, fill=0.0, base=0,
                                   pattern=[[1, P]], channel_multiplier=-1).then_inc(sort_masks, 1)
                for n in range(SORT_PASSES):
                    with pool.Fori(0, TILES) as r:
                        pool.wait_ge(sort_ranked, r + (n * TILES + 1))
                        pool.sem_inc(sort_begun, 1)
                        pool.indirect_dma_start(packed[n], bass.IndirectOffsetOnAxis(
                            ap=s_rank[:, 3:4].bitcast(I32), axis=0), s_move, None).then_inc(sort_moved, 16)
                pool.wait_ge(sort_moved, 16 * TILES * SORT_PASSES)
            pool.wait_ge(edges_sorted, 1)
            pool.wait_ge(tiles_known, 1)
            for k in range(KB):
                for name, to in zip(("src", "dst", "edge_weight"), row_i):
                    pool.indirect_dma_start(to[:, k, :], None, srt[name],
                                            bass.IndirectOffsetOnAxis(ap=item_t[:, k:k + 1], axis=0)).then_inc(rows_in, 16)

            def gather_pass(before, table, to, r0=0, r1=ITERS):
                with pool.Fori(r0, r1) as r:
                    for k in range(SLOTS):
                        pool.wait_ge(staged, r * SLOTS + (before + k + 1))
                        pool.sem_inc(begun, 1)
                        for j in range(G - (k == SLOTS - 1 and r0 >= FULL_ITERS)):
                            pool.indirect_dma_start(
                                to[:, k, j, :], None, table,
                                bass.IndirectOffsetOnAxis(ap=stage[:, k, j:j + 1], axis=0)).then_inc(got[k], 16)

            pool.wait_ge(table_out, 2 * 16)
            gather_pass(0, tab_he, ga_wide, 0, WIN_GATHER_AT)
            pool.wait_ge(win_known, 1)
            for k in range(KW):
                for name, to in zip(("src", "dst", "edge_weight"), (win_rows[0], win_rows[2], win_rows[3])):
                    to = to[:, k * P:(k + 1) * P]
                    pool.indirect_dma_start(to if name == "edge_weight" else to.bitcast(I32), None, srt[name],
                                            bass.IndirectOffsetOnAxis(ap=win_t[:, k:k + 1], axis=0)
                                            ).then_inc(win_rows_in, 16)
            for r0, r1 in cut(WIN_GATHER_AT, FULL_ITERS, ITERS):
                gather_pass(0, tab_he, ga_wide, r0, r1)
            links = [0]

            def chain(ins):
                links[0] += 1
                ins.then_inc(pool_link, 1)
                pool.wait_ge(pool_link, links[0])

            g = nc.gpsimd
            pool.wait_ge(wrow_in, 16)
            pool.wait_ge(exp_out, -(-CI // BPB))
            chain(g.memset(win_acc, 0.0))
            chain(g.memset(win_same[:, 0:1], 0.0))
            chain(g.tensor_tensor(win_same[:, 1:], wrow[:, :-1], wrow[:, 1:], ALU.subtract))
            chain(g.tensor_tensor(win_same[:, 1:], win_same[:, 1:],
                                  ones[:, 0:1].to_broadcast([P, WIN_ITEMS - 1]), ALU.add))
            chain(g.iota(spare0, pattern=[[1, WIN_SPARE]], base=WINDOWS, channel_multiplier=0,
                         allow_small_or_imprecise_dtypes=True))
            spares = spare0.unsqueeze(1).to_broadcast([1, WIN_ITEMS // WIN_SPARE, WIN_SPARE])
            of_steps = [x_.rearrange("o (i s) -> o i s", s=WIN_SPARE) for x_ in (wrow[0:1], wtmp, target[:])]
            chain(g.tensor_tensor(of_steps[1], of_steps[0], spares, ALU.subtract))
            chain(g.tensor_tensor(wrow[0:1, :-1], win_same[0:1, 1:], wtmp[:, :-1], ALU.mult))
            chain(g.tensor_copy(wrow[0:1, WIN_ITEMS - 1:], wtmp[:, WIN_ITEMS - 1:]))
            chain(g.tensor_tensor(wtmp, wtmp, wrow[0:1], ALU.subtract))
            chain(g.tensor_tensor(of_steps[1], of_steps[1], spares, ALU.add))
            g.tensor_copy(target[:], wtmp).then_inc(targets_ready, 1)
            for s in range(1, HOPS):
                pool.wait_ge(table_out, 16 * (2 + s * BANKS))
                for r0, r1 in cut(0, FULL_ITERS, ITERS):
                    gather_pass(staged_before(s), tab_f, ga, r0, r1)

        @block.scalar
        def _(act):
            def std(n, part=(0, BANKS)):
                c0, c1 = part_buckets(part)
                act.wait_ge(var_ready, n)
                nc.scalar.activation(stat[0:BN, 2, c0:c1], stat[0:BN, 1, c0:c1], ACT.Sqrt).then_inc(std_ready, 1)

            def turn_out(n, part):
                for k in range(*part):
                    b0, b1 = bank_buckets(k)
                    act.wait_ge(turned, n * BANKS + k + 1)
                    nc.scalar.copy(hT[:, b0 * BN:b1 * BN], bank(k, (b1 - b0) * BN)).then_inc(turned_out, 1)

            def stage_group(r, k, ahead=0):
                to = (k + ahead) % SLOTS
                nc.scalar.copy(stage[:, to, :], src_it[:, bass.ds(item_of(r, k, ahead), G)]).then_inc(staged, 1)

            def stage_pass(s):
                with act.Fori(0, ITERS) as r:
                    for k in range(SLOTS):
                        act.wait_ge(groups_done, r * SLOTS + (s * GROUPS + k + 1))
                        stage_group(r, k)

            std(1)
            for n, part_ in enumerate(PARTS):
                std(2 + n, part_)
                turn_out(0, part_)
            for q in range(PROJ_BATCHES):
                b0, b1 = q * BANKS, min(NB, (q + 1) * BANKS)
                act.wait_ge(proj_done, q + 1)
                for col, to in ((0, na), (2, x_sb)):
                    nc.scalar.copy(to[0:BN, b0:b1, :], proj_view(b1 - b0, col)).then_inc(proj_out, 1)
            act.wait_ge(items_ready, 1)
            for k in range(AHEAD):
                stage_group(0, k)
            act.wait_ge(item_degs, 1)
            nc.scalar.copy(item_deg.rearrange("p k n g -> p k (n g)"), ps[:, 0:GB * BANK].rearrange(
                "p (k n) -> p k n", n=BANK)[:, :, 0:BN * G]).then_inc(item_degs_out, 1)
            act.wait_ge(logs_ready, 1)
            nc.scalar.activation(log_deg[0:BN], log_deg[0:BN], ACT.Ln).then_inc(logs_ready, 1)
            def score_groups(r0, r1):
                with act.Fori(r0, r1) as r:
                    for k in range(SLOTS):
                        act.wait_ge(hot_turned, r * SLOTS + (k + 1))
                        nc.scalar.copy(hot_t[:, k % 2], bank(k % 2)[0:BN].rearrange("p (g e) -> p g e", g=G)
                                       ).then_inc(hot_t_out, 1)
                        act.wait_ge(scores_done, r * SLOTS + (SLOTS + k))
                        act.wait_ge(stored[(k + AHEAD) % SLOTS], r * 16 + 16)
                        stage_group(r, k, AHEAD)

            score_groups(0, WIN_TURN_AT)
            for n in range(4):
                act.wait_ge(win_turned, n + 1)
                nc.scalar.copy(win_rows[n], ps[:, 4 * BANK:4 * BANK + WIN_ITEMS]).then_inc(win_cols, 1)
            score_groups(WIN_TURN_AT, ITERS)
            act.wait_ge(key_free, 1)
            act.wait_ge(win_out, 32)
            for n in range(-(-CI // BPB)):
                j0, j1 = n * BPB, min(CI, (n + 1) * BPB)
                act.wait_ge(score_turned, n + 1)
                nc.scalar.copy(e_sc[:, j0 * P:j1 * P], bank(n % BANKS, (j1 - j0) * P)).then_inc(score_out, 1)
            for n in range(EXP_PARTS):
                act.wait_ge(shifted, n + 1)
                w = L // EXP_PARTS
                nc.scalar.activation(e_sc[:, n * w:(n + 1) * w], e_sc[:, n * w:(n + 1) * w],
                                     ACT.Exp).then_inc(exps_ready, 1)
            act.wait_ge(exp_out, -(-CI // BPB))
            for s in range(1, HOPS):
                stage_pass(s)
                if s == 1:
                    act.wait_ge(var_ready, 4)
                    nc.scalar.activation(dinv[0:BN], dinv[0:BN], ACT.Sqrt).then_inc(std_ready, 1)
            std(5, PARTS[0])
            turn_out(1, PARTS[0])
            std(6, PARTS[1])
            for part_ in PARTS:
                if part_[0]:
                    turn_out(1, part_)
                for q in range(*part_):
                    b0, b1 = bank_buckets(q)
                    n = (b1 - b0) * BN
                    if q:
                        act.wait_ge(ff2_done, q)
                    for c in range(FFC):
                        act.wait_ge(ff1_done, q * FFC + c + 1)
                        nc.scalar.activation(ffa[:, c, 0:n], bank(c, n), ACT.Relu,
                                             bias=b_ff1[:, c:c + 1]).then_inc(ff1_out, 1)
            for n, part_ in enumerate(PARTS):
                std(7 + n, part_)
                turn_out(2, part_)
            for n in range(LAYERS):
                with act.Fori(0, NB // RING) as r:
                    for u in range(RING):
                        act.wait_ge(conv_scaled, r * RING + (n * NB + u + 1))
                        nc.scalar.activation(turned_q[:, u, :], turned_q[:, u, :],
                                             ACT.Relu if n < LAYERS - 1 else ACT.Identity,
                                             bias=b_gcn[:, n:n + 1]).then_inc(conv_out, 1)

        @block.tensor
        def _(pe):
            def clear(banks):
                for k in banks:
                    nc.tensor.matmul(bank(k), zeros[:, 0:P], zeros[:], start=True, stop=False, skip_group_check=True)

            def sum_pass(s):
                for r0, r1 in ((0, BUILD_ITERS), (BUILD_ITERS, ITERS)) if s else ((0, ITERS),):
                    sum_groups(s, r0, r1, s > 0 and r0 == 0)

            def sum_groups(s, r0, r1, building):
                with pe.Fori(r0, r1) as r:
                    for k in range(SLOTS):
                        if building:
                            pe.wait_ge(prod_ready, r * SLOTS + (steps_before(s) + k + 1))
                            pe.wait_ge(acc_ready, r * SLOTS + (steps_before(s) + k + 1))
                            for j in range(BG):
                                mm = nc.tensor.matmul(ps[:, 7 * BANK + j * CELL:7 * BANK + (j + 1) * CELL],
                                                      hot_p[:, k % 2, j, :], prod[:, k % 2, j, :],
                                                      start=True, stop=True)
                            mm.then_inc(cell_sums, 1)
                        buckets = buckets_of(pe, item_of(r, k))
                        pe.wait_ge(msgs_ready, r * (2 * SLOTS) + (msgs_before(s) + 2 * (k + 1)))
                        for j, b in enumerate(buckets):
                            if s == 1:
                                nc.tensor.matmul(ps[0:BN, bass.ds(b + W_SUMS, 1)], hot[:, k, j, :],
                                                 w_it[:, bass.ds(r * PER_ITER + (k * G + j), 1)],
                                                 start=False, stop=False, skip_group_check=True)
                            mm = nc.tensor.matmul(ps[0:BN, bass.ds(b * F, F)], hot[:, k, j, :], ga[:, k, j, :],
                                                  start=False, stop=False, skip_group_check=True)
                        mm.then_inc(groups_done, 1)

            def turn(n, rows_, part):
                pe.wait_ge(h_ready, len(PARTS) * n + PARTS.index(part) + 1)
                for k in range(*part):
                    b0, b1 = bank_buckets(k)
                    for b in range(b0, b1):
                        t = nc.tensor.transpose(bank(k)[:, (b - b0) * BN:(b - b0 + 1) * BN], rows_[0:BN, b, :],
                                                ident[0:BN, 0:BN])
                    t.then_inc(turned, 1)

            pe.sem_inc(groups_done, SLOTS)
            pe.sem_inc(hots_used, SLOTS)
            pe.wait_ge(masks_set, MASKS)
            pe.wait_ge(zeros_set, 3)
            pe.wait_ge(counted, 1)
            nc.tensor.matmul(small[:, 0:NB + 1], ones[:], thr[:, 1, :], start=True, stop=True).then_inc(summed, 1)
            pe.wait_ge(order_known, 1)
            with pe.If(pe.value_load(disorder[0:1, 0:1], min_val=0, max_val=TILES * P) != 0):
                pe.wait_ge(sort_masks, 3)
                for n in range(SORT_PASSES):
                    pe.wait_ge(sort_counted, n + 1)
                    nc.tensor.matmul(bank(0, RADIX), ones[:], s_count, start=True, stop=True).then_inc(sort_summed, 1)
                    with pe.Fori(0, TILES) as r:
                        pe.wait_ge(sort_hot, r + (n * TILES + 1))
                        nc.tensor.matmul(bank(1, RADIX), s_lower, s_hot, start=True, stop=True)
                        nc.tensor.matmul(bank(2, RADIX), ones[:], s_hot, start=True, stop=True).then_inc(sort_prefix, 1)
                pe.wait_ge(sort_ranked, TILES * SORT_PASSES)
            pe.wait_ge(consts_in, 16 * LOADS)
            for k in range(3):
                nc.tensor.transpose(bank(0)[:, k * F:(k + 1) * F], w_raw[:, k, :], ident[:])
            for c in range(FFC):
                nc.tensor.transpose(bank(1)[:, c * P:(c + 1) * P], ff1_raw[:, c, :], ident[:])
            for c in range(FFC):
                t = nc.tensor.transpose(bank(2)[:, c * F:(c + 1) * F], ff2_raw[:, c * P:(c + 1) * P], ident[:])
            t.then_inc(weights_turned, 1)
            pe.wait_ge(weights_ready, 3)
            pe.wait_ge(rows_ready, 2)
            for v in range(3):
                rows_ = (row_f[0], row_f[2], row_raw[2])[v]
                if v >= 1:
                    pe.wait_ge(items_ready, v)
                for k in range(KB):
                    t = nc.tensor.transpose(bank(k, P), rows_[:, k, :], ident[:])
                t.then_inc(rows_turned, 1)
            for part_ in PARTS:
                turn(0, na, part_)
            pe.wait_ge(turned_out, BANKS)
            for q in range(PROJ_BATCHES):
                b0, b1 = q * BANKS, min(NB, (q + 1) * BANKS)
                if q:
                    pe.wait_ge(proj_out, 2 * q)
                    pe.wait_ge(tails_out, 2 * q)
                for b in range(b0, b1):
                    mm = nc.tensor.matmul(bank(b - b0, 3 * F)[0:BN], hT[:, b * BN:(b + 1) * BN], w_qkv[:],
                                          start=True, stop=True)
                mm.then_inc(proj_done, 1)
            pe.wait_ge(proj_out, 2 * PROJ_BATCHES)
            pe.wait_ge(tails_out, 2 * PROJ_BATCHES)
            pe.wait_ge(slide_set, 1)
            clear(range(GB))
            per_block = P // SLOTS
            for kb in range(GB):
                with pe.Fori(0, min(per_block, ITERS - kb * per_block)) as r:
                    for k in range(SLOTS):
                        pe.wait_ge(hots_ready, r * SLOTS + (kb * per_block * SLOTS + k + 1))
                        nc.tensor.matmul(bank(kb, BN * G), slide[:, bass.ds(r * SLOTS + k, P)],
                                         hot_b[:, k].rearrange("p f g -> p (f g)"),
                                         start=False, stop=False, skip_group_check=True).then_inc(hots_used, 1)
            pe.drain().then_inc(item_degs, 1)
            pe.wait_ge(item_degs_out, 1)
            for k in range(GB * G):
                mm = nc.tensor.matmul(small[0:BN, 0:NB], item_deg[:, k // G, :, k % G], grp_hot[:, k, :],
                                      start=(k == 0), stop=(k == GB * G - 1))
            mm.then_inc(degs_ready, 1)
            pe.wait_ge(scaled, 1)
            pe.wait_ge(bucket_in, 16)

            def score_groups(r0, r1):
                with pe.Fori(r0, r1) as r:
                    for k in range(SLOTS):
                        pe.wait_ge(msgs_ready, r * SLOTS + (k + 1))
                        for j in range(G):
                            t = nc.tensor.transpose(bank(k % 2)[0:BN, j * P:(j + 1) * P], hot[:, k, j, :], ident[:])
                        t.then_inc(hot_turned, 1)
                        buckets = buckets_of(pe, item_of(r, k))
                        pe.wait_ge(hot_t_out, r * SLOTS + (k + 1))
                        pe.wait_ge(scores_done, r * SLOTS + (SLOTS + k - 1))
                        for j, b in enumerate(buckets):
                            mm = nc.tensor.matmul(bank(2 + k % 2)[:, j * F:(j + 1) * F], hot_t[:, k % 2, j, :],
                                                  nb_pad[0:BN, bass.ds(b, 1), :].rearrange("p b f -> p (b f)"),
                                                  start=True, stop=True)
                        mm.then_inc(tails_ready, 1)

            score_groups(0, WIN_COUNT_AT)
            pe.wait_ge(win_counted, 1)
            half = -(-NB // 2)
            nc.tensor.matmul(bank(4, half * WPB), ones[0:BN, :], win_tmp[0][0:BN, 0:half * WPB], start=True, stop=True)
            nc.tensor.matmul(bank(5, (NB - half) * WPB), ones[0:BN, :], win_tmp[0][0:BN, half * WPB:],
                             start=True, stop=True).then_inc(win_summed, 1)
            score_groups(WIN_COUNT_AT, WIN_TURN_AT)
            for n in range(4):
                pe.wait_ge(win_rows_ready, n + 1)
                if n:
                    pe.wait_ge(win_cols, n)
                for k in range(KW):
                    t = nc.tensor.transpose(ps[:, 4 * BANK + k * P:4 * BANK + (k + 1) * P],
                                            win_rows[n][:, k * P:(k + 1) * P], ident[:])
                t.then_inc(win_turned, 1)
            score_groups(WIN_TURN_AT, ITERS)
            pe.wait_ge(scores_done, SLOTS + GROUPS)
            by_chunk = ex_it[:].rearrange("p (j c) h -> p j (c h)", c=CHUNKS)
            for n in range(-(-CI // BPB)):
                if n >= BANKS:
                    pe.wait_ge(score_out, n - BANKS + 1)
                for j in range(n * BPB, min(CI, (n + 1) * BPB)):
                    t = nc.tensor.transpose(bank(n % BANKS)[:, (j % BPB) * P:(j % BPB + 1) * P], by_chunk[:, j, :], ident[:])
                t.then_inc(score_turned, 1)
            for n in range(SCANS):
                pe.wait_ge(ends_ready, n + 1)
                for k in range(4):
                    t = nc.tensor.matmul(small[0:1, k * P:(k + 1) * P], ends[:, k:k + 1], ident[:],
                                         start=True, stop=True)
                t.then_inc(ends_turned, 1)
                pe.wait_ge(carry_ready, n + 1)
                nc.tensor.matmul(bank(0, 1), carry[0:1, 4, :], ones[0:1, 0:1], start=True,
                                 stop=True).then_inc(carry_turned, 1)
            for n in range(-(-CI // BPB)):
                pe.wait_ge(shares_ready, -(-min(CI, (n + 1) * BPB) * EXP_PARTS // CI))
                if n == 0:
                    pe.wait_ge(score_out, -(-CI // BPB))
                if n >= BANKS:
                    pe.wait_ge(exp_out, n - BANKS + 1)
                for j in range(n * BPB, min(CI, (n + 1) * BPB)):
                    t = nc.tensor.transpose(bank(n % BANKS)[:, (j % BPB) * P:(j % BPB + 1) * P],
                                            e_sc[:, j * P:(j + 1) * P], ident[:])
                t.then_inc(exp_turned, 1)
            pe.wait_ge(exp_out, -(-CI // BPB))
            for n in range(HOPS):
                if n:
                    pe.wait_ge(sums_out, n * BANKS)
                clear(range(BANKS))
                sum_pass(n)
            for part_ in PARTS:
                if part_[0]:
                    pe.wait_ge(ff2_out, part_[0])
                turn(1, nb_, part_)
                pe.wait_ge(turned_out, BANKS + part_[1])
                for q in range(*part_):
                    b0, b1 = bank_buckets(q)
                    n = (b1 - b0) * BN
                    for c in range(FFC):
                        if q:
                            pe.wait_ge(ff1_out, (q - 1) * FFC + c + 1)
                        nc.tensor.matmul(bank(c, n), ff1_t[:, c * P:(c + 1) * P], hT[:, b0 * BN:b1 * BN],
                                         start=True, stop=True).then_inc(ff1_done, 1)
                    pe.wait_ge(ff1_out, (q + 1) * FFC)
                    if q >= 2:
                        pe.wait_ge(ff2_out, q - 1)
                    for b in range(b0, b1):
                        for c in range(FFC):
                            mm = nc.tensor.matmul(bank(4 + q % 2)[0:BN, (b - b0) * F:(b - b0 + 1) * F],
                                                  ffa[:, c, (b - b0) * BN:(b - b0 + 1) * BN], ff2_t[:, c, :],
                                                  start=(c == 0), stop=(c == FFC - 1))
                    mm.then_inc(ff2_done, 1)
            for part_ in PARTS:
                turn(2, na, part_)
            for k in range(BANKS):
                pe.wait_ge(turned_out, 2 * BANKS + k + 1)
                b0, b1 = bank_buckets(k)
                for b in range(b0, b1):
                    mm = nc.tensor.matmul(bank(k)[0:BN, (b - b0) * F:(b - b0 + 1) * F],
                                          hT[:, b * BN:(b + 1) * BN], w_gcn[:, 0, :], start=True, stop=True)
                mm.then_inc(gcn_done, 1)
            pe.wait_ge(table_ready, 1 + BANKS)

            def next_product(n, r, u):
                pe.wait_ge(conv_out, r * RING + (n * NB + u + 1))
                if n or u >= 2:
                    pe.wait_ge(next_out, r * RING + (n * NB + u - 1))
                nc.tensor.matmul(bank(NEXT_BANK[u], F)[0:BN], turned_q[:, u, :],
                                 w_gcn[:, n + 1, :] if n < LAYERS - 1 else ident[:],
                                 start=True, stop=True).then_inc(next_done, 1)

            for n in range(LAYERS):
                rows_ = (nb_, na)[n % 2]
                if n:
                    pe.wait_ge(next_out, n * NB)
                with pe.Fori(0, NB // RING) as r:
                    for u in range(RING):
                        pe.wait_ge(loops_in, r * RING + (n * NB + u + 1))
                        cells = cells_of(u)
                        for b in range(NB):
                            mm = nc.tensor.matmul(bank(u, BN).rearrange("p (w d) -> p w d", d=WN), rows_[0:BN, b, :],
                                                  cells[:, :, b, :], start=(b == 0), stop=(b == NB - 1))
                        mm.then_inc(conv_done, 1)
                        if u:
                            next_product(n, r, u - 1)
                    next_product(n, r, RING - 1)

        @block.vector
        def _(dve):
            count = [0]

            def link(ins):
                count[0] += 1
                ins.then_inc(dve_link, 1)
                dve.wait_ge(dve_link, count[0])

            v = nc.vector

            def tt(to, x, y, op):
                link(v.tensor_tensor(to, x, y, op))

            def layernorm(to, x, scratch, n, part=(0, BANKS)):
                c0, c1 = part_buckets(part)
                to, x, scratch = (y[0:BN, c0:c1] for y in (to, x, scratch))
                mean, var, dev, inv = (stat[0:BN, k, c0:c1] for k in range(4))
                link(v.tensor_reduce(mean, x, AX.X, ALU.add))
                link(v.tensor_scalar(mean, mean, 1.0 / F, None, ALU.mult))
                tt(to, x, over_f(mean), ALU.subtract)
                tt(scratch, to, to, ALU.mult)
                link(v.tensor_reduce(inv, scratch, AX.X, ALU.add))
                v.tensor_scalar(var, inv, 1.0 / F, EPS, ALU.mult, ALU.add).then_inc(var_ready, 1)
                dve.wait_ge(std_ready, n)
                link(v.reciprocal(inv, dev))
                tt(to, to, over_f(inv), ALU.mult)

            def over_f(x):
                return x.unsqueeze(2).to_broadcast([BN, x.shape[1], F])

            def over_nodes(k, n=NB):
                return rowvec[0:BN, k:k + 1, :].to_broadcast([BN, n, F])

            def onehots(to, r, k, ahead=0):
                return v.tensor_tensor(to[:, (k + ahead) % SLOTS],
                                       dloc[:, bass.ds(item_of(r, k, ahead), G)].unsqueeze(2).to_broadcast([P, G, BN]),
                                       iota_bn.unsqueeze(1).to_broadcast([P, G, BN]), ALU.is_equal)

            def message_pass(s):
                for r0, r1 in cut(0, FULL_ITERS, BUILD_ITERS, ITERS) if s else cut(0, ITERS):
                    message_groups(s, r0, r1, s > 0 and r0 < BUILD_ITERS)
                dve.wait_ge(groups_done, SLOTS + (s + 1) * GROUPS)

            def build_factors(s, r, k):
                i = win_item(s, r, k)
                v.tensor_tensor(hot_p[:, k % 2], win_p[:, bass.ds(i, BG)].unsqueeze(2).to_broadcast([P, BG, P]),
                                iota_p[:].unsqueeze(1).to_broadcast([P, BG, P]), ALU.is_equal)
                v.tensor_tensor(hot_bk[:, k % 2], win_b[:, bass.ds(i, BG)].unsqueeze(2).to_broadcast([P, BG, NB]),
                                iota_bn[:, 0:NB].unsqueeze(1).to_broadcast([P, BG, NB]),
                                ALU.is_equal).then_inc(build_link, 1)
                for j in range(BG):
                    v.tensor_scalar(hot_d[:, k % 2, j, :], iota_bn[:, 0:WN], win_dd[:, bass.ds(win_item(s, r, k, j), 1)],
                                    win_w[:, bass.ds(win_item(s, r, k, j), 1)], ALU.is_equal,
                                    ALU.mult).then_inc(build_link, 1)
                dve.wait_ge(build_link, r * (SLOTS * (BG + 1)) + (steps_before(s) + k + 1) * (BG + 1))
                v.tensor_tensor(prod[:, k % 2].rearrange("p j (b d) -> p j b d", d=WN),
                                hot_bk[:, k % 2].unsqueeze(3).to_broadcast([P, BG, NB, WN]),
                                hot_d[:, k % 2].unsqueeze(2).to_broadcast([P, BG, NB, WN]),
                                ALU.mult).then_inc(prod_ready, 1)

            def build_sums(s, r, k):
                dve.wait_ge(cell_sums, r * SLOTS + (steps_before(s) + k + 1))
                dve.wait_ge(acc_out[k], r * (16 * BG) + 16 * BG * ((s - 1) * BUILD_ITERS + 1))
                for j in range(BG):
                    before = win_acc[:, k, j - 1, 0:CELL] if j else win_acc[:, (k - 1) % SLOTS, BG - 1, 0:CELL]
                    ins = v.scalar_tensor_tensor(
                        out=win_acc[:, k, j, 0:CELL], in0=before,
                        scalar=win_same[:, bass.ds(win_item(s, r, k, j), 1)],
                        in1=ps[:, 7 * BANK + j * CELL:7 * BANK + (j + 1) * CELL], op0=ALU.mult, op1=ALU.add)
                    if j < BG - 1:
                        ins.then_inc(sum_link, 1)
                        dve.wait_ge(sum_link, r * (SLOTS * (BG - 1)) + ((steps_before(s) + k) * (BG - 1) + j + 1))
                ins.then_inc(acc_ready, 1)
                dve.wait_ge(acc_ready, r * SLOTS + (steps_before(s) + k + 2))

            def message_groups(s, r0, r1, building):
                with dve.Fori(r0, r1) as r:
                    for k in range(SLOTS):
                        if building:
                            build_factors(s, r, k)
                        if s == 0:
                            dve.wait_ge(loaded[k], r * 16 + 16)
                        else:
                            dve.wait_ge(got[k], got_at(s, r, k, r0))
                        onehots(hot, r, k).then_inc(msgs_ready, 1)
                        i = item_of(r, k)
                        rows_ = ga[:, k].rearrange("p g (h d) -> p (g h) d", h=HEADS)
                        by = ex_it[:, bass.ds(i, G), :].rearrange("p g h -> p (g h)").unsqueeze(2).to_broadcast(
                            [P, G * HEADS, HD])
                        v.tensor_tensor(rows_, rows_, by, ALU.mult).then_inc(msgs_ready, 1)
                        if building:
                            build_sums(s, r, k)

            def sort_edges():
                sort_count = [0]

                def chain(ins):
                    sort_count[0] += 1
                    ins.then_inc(sort_link, 1)
                    dve.wait_ge(sort_link, sort_count[0])

                dve.wait_ge(sort_in, 32)
                chain(v.memset(edges, 0.0))
                chain(v.tensor_copy(edges[:, :, 0], s_raw.bitcast(I32)))
                chain(v.tensor_copy(edges[:, :, 1], dst_allf))
                chain(v.tensor_copy(edges[:, :, 2], s_digit))
                dve.wait_ge(sort_masks, 3)
                for n in range(SORT_PASSES):
                    if n:
                        dve.wait_ge(sort_in, 32 + 16 * n)
                    chain(v.tensor_copy(s_raw.bitcast(I32), edges[:, :, 1]))
                    chain(v.tensor_scalar(s_raw.bitcast(I32), s_raw.bitcast(I32), *(
                        (RADIX - 1, None, ALU.bitwise_and) if n == 0 else (RADIX_BITS, None, ALU.arith_shift_right))))
                    chain(v.tensor_copy(s_digit, s_raw.bitcast(I32)))
                    for d in range(RADIX):
                        chain(v.tensor_scalar(s_raw, s_digit, float(d), 0.0, ALU.is_lt, ALU.add,
                                              accum_out=s_count[:, d:d + 1]))
                    dve.sem_inc(sort_counted, 1)
                    dve.wait_ge(sort_summed, n + 1)
                    chain(v.tensor_copy(s_base, bank(0, RADIX)))
                    steps, before = [0], sort_count[0]
                    STEPS = 8 + 4 * (n == 0)

                    with dve.Fori(0, TILES) as r:
                        def step(ins):
                            steps[0] += 1
                            ins.then_inc(sort_link, 1)
                            dve.wait_ge(sort_link, r * STEPS + (before + steps[0]))

                        v.tensor_tensor(s_hot, s_iota, s_digit[:, bass.ds(r, 1)].to_broadcast([P, RADIX]),
                                        ALU.is_equal).then_inc(sort_hot, 1)
                        step(v.tensor_copy(s_move, edges[:, bass.ds(r, 1), :].rearrange("p t c -> p (t c)")))
                        dve.wait_ge(sort_prefix, r + (n * TILES + 1))
                        step(v.tensor_tensor(s_tmp, s_base, bank(1, RADIX), ALU.add))
                        step(v.tensor_tensor(s_tmp, s_tmp, s_hot, ALU.mult))
                        step(v.tensor_reduce(s_rank[:, 0:1], s_tmp, AX.X, ALU.add))
                        step(v.tensor_tensor(s_base, s_base, bank(2, RADIX), ALU.add))
                        step(v.tensor_copy(s_rank[:, 1:2].bitcast(I32), s_rank[:, 0:1]))
                        if n == 0:
                            step(v.tensor_scalar(s_rank[:, 2:3].bitcast(I32), s_rank[:, 1:2].bitcast(I32),
                                                 P.bit_length() - 1, None, ALU.arith_shift_right))
                            step(v.tensor_scalar(s_rank[:, 1:2].bitcast(I32), s_rank[:, 1:2].bitcast(I32),
                                                 P - 1, None, ALU.bitwise_and))
                            step(v.tensor_copy(s_rank[:, 0:1], s_rank[:, 1:2].bitcast(I32)))
                            step(v.tensor_copy(s_tmp[:, 0:1], s_rank[:, 2:3].bitcast(I32)))
                            step(v.scalar_tensor_tensor(out=s_rank[:, 1:2], in0=s_rank[:, 0:1], scalar=float(TILES),
                                                        in1=s_tmp[:, 0:1], op0=ALU.mult, op1=ALU.add))
                            step(v.tensor_copy(s_rank[:, 3:4].bitcast(I32), s_rank[:, 1:2]))
                        else:
                            step(v.tensor_copy(s_tmp[:, 0:1], s_rank[:, 0:1]))
                            step(v.tensor_copy(s_rank[:, 3:4].bitcast(I32), s_rank[:, 0:1]))
                        dve.sem_inc(sort_ranked, 1)
                        dve.wait_ge(sort_moved, r * 16 + 16 * (n * TILES + 1))
                    assert steps[0] == STEPS, steps
                    sort_count[0] = before + STEPS * TILES
                dve.wait_ge(sort_in, 32 + 16 * SORT_PASSES)
                chain(v.tensor_copy(s_raw.bitcast(I32), edges[:, :, 0]))
                chain(v.tensor_copy(s_digit.bitcast(I32), edges[:, :, 1]))
                chain(v.tensor_copy(dst_allw, edges[:, :, 2]))
                dve.sem_inc(sort_split, 1)

            dve.sem_inc(scores_done, SLOTS)
            v.memset(zeros[:], 0.0).then_inc(zeros_set, 1)
            v.memset(ones[:], 1.0).then_inc(zeros_set, 1)
            v.memset(nb_pad[:, NB, :], 0.0).then_inc(zeros_set, 1)
            dve.wait_ge(masks_set, MASKS)
            dve.wait_ge(dst_in, 32)
            link(v.tensor_scalar(step5[:], step5[:], 0.0, None, ALU.is_ge))
            link(v.tensor_copy(dst_allf, dst_all))
            link(v.scalar_tensor_tensor(out=nb_.rearrange("p b f -> p (b f)")[:, 0:TILES], in0=dst_allf, scalar=0.0,
                                        in1=dst_next, op0=ALU.add, op1=ALU.is_gt, accum_out=thr[:, 1, NB:NB + 1]))
            for b in range(NB):
                link(v.tensor_scalar(nb_.rearrange("p b f -> p (b f)")[:, 0:TILES], dst_allf, float(BN * (b + 1)),
                                     0.0, ALU.is_lt, ALU.add, accum_out=thr[:, 1, b:b + 1]))
            dve.sem_inc(counted, 1)
            dve.wait_ge(summed, 1)
            v.tensor_copy(disorder[:], small[:, NB:NB + 1]).then_inc(order_known, 1)
            dve.wait_ge(order_known, 1)
            with dve.If(dve.value_load(disorder[0:1, 0:1], min_val=0, max_val=TILES * P) != 0):
                sort_edges()
            link(v.tensor_copy(thr_i[:], small[:, 0:NB + 1]))
            link(v.tensor_scalar(thr_i[:], thr_i[:], P.bit_length() - 1, None, ALU.arith_shift_right))
            link(v.tensor_copy(thr[:, 2, :], thr_i[:]))
            tt(thr[:, 2, :], thr[:, 2, :], thr[:, 0, :], ALU.add)
            link(v.tensor_scalar(thr[:, 0, :], thr[:, 0, :], -1.0, None, ALU.add))
            link(v.tensor_scalar(item_b[:], item_t[:], CHUNKS - 1, None, ALU.bitwise_and))
            link(v.tensor_scalar(item_t[:], item_t[:], CHUNKS.bit_length() - 1, None, ALU.arith_shift_right))
            link(v.tensor_copy(item_f[:, 1, :], item_b[:]))
            link(v.tensor_copy(item_f[:, 2, :], item_t[:]))
            link(v.scalar_tensor_tensor(out=item_f[:, 0, :], in0=item_f[:, 1, :], scalar=float(CI),
                                        in1=item_f[:, 2, :], op0=ALU.mult, op1=ALU.add))
            tt(ge[:], item_f[:, 0, :].unsqueeze(2).to_broadcast([P, KB, NB]),
               thr[:, 2, 0:NB].unsqueeze(1).to_broadcast([P, KB, NB]), ALU.is_ge)
            link(v.tensor_reduce(item_f[:, 1, :], ge[:], AX.X, ALU.add))
            tt(item_f[:, 2, :], item_f[:, 0, :], item_f[:, 1, :], ALU.subtract)
            link(v.tensor_copy(item_b[:], item_f[:, 1, :]))
            link(v.tensor_scalar(item_f[:, 3, :], item_f[:, 1, :], float(BN), None, ALU.mult))
            v.tensor_scalar(item_t[:], item_f[:, 2, :], float(TILES - 1), None, ALU.min).then_inc(tiles_known, 1)
            link(v.tensor_scalar(grp_i[:, 1, :], grp_i[:, 0, :], CHUNKS - 1, None, ALU.bitwise_and))
            link(v.tensor_scalar(grp_i[:, 0, :], grp_i[:, 0, :], CHUNKS.bit_length() - 1, None, ALU.arith_shift_right))
            link(v.tensor_copy(grp_f[:], grp_i[:]))
            link(v.scalar_tensor_tensor(out=grp_f[:, 0, :], in0=grp_f[:, 1, :], scalar=float(CI),
                                        in1=grp_f[:, 0, :], op0=ALU.mult, op1=ALU.add))
            by_group = [P, GB * G, NB]
            tt(grp_hot[:], grp_f[:, 0, :].unsqueeze(2).to_broadcast(by_group),
               thr[:, 2, 0:NB].unsqueeze(1).to_broadcast(by_group), ALU.is_ge)
            link(v.tensor_reduce(grp_f[:, 1, :], grp_hot[:], AX.X, ALU.add))
            tt(grp_hot[:], grp_f[:, 1, :].unsqueeze(2).to_broadcast(by_group),
               thr[:, 0, 0:NB].unsqueeze(1).to_broadcast(by_group), ALU.is_equal)
            dve.wait_ge(weights_turned, 1)
            v.tensor_copy(w_qkv[:], bank(0, 3 * F)).then_inc(weights_ready, 1)
            v.tensor_copy(ff1_t[:], bank(1)).then_inc(weights_ready, 1)
            v.tensor_copy(ff2_t[:].rearrange("p c f -> p (c f)"), bank(2)).then_inc(weights_ready, 1)
            dve.wait_ge(rows_in, 3 * KB * 16)
            v.tensor_copy(row_f[0], row_i[0]).then_inc(rows_ready, 1)
            v.tensor_tensor(row_f[2], row_i[1], item_f[:, 3, :].unsqueeze(2).to_broadcast([P, KB, P]),
                            ALU.subtract).then_inc(rows_ready, 1)
            v.scalar_tensor_tensor(out=row_f[1], in0=row_i[1], scalar=float(KEY), op0=ALU.mult,
                                   in1=item_f[:, 1, :].unsqueeze(2).to_broadcast([P, KB, P]),
                                   op1=ALU.add).then_inc(rows_ready, 1)
            turned_rows = ps[:, 0:KB * BANK].rearrange("p (k n) -> p k n", n=BANK)[:, :, 0:P]
            for n, to in enumerate((src_it[:], dloc[:], w_it[:])):
                dve.wait_ge(rows_turned, n + 1)
                v.tensor_copy(to.rearrange("p (k e) -> p k e", e=P), turned_rows).then_inc(items_ready, 1)
            dve.wait_ge(items_ready, 3)
            dve.wait_ge(x_in, 16)
            dve.wait_ge(key_out, 16)
            layernorm(h0, h0, na, 1)
            link(v.tensor_scalar(h0[0:BN], h0[0:BN], 0.0, None, ALU.max))
            for n, part_ in enumerate(PARTS):
                c0, c1 = part_buckets(part_)
                layernorm(na, h0, nb_, 2 + n, part_)
                tt(na[0:BN, c0:c1], na[0:BN, c0:c1], over_nodes(G1, c1 - c0), ALU.mult)
                v.tensor_tensor(na[0:BN, c0:c1], na[0:BN, c0:c1], over_nodes(B1, c1 - c0), ALU.add).then_inc(h_ready, 1)
            dve.wait_ge(turned_out, BANKS)
            for q in range(PROJ_BATCHES):
                b0, b1 = q * BANKS, min(NB, (q + 1) * BANKS)
                dve.wait_ge(proj_out, 2 * (q + 1))
                v.tensor_copy(nb_[0:BN, b0:b1, :], proj_view(b1 - b0, 1)).then_inc(tails_out, 1)
                v.tensor_scalar(fe_a[0:BN, b0:b1, :], proj_view(b1 - b0, 2), ALPHA, None,
                                ALU.mult).then_inc(tails_out, 1)
            dve.wait_ge(tails_out, 2 * PROJ_BATCHES)
            dve.sem_inc(table_ready, 1)
            link(v.tensor_copy(iota_g, iota_bn.unsqueeze(2).to_broadcast([P, BN, G])))
            link(v.tensor_copy(dloc_b, dloc[:]))
            with dve.Fori(0, ITERS) as r:
                for k in range(SLOTS):
                    dve.wait_ge(hots_used, r * SLOTS + (k + 1))
                    v.tensor_tensor(hot_b[:, k], dloc_b[:, bass.ds(item_of(r, k), G)].unsqueeze(1).to_broadcast([P, BN, G]),
                                    iota_g, ALU.is_equal).then_inc(hots_ready, 1)
            dve.wait_ge(degs_ready, 1)
            v.tensor_scalar(log_deg[0:BN], small[0:BN, 0:NB], 1.0, None, ALU.max).then_inc(logs_ready, 1)
            link(v.tensor_copy(deg_n[0:BN], small[0:BN, 0:NB]))
            dve.wait_ge(logs_ready, 2)
            link(v.tensor_scalar(log_deg[0:BN], log_deg[0:BN], 1.0 / HD, None, ALU.mult))
            v.tensor_tensor(nb_[0:BN, 0:NB], nb_[0:BN, 0:NB], over_f(log_deg[0:BN]), ALU.mult).then_inc(scaled, 1)
            onehots(hot, 0, 0).then_inc(msgs_ready, 1)

            def score_groups(r0, r1):
                with dve.Fori(r0, r1) as r:
                    for k in range(SLOTS):
                        onehots(hot, r, k, 1).then_inc(msgs_ready, 1)
                        heads = ga_wide[:, k, :, 0:F]
                        dve.wait_ge(got[k], got_at(0, r, k, r0))
                        dve.wait_ge(tails_ready, r * SLOTS + (k + 1))
                        v.tensor_tensor(heads, heads, bank(2 + k % 2).rearrange("p (g f) -> p g f", g=G),
                                        ALU.mult).then_inc(step_link, 1)
                        dve.wait_ge(step_link, r * (3 * SLOTS) + (3 * k + 1))
                        v.scalar_tensor_tensor(out=heads, in0=heads, scalar=SLOPE, in1=heads, op0=ALU.mult,
                                               op1=ALU.max).then_inc(step_link, 1)
                        dve.wait_ge(step_link, r * (3 * SLOTS) + (3 * k + 2))
                        v.tensor_tensor(heads, heads, rowvec[:, ATTN:ATTN + 1, :].to_broadcast([P, G, F]),
                                        ALU.mult).then_inc(step_link, 1)
                        dve.wait_ge(step_link, r * (3 * SLOTS) + (3 * k + 3))
                        v.tensor_reduce(ex_it[:, bass.ds(item_of(r, k), G), :],
                                        heads.rearrange("p g (h d) -> p g h d", h=HEADS),
                                        AX.X, ALU.add).then_inc(scores_done, 1)

            score_groups(0, WIN_COUNT_AT)
            ends_at, ends_i, junk = win_tmp
            dve.wait_ge(table_out, 32)
            by_window = ends_at.rearrange("p (b j) -> p b j", j=WPB)
            run_deg, before_deg = stat[0:BN, 0, :], stat[0:BN, 1, :]
            link(v.tensor_tensor_scan(run_deg, ones[0:BN, 0:NB], deg_n[0:BN], 0.0, ALU.mult, ALU.add))
            tt(before_deg, run_deg, deg_n[0:BN], ALU.subtract)
            tt(by_window[0:BN], deg_n[0:BN].unsqueeze(2).to_broadcast([BN, NB, WPB]),
               step5[0:BN].unsqueeze(1).to_broadcast([BN, NB, WPB]), ALU.mult)
            v.tensor_tensor(by_window[0:BN], by_window[0:BN], before_deg.unsqueeze(2).to_broadcast([BN, NB, WPB]),
                            ALU.add).then_inc(win_counted, 1)
            dve.wait_ge(win_summed, 1)
            half = -(-NB // 2) * WPB
            link(v.tensor_copy(ends_i.bitcast(I32)[:, 0:half], bank(4, half)))
            link(v.tensor_copy(ends_i.bitcast(I32)[:, half:], bank(5, WINDOWS - half)))
            link(v.tensor_scalar(ends_i.bitcast(I32), ends_i.bitcast(I32), P.bit_length() - 1, None,
                                 ALU.arith_shift_right))
            link(v.tensor_copy(ends_at, ends_i.bitcast(I32)))
            link(v.tensor_scalar(stat[:, 2, :], iota_bn[:, 0:NB], float(WPB), 1.0, ALU.mult, ALU.add))
            tt(by_window, by_window, stat[:, 2, :].unsqueeze(2).to_broadcast([P, NB, WPB]), ALU.add)
            tt(by_window, by_window, iota_bn[:, 0:WPB].unsqueeze(1).to_broadcast([P, NB, WPB]), ALU.add)
            for k in range(KW):
                link(v.tensor_scalar(junk, ends_at, win_it[:, k:k + 1], 0.0, ALU.is_le, ALU.add,
                                     accum_out=win_f[:, 0, k:k + 1]))
            link(v.tensor_scalar(win_f[:, 1, :], win_f[:, 0, :], float(WN), None, ALU.mult))
            tt(win_it[:], win_it[:], win_f[:, 0, :], ALU.subtract)
            v.tensor_scalar(win_t[:], win_it[:], float(TILES - 1), None, ALU.min).then_inc(win_known, 1)
            score_groups(WIN_COUNT_AT, WIN_ROWS_AT)
            dve.wait_ge(win_rows_in, 16 * 3 * KW)
            w_src, w_bkt, w_dst = win_rows[0:3]
            link(v.tensor_copy(w_src, w_src.bitcast(I32)))
            link(v.tensor_scalar(w_bkt, w_src, -(BN - 1) / 2, 1.0 / BN, ALU.add, ALU.mult))
            link(v.tensor_scalar(w_bkt, w_bkt, ROUND, None, ALU.add))
            link(v.tensor_scalar(w_bkt, w_bkt, -ROUND, None, ALU.add))
            v.scalar_tensor_tensor(out=w_src, in0=w_bkt, scalar=-float(BN), in1=w_src, op0=ALU.mult,
                                   op1=ALU.add).then_inc(win_rows_ready, 2)
            v.tensor_tensor(w_dst.rearrange("p (k e) -> p k e", e=P), w_dst.bitcast(I32).rearrange("p (k e) -> p k e", e=P),
                            win_f[:, 1, :].unsqueeze(2).to_broadcast([P, KW, P]),
                            ALU.subtract).then_inc(win_rows_ready, 2)
            score_groups(WIN_ROWS_AT, KEY_AT)
            half = KEY_MAIN // 2
            dve.wait_ge(key_in, 16 * 2 * CHUNKS)
            link(v.memset(gap[:], 0.0))
            tt(gap[:, 1:half], key[:, 1:half], key[:, 0:half - 1], ALU.not_equal)
            score_groups(KEY_AT, KEY_AT2)
            tt(gap[:, half:KEY_MAIN], key[:, half:], key[:, half - 1:KEY_MAIN - 1], ALU.not_equal)
            tt(gap[:, KEY_MAIN:KEY_MAIN + 1], key_last[:, 0:1], key[:, KEY_MAIN - 1:], ALU.not_equal)
            tt(gap[:, KEY_MAIN + 1:L], key_last[:, 1:], key_last[:, :-1], ALU.not_equal)
            link(v.tensor_scalar(gap[:], gap[:], -BIG, None, ALU.mult))
            score_groups(KEY_AT2, FULL_ITERS)
            link(v.tensor_reduce(ends[:, 1:2], gap[:, 0:L], AX.X, ALU.min))
            link(v.tensor_copy(ends[:, 2:3], key[:, 0:1]))
            link(v.tensor_copy(ends[:, 3:4], key_last[:, P - 1:P]))
            score_groups(FULL_ITERS, ITERS)
            dve.wait_ge(scores_done, SLOTS + GROUPS)
            for k in range(SLOTS):
                dve.wait_ge(stored[k], 16 * (ITERS + (k == SLOTS - 1)))
            dve.sem_inc(key_free, 1)
            dve.wait_ge(score_out, -(-CI // BPB))

            def scan_carried(n, to, gaps, data, last, back, summing=False):
                none = 0.0 if summing else -BIG
                ops = (ALU.mult, ALU.add) if summing else (ALU.add, ALU.max)
                link(v.tensor_tensor_scan(to, gaps, data, none, *ops))
                v.tensor_copy(ends[:, 0:1], last).then_inc(ends_ready, 1)
                dve.wait_ge(ends_turned, n + 1)
                link(v.tensor_copy(rows[:], small[0:1, 0:4 * P].rearrange("o (k c h) -> o k h c", k=4, h=HEADS)))
                way = slice(None, None, -1) if back else slice(None)
                row = [rows[0:1, k, :, way] for k in range(4)]
                final, gate, first, last_ = (row[0], row[1], row[3], row[2]) if back else row
                gates, new, run, cut = (carry[0:1, k, :].rearrange("o (h c) -> o h c", h=HEADS) for k in range(4))
                link(v.memset(carry[0:1, 3, :], 1.0))
                link(v.memset(carry[0:1, 0:2, :], none))
                tt(cut[:, :, 1:], first[:, :, 1:], last_[:, :, :-1], ALU.not_equal)
                link(v.scalar_tensor_tensor(out=gates[:, :, 1:], in0=cut[:, :, :-1], scalar=-BIG,
                                            in1=gate[:, :, :-1], op0=ALU.mult, op1=ALU.add))
                if summing:
                    link(v.tensor_scalar(gates[:, :, 1:], gates[:, :, 1:], 0.0, None, ALU.is_equal))
                link(v.tensor_copy(new[:, :, 1:], final[:, :, :-1]))
                link(v.tensor_tensor_scan(carry[0:1, 2, :], carry[0:1, 0, :], carry[0:1, 1, :], none, *ops))
                to_col = carry[0:1, 4, :].rearrange("o (c h) -> o h c", h=HEADS)[:, :, way]
                if summing:
                    link(v.tensor_scalar(cut, cut, -1.0, 1.0, ALU.mult, ALU.add))
                    v.tensor_tensor(to_col, cut, run, ALU.mult).then_inc(carry_ready, 1)
                else:
                    v.scalar_tensor_tensor(out=to_col, in0=cut, scalar=-BIG, in1=run, op0=ALU.mult,
                                           op1=ALU.add).then_inc(carry_ready, 1)
                dve.wait_ge(carry_turned, n + 1)
                link(v.tensor_copy(carry_col[:, n:n + 1], bank(0, 1)))
                link(v.tensor_tensor_scan(to, gaps, data, carry_col[:, n:n + 1], *ops))

            scan_carried(0, fw, gap[:, 0:L], e_sc, fw[:, L - 1:L], False)
            scan_carried(1, bw[:, ::-1], gap[:, 1:L + 1][:, ::-1], fw[:, ::-1], bw[:, 0:1], True)
            w = L // EXP_PARTS
            parts = [slice(n * w, (n + 1) * w) for n in range(EXP_PARTS)]
            for part_ in parts:
                v.tensor_tensor(e_sc[:, part_], e_sc[:, part_], bw[:, part_], ALU.subtract).then_inc(shifted, 1)
            dve.wait_ge(shifted, EXP_PARTS)
            link(v.tensor_scalar(bw, gap[:, 0:L], 0.0, None, ALU.is_equal))
            dve.wait_ge(exps_ready, EXP_PARTS)
            scan_carried(2, fw, bw, e_sc, fw[:, L - 1:L], False, summing=True)
            scan_carried(3, bw[:, ::-1], gap[:, 1:L + 1][:, ::-1], fw[:, ::-1], bw[:, 0:1], True)
            for part_ in parts:
                link(v.reciprocal(bw[:, part_], bw[:, part_]))
                v.scalar_tensor_tensor(out=e_sc[:, part_], in0=e_sc[:, part_], scalar=1.0 - ALPHA, in1=bw[:, part_],
                                       op0=ALU.mult, op1=ALU.mult).then_inc(shares_ready, 1)
            for n in range(-(-CI // BPB)):
                j0, j1 = n * BPB, min(CI, (n + 1) * BPB)
                dve.wait_ge(exp_turned, n + 1)
                v.tensor_copy(ex_it[:, j0 * CHUNKS:j1 * CHUNKS, :].rearrange("p i h -> p (i h)"),
                              bank(n % BANKS, (j1 - j0) * P)).then_inc(exp_out, 1)
            dve.wait_ge(exp_out, -(-CI // BPB))
            dve.sem_inc(acc_ready, 1)
            for n in range(HOPS):
                message_pass(n)
                if n == 0:
                    dve.wait_ge(targets_ready, 1)
                    dve.wait_ge(cols_in, 16)
                if n == 1:
                    link(v.tensor_scalar(stat[0:BN, 0, :], ps[0:BN, W_SUMS:W_SUMS + NB], 1.0, None, ALU.add))
                for k in range(BANKS):
                    b0, b1 = bank_buckets(k)
                    v.tensor_tensor(na[0:BN, b0:b1], bank(k, (b1 - b0) * F)[0:BN].rearrange("p (b f) -> p b f", f=F),
                                    fe_a[0:BN, b0:b1], ALU.add).then_inc(sums_out, 1)
                dve.wait_ge(sums_out, (n + 1) * BANKS)
                if n == 1:
                    link(v.tensor_scalar(w_deg[0:BN], stat[0:BN, 0, :], 0.0, None, ALU.is_gt))
                    v.tensor_scalar(dinv[0:BN], stat[0:BN, 0, :], 1e-30, None, ALU.max).then_inc(var_ready, 1)
                if n == HOPS - 2:
                    dve.wait_ge(std_ready, 4)
                    link(v.reciprocal(dinv[0:BN], dinv[0:BN]))
                    v.tensor_tensor(dinv[0:BN], dinv[0:BN], w_deg[0:BN], ALU.mult).then_inc(dinv_ready, 1)
            dve.sem_inc(hops_done, 1)
            tt(na[0:BN], na[0:BN], h0[0:BN], ALU.add)
            dve.wait_ge(x_again, 16)
            for n, part_ in enumerate(PARTS):
                c0, c1 = part_buckets(part_)
                layernorm(nb_, na, h0, 5 + n, part_)
                tt(nb_[0:BN, c0:c1], nb_[0:BN, c0:c1], over_nodes(G2, c1 - c0), ALU.mult)
                v.tensor_tensor(nb_[0:BN, c0:c1], nb_[0:BN, c0:c1], over_nodes(B2, c1 - c0), ALU.add).then_inc(h_ready, 1)
            tt(h0[0:BN], na[0:BN], x_sb[0:BN], ALU.add)
            tt(h0[0:BN], h0[0:BN], over_nodes(BFF2), ALU.add)
            dve.sem_inc(x_used, 1)
            for q in range(BANKS):
                b0, b1 = bank_buckets(q)
                dve.wait_ge(ff2_done, q + 1)
                v.tensor_tensor(h0[0:BN, b0:b1, :], h0[0:BN, b0:b1, :],
                                bank(4 + q % 2, (b1 - b0) * F)[0:BN].rearrange("p (b f) -> p b f", f=F),
                                ALU.add).then_inc(ff2_out, 1)
            dve.wait_ge(ff2_out, BANKS)
            for n, part_ in enumerate(PARTS):
                c0, c1 = part_buckets(part_)
                layernorm(na, h0, nb_, 7 + n, part_)
                v.tensor_scalar(na[0:BN, c0:c1], na[0:BN, c0:c1], 0.0, None, ALU.max).then_inc(h_ready, 1)
            for k in range(BANKS):
                b0, b1 = bank_buckets(k)
                dve.wait_ge(gcn_done, k + 1)
                v.tensor_tensor(nb_[0:BN, b0:b1, :],
                                bank(k, (b1 - b0) * F)[0:BN].rearrange("p (b f) -> p b f", f=F),
                                dinv[0:BN, b0:b1].unsqueeze(2).to_broadcast([BN, b1 - b0, F]),
                                ALU.mult).then_inc(table_ready, 1)
            dve.wait_ge(dinv_in, 16)

            def add_loops(n, r, u):
                dve.wait_ge(adj_in[u % RING], r * 16 + 16 * (n * (NB // RING) + u // RING + 1))
                own = cells_of(u % RING)[:, :, bass.ds(r * RING + u, 1), :].rearrange("p w b d -> p w (b d)")
                v.tensor_tensor(own, own, ident[0:BN, 0:BN].rearrange("p (w d) -> p w d", d=WN),
                                ALU.add).then_inc(loops_in, 1)

            def scale_bucket(n, r, u):
                dve.wait_ge(conv_done, r * RING + (n * NB + u + 1))
                v.tensor_tensor(turned_q[:, u, :], bank(u, BN), dinv_row[:, bass.ds(r * (RING * BN) + u * BN, BN)],
                                ALU.mult).then_inc(conv_scaled, 1)

            def next_rows(n, r, u):
                dve.wait_ge(next_done, r * RING + (n * NB + u + 1))
                to = (na, nb_)[n % 2][0:BN, bass.ds(r * RING + u, 1), :].rearrange("p b f -> p (b f)")
                if n < LAYERS - 1:
                    ins = v.tensor_scalar(to, bank(NEXT_BANK[u], F)[0:BN], dinv[0:BN, bass.ds(r * RING + u, 1)], None,
                                          ALU.mult)
                else:
                    ins = v.tensor_tensor(to, bank(NEXT_BANK[u], F)[0:BN],
                                          h0[0:BN, bass.ds(r * RING + u, 1), :].rearrange("p b f -> p (b f)"), ALU.add)
                ins.then_inc(next_out, 1)

            for n in range(LAYERS):
                add_loops(n, 0, 0)
                for r0, r1 in ((0, NB // RING - 1), (NB // RING - 1, NB // RING)):
                    with dve.Fori(r0, r1) as r:
                        for u in range(RING):
                            if u < RING - 1 or r0 == 0:
                                add_loops(n, r, u + 1)
                            scale_bucket(n, r, u)
                            if u:
                                next_rows(n, r, u - 1)
                        next_rows(n, r, RING - 1)


_EDGE = {"src": 0, "dst": N_NODES + BN, "edge_weight": 0}


def kernel(**inputs):
    import numpy as np
    import concourse.bacc as bacc
    from concourse.bass_utils import run_bass_kernel_spmd

    nc = bacc.Bacc("TRN2", target_bir_lowering=False, num_devices=1)
    arrays, args = {}, {}
    for name, value in inputs.items():
        x = np.ascontiguousarray(value)
        if name in _EDGE:
            x = np.pad(x, (0, (TILES + 1) * P - N_EDGES), constant_values=_EDGE[name])
        arrays["in_" + name] = x
        args[name] = nc.dram_tensor("in_" + name, x.shape, mybir.dt.from_np(x.dtype), kind="ExternalInput").ap()
    out = nc.dram_tensor("out_0", (N_NODES, F), F32, kind="ExternalOutput").ap()
    gnn_stack(nc, args, out)
    r = run_bass_kernel_spmd(nc, [arrays], core_ids=[0])
    return r.results[0]["out_0"]
```
